# Optimizing a Trainium2 kernel written in Bass

```python
import numpy as np
import jax
import jax.numpy as jnp

def _softmax(x, axis=-1):
    return jax.nn.softmax(x, axis=axis)

def _gelu(x):
    return jax.nn.gelu(x, approximate=True)

def _silu(x):
    return jax.nn.silu(x)

def _sigmoid(x):
    return jax.nn.sigmoid(x)

def _layernorm(x, axis=-1, eps=1e-05):
    m = jnp.mean(x, axis=axis, keepdims=True)
    v = jnp.var(x, axis=axis, keepdims=True)
    return (x - m) / jnp.sqrt(v + eps)

def _scatter_add(tgt, idx, src, axis=0):
    return tgt.at[idx].add(src)

def _segment_sum(src, seg, n):
    return jax.ops.segment_sum(src, seg, n)
kernel_name = 'mk_vit_tower_d2_tok_img1024_r4_014690'

def setup_inputs(seed: int=0):
    np.random.seed(seed)
    _w = jnp.asarray

    def _rec_inputs():
        import jax
        import jax.numpy as jnp
        _rk = jax.random.key(seed)
        x = -0.00016672 + 0.999947 * jax.random.normal(jax.random.fold_in(_rk, 1), (64, 3, 96, 96), jnp.float32)
        return x
    x = _rec_inputs()

    def _L0_tok_setup():
        import jax, jax.numpy as jnp
        import numpy as np
        B, C, H, W = (64, 3, 96, 96)
        P = 16
        HP, WP = (H // P, W // P)
        N = HP * WP
        F = C * P * P
        D = 256
        key = jax.random.key(seed)
        k1, k2, k3, k4, k5 = jax.random.split(key, 5)
        data = jax.random.normal(k1, (B, C, H, W), dtype=jnp.float32)
        lim = 1.0 / np.sqrt(F)
        W_lin = jax.random.uniform(k2, (D, F), minval=-lim, maxval=lim, dtype=jnp.float32)
        b_lin = jax.random.uniform(k3, (D,), minval=-lim, maxval=lim, dtype=jnp.float32)
        class_token = jax.random.normal(k4, (1, 1, D), dtype=jnp.float32)
        position_embeddings = jax.random.normal(k5, (1, N + 1, D), dtype=jnp.float32)
        return {'data': data, 'W_lin': W_lin, 'b_lin': b_lin, 'class_token': class_token, 'position_embeddings': position_embeddings}
    _L0_tok_all = _L0_tok_setup()
    _L0_tok_in = {k: v for k, v in _L0_tok_all.items() if k in ('W_lin', 'b_lin', 'class_token', 'position_embeddings')}
    del _L0_tok_all

    def _L0_attn_setup():
        import jax, jax.numpy as jnp
        import numpy as np
        B, T, D = (2, 512, 256)
        HEAD_DIM, N_HEADS, N_HH, HEAD_V_DIM, CONV_SIZE = (128, 8, 3, 128, 4)

        def _short_conv(x, w):
            cs = w.shape[-1]
            t = x.shape[1]
            xp = jnp.pad(x, ((0, 0), (cs - 1, 0), (0, 0)))
            y = sum((xp[:, i:i + t, :] * w[:, i] for i in range(cs)))
            return jax.nn.silu(y)

        def _l2norm(x, eps=1e-06):
            return x * jax.lax.rsqrt(jnp.sum(x * x, -1, keepdims=True) + eps)

        def _forward(x, Wq, Wk, Wv, Wb, Wa, A_log, dt_bias, conv_q, conv_k, conv_v, Wg, rms_weight, Wo):
            b, t, _ = x.shape
            h, d, dv, nh = (N_HEADS, HEAD_DIM, HEAD_V_DIM, N_HH)
            q = _short_conv(x @ Wq, conv_q).reshape(b, t, h, d)
            k = _short_conv(x @ Wk, conv_k).reshape(b, t, nh, h, d).transpose(0, 1, 3, 2, 4)
            v = _short_conv(x @ Wv, conv_v).reshape(b, t, nh, h, dv).transpose(0, 1, 3, 2, 4)
            beta = 2.0 * jax.nn.sigmoid(x @ Wb).reshape(b, t, nh, h).transpose(0, 1, 3, 2)
            g = -jnp.exp(A_log) * jax.nn.softplus(x @ Wa + dt_bias)
            q = _l2norm(q) * d ** (-0.5)
            k = _l2norm(k)

            def step(S, inp):
                qt, kt, vt, bt, gt = inp
                S = S * jnp.exp(gt)[..., None, None]
                for i in range(nh):
                    ki, vi, bi = (kt[:, :, i], vt[:, :, i], bt[:, :, i])
                    kS = jnp.einsum('bhd,bhde->bhe', ki, S)
                    S = S + bi[..., None, None] * (ki[..., None] * (vi - kS)[:, :, None, :])
                o = jnp.einsum('bhd,bhde->bhe', qt, S)
                return (S, o)
            xs = tuple((jnp.moveaxis(a, 1, 0) for a in (q, k, v, beta, g)))
            S0 = jnp.zeros((b, h, d, dv), x.dtype)
            _, o = jax.lax.scan(step, S0, xs)
            o = jnp.moveaxis(o, 0, 1)
            gate = (x @ Wg).reshape(b, t, h, dv)
            o = o * jax.lax.rsqrt(jnp.mean(o * o, -1, keepdims=True) + 1e-05) * rms_weight
            o = o * jax.nn.silu(gate)
            return o.reshape(b, t, h * dv) @ Wo
        key = jax.random.key(seed)
        ks = jax.random.split(key, 16)
        h, d, dv, nh, cs = (N_HEADS, HEAD_DIM, HEAD_V_DIM, N_HH, CONV_SIZE)
        f = lambda k, shape, s=0.02: jax.random.normal(k, shape, jnp.float32) * s
        return {'x': f(ks[0], (B, T, D), 1.0), 'cos': f(ks[1], (T, d), 1.0), 'sin': f(ks[2], (T, d), 1.0), 'Wq': f(ks[3], (D, h * d)), 'Wk': f(ks[4], (D, h * d * nh)), 'Wv': f(ks[5], (D, h * dv * nh)), 'Wb': f(ks[6], (D, h * nh)), 'Wa': f(ks[7], (D, h)), 'A_log': jnp.log(jax.random.uniform(ks[8], (h,), jnp.float32, 0.5, 8.0)), 'dt_bias': f(ks[9], (h,), 0.1), 'conv_q': f(ks[10], (h * d, cs), 0.5), 'conv_k': f(ks[11], (h * d * nh, cs), 0.5), 'conv_v': f(ks[12], (h * dv * nh, cs), 0.5), 'Wg': f(ks[13], (D, h * dv)), 'rms_weight': jnp.ones((dv,), jnp.float32), 'Wo': f(ks[14], (h * dv, D))}
    _L0_attn_all = _L0_attn_setup()
    _L0_attn_in = {k: v for k, v in _L0_attn_all.items() if k in ('cos', 'sin', 'Wq', 'Wk', 'Wv', 'Wb', 'Wa', 'A_log', 'dt_bias', 'conv_q', 'conv_k', 'conv_v', 'Wg', 'rms_weight', 'Wo')}
    del _L0_attn_all

    def _L0_ffn_setup():
        import jax, jax.numpy as jnp
        import numpy as np
        DIM = 256
        HIDDEN = 1024
        E = 8
        B, S = (2, 1024)
        key = jax.random.key(seed)
        ks = jax.random.split(key, 8)
        sd = 1.0 / np.sqrt(DIM)
        sh = 1.0 / np.sqrt(HIDDEN)
        return {'x': jax.random.normal(ks[0], (B, S, DIM), dtype=jnp.float32), 'router_w': jax.random.uniform(ks[1], (DIM, E), jnp.float32, -sd, sd), 'router_b': jax.random.uniform(ks[2], (E,), jnp.float32, -sd, sd), 'w1': jax.random.uniform(ks[3], (E, DIM, 2 * HIDDEN), jnp.float32, -sd, sd), 'b1': jax.random.uniform(ks[4], (E, 2 * HIDDEN), jnp.float32, -sd, sd), 'w2': jax.random.uniform(ks[5], (E, HIDDEN, DIM), jnp.float32, -sh, sh), 'b2': jax.random.uniform(ks[6], (E, DIM), jnp.float32, -sh, sh)}
    _L0_ffn_all = _L0_ffn_setup()
    _L0_ffn_in = {k: v for k, v in _L0_ffn_all.items() if k in ('router_w', 'router_b', 'w1', 'b1', 'w2', 'b2')}
    del _L0_ffn_all

    def _L1_attn_setup():
        import jax, jax.numpy as jnp
        import numpy as np
        B, T, C, H = (4, 512, 256, 16)
        INIT_STD = 0.02
        key = jax.random.key(seed)
        ks = jax.random.split(key, 9)
        x = jax.random.normal(ks[0], (B, T, C), dtype=jnp.float32)

        def dense(kw):
            return jax.random.normal(kw, (C, C), dtype=jnp.float32) * INIT_STD
        return {'x': x, 'Wq': dense(ks[1]), 'bq': jnp.zeros((C,), jnp.float32), 'Wk': dense(ks[2]), 'bk': jnp.zeros((C,), jnp.float32), 'Wv': dense(ks[3]), 'bv': jnp.zeros((C,), jnp.float32), 'Wo': dense(ks[4]), 'bo': jnp.zeros((C,), jnp.float32)}
    _L1_attn_all = _L1_attn_setup()
    _L1_attn_in = {k: v for k, v in _L1_attn_all.items() if k in ('Wq', 'bq', 'Wk', 'bk', 'Wv', 'bv', 'Wo', 'bo')}
    del _L1_attn_all

    def _L1_ffn_setup():
        import jax, jax.numpy as jnp
        import numpy as np
        D_MODEL = 256
        MLP_DIM = 1024
        N_EXPERTS = 8
        B, T = (4, 256)
        key = jax.random.key(seed)
        ks = jax.random.split(key, 7)
        scale_in = (1.0 / D_MODEL) ** 0.5
        scale_out = (1.0 / MLP_DIM) ** 0.5
        bound_g = (1.0 / D_MODEL) ** 0.5
        w_gate = jax.random.uniform(ks[0], (D_MODEL, N_EXPERTS), minval=-bound_g, maxval=bound_g, dtype=jnp.float32)
        b_gate = jax.random.uniform(ks[1], (N_EXPERTS,), minval=-bound_g, maxval=bound_g, dtype=jnp.float32)
        W1 = jax.random.uniform(ks[2], (N_EXPERTS, D_MODEL, MLP_DIM), minval=-scale_in, maxval=scale_in, dtype=jnp.float32)
        b1 = jnp.zeros((N_EXPERTS, MLP_DIM), dtype=jnp.float32)
        W2 = jax.random.uniform(ks[3], (N_EXPERTS, MLP_DIM, D_MODEL), minval=-scale_out, maxval=scale_out, dtype=jnp.float32)
        b2 = jnp.zeros((N_EXPERTS, D_MODEL), dtype=jnp.float32)
        x = jax.random.normal(ks[4], (B, T, D_MODEL), dtype=jnp.float32)
        return {'x': x, 'w_gate': w_gate, 'b_gate': b_gate, 'W1': W1, 'b1': b1, 'W2': W2, 'b2': b2}
    _L1_ffn_all = _L1_ffn_setup()
    _L1_ffn_in = {k: v for k, v in _L1_ffn_all.items() if k in ('w_gate', 'b_gate', 'W1', 'b1', 'W2', 'b2')}
    del _L1_ffn_all
    return {'x': x, 'L0_tok_W_lin': _L0_tok_in['W_lin'], 'L0_tok_b_lin': _L0_tok_in['b_lin'], 'L0_tok_class_token': _L0_tok_in['class_token'], 'L0_tok_position_embeddings': _L0_tok_in['position_embeddings'], 'L0_attn_cos': _L0_attn_in['cos'], 'L0_attn_sin': _L0_attn_in['sin'], 'L0_attn_Wq': _L0_attn_in['Wq'], 'L0_attn_Wk': _L0_attn_in['Wk'], 'L0_attn_Wv': _L0_attn_in['Wv'], 'L0_attn_Wb': _L0_attn_in['Wb'], 'L0_attn_Wa': _L0_attn_in['Wa'], 'L0_attn_A_log': _L0_attn_in['A_log'], 'L0_attn_dt_bias': _L0_attn_in['dt_bias'], 'L0_attn_conv_q': _L0_attn_in['conv_q'], 'L0_attn_conv_k': _L0_attn_in['conv_k'], 'L0_attn_conv_v': _L0_attn_in['conv_v'], 'L0_attn_Wg': _L0_attn_in['Wg'], 'L0_attn_rms_weight': _L0_attn_in['rms_weight'], 'L0_attn_Wo': _L0_attn_in['Wo'], 'L0_ffn_router_w': _L0_ffn_in['router_w'], 'L0_ffn_router_b': _L0_ffn_in['router_b'], 'L0_ffn_w1': _L0_ffn_in['w1'], 'L0_ffn_b1': _L0_ffn_in['b1'], 'L0_ffn_w2': _L0_ffn_in['w2'], 'L0_ffn_b2': _L0_ffn_in['b2'], 'L1_attn_Wq': _L1_attn_in['Wq'], 'L1_attn_bq': _L1_attn_in['bq'], 'L1_attn_Wk': _L1_attn_in['Wk'], 'L1_attn_bk': _L1_attn_in['bk'], 'L1_attn_Wv': _L1_attn_in['Wv'], 'L1_attn_bv': _L1_attn_in['bv'], 'L1_attn_Wo': _L1_attn_in['Wo'], 'L1_attn_bo': _L1_attn_in['bo'], 'L1_ffn_w_gate': _L1_ffn_in['w_gate'], 'L1_ffn_b_gate': _L1_ffn_in['b_gate'], 'L1_ffn_W1': _L1_ffn_in['W1'], 'L1_ffn_b1': _L1_ffn_in['b1'], 'L1_ffn_W2': _L1_ffn_in['W2'], 'L1_ffn_b2': _L1_ffn_in['b2']}

def reference(x, L0_tok_W_lin, L0_tok_b_lin, L0_tok_class_token, L0_tok_position_embeddings, L0_attn_cos, L0_attn_sin, L0_attn_Wq, L0_attn_Wk, L0_attn_Wv, L0_attn_Wb, L0_attn_Wa, L0_attn_A_log, L0_attn_dt_bias, L0_attn_conv_q, L0_attn_conv_k, L0_attn_conv_v, L0_attn_Wg, L0_attn_rms_weight, L0_attn_Wo, L0_ffn_router_w, L0_ffn_router_b, L0_ffn_w1, L0_ffn_b1, L0_ffn_w2, L0_ffn_b2, L1_attn_Wq, L1_attn_bq, L1_attn_Wk, L1_attn_bk, L1_attn_Wv, L1_attn_bv, L1_attn_Wo, L1_attn_bo, L1_ffn_w_gate, L1_ffn_b_gate, L1_ffn_W1, L1_ffn_b1, L1_ffn_W2, L1_ffn_b2):
    import jax
    import jax.numpy as jnp

    def _L0_tok_ref(data, W_lin, b_lin, class_token, position_embeddings):
        import jax, jax.numpy as jnp
        import numpy as np
        B, C, H, W = (64, 3, 96, 96)
        P = 16
        HP, WP = (H // P, W // P)
        N = HP * WP
        F = C * P * P
        D = 256
        b = data.shape[0]
        x = data.reshape(b, C, HP, P, WP, P)
        x = x.transpose(0, 2, 4, 1, 3, 5).reshape(b, N, F)
        x = jnp.einsum('bnf,df->bnd', x, W_lin) + b_lin
        cls = jnp.broadcast_to(class_token, (b, 1, D))
        out = jnp.concatenate([cls, x], axis=1) + position_embeddings
        return out

    def _L0_attn_ref(x, cos, sin, Wq, Wk, Wv, Wb, Wa, A_log, dt_bias, conv_q, conv_k, conv_v, Wg, rms_weight, Wo):
        import jax, jax.numpy as jnp
        import numpy as np
        B, T, D = (2, 512, 256)
        HEAD_DIM, N_HEADS, N_HH, HEAD_V_DIM, CONV_SIZE = (128, 8, 3, 128, 4)

        def _short_conv(x, w):
            cs = w.shape[-1]
            t = x.shape[1]
            xp = jnp.pad(x, ((0, 0), (cs - 1, 0), (0, 0)))
            y = sum((xp[:, i:i + t, :] * w[:, i] for i in range(cs)))
            return jax.nn.silu(y)

        def _l2norm(x, eps=1e-06):
            return x * jax.lax.rsqrt(jnp.sum(x * x, -1, keepdims=True) + eps)

        def _forward(x, Wq, Wk, Wv, Wb, Wa, A_log, dt_bias, conv_q, conv_k, conv_v, Wg, rms_weight, Wo):
            b, t, _ = x.shape
            h, d, dv, nh = (N_HEADS, HEAD_DIM, HEAD_V_DIM, N_HH)
            q = _short_conv(x @ Wq, conv_q).reshape(b, t, h, d)
            k = _short_conv(x @ Wk, conv_k).reshape(b, t, nh, h, d).transpose(0, 1, 3, 2, 4)
            v = _short_conv(x @ Wv, conv_v).reshape(b, t, nh, h, dv).transpose(0, 1, 3, 2, 4)
            beta = 2.0 * jax.nn.sigmoid(x @ Wb).reshape(b, t, nh, h).transpose(0, 1, 3, 2)
            g = -jnp.exp(A_log) * jax.nn.softplus(x @ Wa + dt_bias)
            q = _l2norm(q) * d ** (-0.5)
            k = _l2norm(k)

            def step(S, inp):
                qt, kt, vt, bt, gt = inp
                S = S * jnp.exp(gt)[..., None, None]
                for i in range(nh):
                    ki, vi, bi = (kt[:, :, i], vt[:, :, i], bt[:, :, i])
                    kS = jnp.einsum('bhd,bhde->bhe', ki, S)
                    S = S + bi[..., None, None] * (ki[..., None] * (vi - kS)[:, :, None, :])
                o = jnp.einsum('bhd,bhde->bhe', qt, S)
                return (S, o)
            xs = tuple((jnp.moveaxis(a, 1, 0) for a in (q, k, v, beta, g)))
            S0 = jnp.zeros((b, h, d, dv), x.dtype)
            _, o = jax.lax.scan(step, S0, xs)
            o = jnp.moveaxis(o, 0, 1)
            gate = (x @ Wg).reshape(b, t, h, dv)
            o = o * jax.lax.rsqrt(jnp.mean(o * o, -1, keepdims=True) + 1e-05) * rms_weight
            o = o * jax.nn.silu(gate)
            return o.reshape(b, t, h * dv) @ Wo
        return _forward(x, Wq, Wk, Wv, Wb, Wa, A_log, dt_bias, conv_q, conv_k, conv_v, Wg, rms_weight, Wo)

    def _L0_ffn_ref(x, router_w, router_b, w1, b1, w2, b2):
        import jax, jax.numpy as jnp
        import numpy as np
        DIM = 256
        HIDDEN = 1024
        E = 8
        B, S = (2, 1024)
        logits = jnp.einsum('bsd,de->bse', x, router_w) + router_b
        probs = jax.nn.softmax(logits, axis=-1)
        top1 = jnp.argmax(probs, axis=-1)
        out = jnp.zeros_like(x)
        for i in range(E):
            h = jnp.einsum('bsd,df->bsf', x, w1[i]) + b1[i]
            a, g = jnp.split(h, 2, axis=-1)
            y = jnp.einsum('bsh,hd->bsd', a * jax.nn.sigmoid(g), w2[i]) + b2[i]
            out = out + jnp.where((top1 == i)[..., None], y, 0.0)
        return out

    def _L1_attn_ref(x, Wq, bq, Wk, bk, Wv, bv, Wo, bo):
        import jax, jax.numpy as jnp
        import numpy as np
        B, T, C, H = (4, 512, 256, 16)
        INIT_STD = 0.02
        b, t, c = x.shape
        hd = c // H

        def split_heads(y):
            return jnp.transpose(y.reshape(b, t, H, hd), (0, 2, 1, 3))
        q = split_heads(x @ Wq + bq)
        k = split_heads(x @ Wk + bk)
        v = split_heads(x @ Wv + bv)
        scale = 1.0 / jnp.sqrt(jnp.float32(hd))
        att = jnp.einsum('bhqd,bhkd->bhqk', q, k) * scale
        mask = jnp.tril(jnp.ones((t, t), dtype=bool))[None, None]
        att = jnp.where(mask, att, jnp.float32(-jnp.inf))
        att = jax.nn.softmax(att, axis=-1)
        y = jnp.einsum('bhqk,bhkd->bhqd', att, v)
        y = jnp.transpose(y, (0, 2, 1, 3)).reshape(b, t, c)
        return y @ Wo + bo

    def _L1_ffn_ref(x, w_gate, b_gate, W1, b1, W2, b2):
        import jax, jax.numpy as jnp
        import numpy as np
        D_MODEL = 256
        MLP_DIM = 1024
        N_EXPERTS = 8
        B, T = (4, 256)
        b, t, d = x.shape
        x_flat = x.reshape(b * t, d)
        logits = x_flat @ w_gate + b_gate
        probs = jax.nn.softmax(logits, axis=-1)
        route_p = jnp.max(probs, axis=-1)
        route_idx = jnp.argmax(probs, axis=-1)
        h = jnp.einsum('nd,edm->enm', x_flat, W1) + b1[:, None, :]
        h = jax.nn.relu(h)
        y = jnp.einsum('enm,emd->end', h, W2) + b2[:, None, :]
        n = b * t
        out = y[route_idx, jnp.arange(n)] * route_p[:, None]
        return out.reshape(b, t, d)
    h = _L0_tok_ref(x, L0_tok_W_lin, L0_tok_b_lin, L0_tok_class_token, L0_tok_position_embeddings)
    h = h + _L0_attn_ref(_layernorm(h, axis=-1), L0_attn_cos, L0_attn_sin, L0_attn_Wq, L0_attn_Wk, L0_attn_Wv, L0_attn_Wb, L0_attn_Wa, L0_attn_A_log, L0_attn_dt_bias, L0_attn_conv_q, L0_attn_conv_k, L0_attn_conv_v, L0_attn_Wg, L0_attn_rms_weight, L0_attn_Wo)
    h = h + _L0_ffn_ref(_layernorm(h, axis=-1), L0_ffn_router_w, L0_ffn_router_b, L0_ffn_w1, L0_ffn_b1, L0_ffn_w2, L0_ffn_b2)
    h = h + _L1_attn_ref(_layernorm(h, axis=-1), L1_attn_Wq, L1_attn_bq, L1_attn_Wk, L1_attn_bk, L1_attn_Wv, L1_attn_bv, L1_attn_Wo, L1_attn_bo)
    h = h + _L1_ffn_ref(_layernorm(h, axis=-1), L1_ffn_w_gate, L1_ffn_b_gate, L1_ffn_W1, L1_ffn_b1, L1_ffn_W2, L1_ffn_b2)
    return h

_drawn_inputs = setup_inputs


def setup_inputs(seed=0):
    import zlib

    import numpy as np

    out = dict(_drawn_inputs(seed))
    spreads = {'L0_attn_rms_weight': (1.0, 0.6),
     'L1_attn_bq': (0.0, 0.8),
     'L1_attn_bk': (0.0, 0.8),
     'L1_attn_bv': (0.0, 0.1),
     'L1_attn_bo': (0.0, 0.1),
     'L1_ffn_b1': (0.0, 0.8),
     'L1_ffn_b2': (0.0, 0.352)}
    factors = {'L0_attn_Wb': 3.759,
     'L0_attn_Wa': 6.191,
     'L0_attn_dt_bias': 6.798,
     'L0_ffn_b1': 5.533,
     'L0_ffn_b2': 3.465,
     'L1_attn_Wq': 8.0,
     'L1_attn_Wk': 8.0,
     'L1_ffn_b_gate': 5.831}
    for name, (base, spread) in spreads.items():
        noise = np.random.default_rng([zlib.crc32(name.encode()), seed]).standard_normal(out[name].shape)
        drawn = base * np.exp(spread * noise) if base else spread * noise
        out[name] = jnp.asarray(drawn.astype(out[name].dtype))
    for name, factor in factors.items():
        out[name] = (out[name] * factor).astype(out[name].dtype)
    return out
```

```python
import numpy as np
import concourse.bass as bass
from concourse import mybir
from contextlib import ExitStack

F32 = mybir.dt.float32
I32 = mybir.dt.int32
ALU = mybir.AluOpType
ACT = mybir.ActivationFunctionType
AX = mybir.AxisListType

A_LINKS = 22
A_XN = 4
A_XN2 = 14
POOL_LINKS = 3
DVE_LINKS = 49
LINK_XN = 4
LINK_XN2 = 45

IMAGES, CHANNELS, SIDE, PATCH = 64, 3, 96, 16
GRID = SIDE // PATCH
PATCHES = GRID * GRID
T = PATCHES + 1
F = CHANNELS * PATCH * PATCH
FC = F // 128
D = 256
DC = D // 128
PER = 3
ROWS = PER * T
GROUPS = -(-IMAGES // PER)
FIRST_OF_LAST = IMAGES - PER
NEW_ROWS_OF_LAST = (IMAGES - PER * (GROUPS - 1)) * T
TOKENS = GROUPS * ROWS

H, HD, NH, TAPS = 8, 128, 3, 4
MICRO = NH * T
QB, KB, VB = H, NH * H, NH * H
CB = QB + KB + VB
CQ = CB // 4
LEVELS = [1, 2, 4, 8, 16, 32, 64]
E = 8
HID = 1024
AH, AD = 16, 16


def bc(ap, axis, n):
    shape = list(ap.shape)
    shape.insert(axis, n)
    return ap.unsqueeze(axis).to_broadcast(shape)


OPEN = 1


def open_counts(eng, sems):
    for x in sems:
        eng.sem_inc(x, OPEN)


class Chain:

    def __init__(self, eng, sem, per_turn, turn):
        self.eng, self.sem, self.per, self.turn, self.n = eng, sem, per_turn, turn, 0

    def link(self, ins):
        ins.then_inc(self.sem, 1)
        self.n += 1

    def wait(self):
        self.eng.wait_ge(self.sem, OPEN + self.turn * self.per + self.n)


def layer_norm(dve, chain, st, mv, ve, rstd, xn, h, var_ready, rstd_ready, turn, nth, per):
    chain.link(dve.bn_stats(st, h))
    chain.wait()
    dve.memset(ve, 0.0)
    chain.link(dve.bn_aggr(mv, st))
    chain.wait()
    dve.tensor_scalar(ve, mv[:, 1:2], 1e-5, None, ALU.add).then_inc(var_ready, 1)
    dve.wait_ge(rstd_ready, OPEN + turn * per + nth)
    chain.link(dve.tensor_scalar(xn, h, mv[:, 0:1], rstd, ALU.subtract, ALU.mult))


def delta_phase(nc, ctx, a, h_dram, xT_dram, route):
    def sb(name, shape, dt=F32):
        return ctx.enter_context(nc.sbuf_tensor(name, shape, dt))

    def sem(name):
        return ctx.enter_context(nc.semaphore(name))

    bank = [ctx.enter_context(nc.psum_tensor(f"d_bank{i}", [128, 512], F32)) for i in range(8)]

    wlin = sb("wlin", [128, FC, D])
    wqkv = sb("wqkv", [128, DC, CB * 128])
    wgate = sb("wgate", [128, DC, H * HD])
    wout = sb("wout", [128, H, D])
    wab = sb("wab", [128, DC, 32])
    wrt = sb("wrt", [128, DC, E])
    taps = sb("taps", [128, CB, TAPS])
    ident = sb("ident", [128, 128])
    addend = sb("addend", [ROWS, D])
    pos3 = sb("pos3", [ROWS, D])
    dtb = sb("dtb", [ROWS, H])
    alog = sb("alog", [ROWS, H])
    negA = sb("negA", [ROWS, H])
    rmsw = sb("rmsw", [ROWS, HD])
    rbias = sb("rbias", [ROWS, E])
    countdown = sb("countdown", [ROWS, E])
    phalf = sb("phalf", [ROWS, 32])
    nhalf = sb("nhalf", [ROWS, 32])
    ones = sb("ones", [128, 1])
    m_low = sb("m_low", [MICRO, MICRO])
    m_pair = sb("m_pair", [MICRO, MICRO])
    m_lvl = sb("m_lvl", [MICRO, len(LEVELS), MICRO])
    s_gt = sb("s_gt", [ROWS, T])
    s_le = sb("s_le", [ROWS, T])
    up_to = sb("up_to", [ROWS, PER, MICRO])
    after = sb("after", [ROWS, PER, MICRO])
    causal = sb("causal", [MICRO, T])
    spread = sb("spread", [ROWS, PER * NH, MICRO])

    xin = sb("xin", [128, FC, ROWS])
    st = sb("st", [ROWS, 6])
    mv = sb("mv", [ROWS, 2])
    ve = sb("ve", [ROWS, 1])
    rstd = sb("rstd", [ROWS, 1])
    hcur = sb("hcur", [ROWS, D])
    xn = sb("xn", [ROWS, D])
    xnT = sb("xnT", [128, DC, ROWS])
    blog = sb("blog", [ROWS, NH * H])
    sp = sb("sp", [ROWS, 4, H])
    g = sb("g", [ROWS, H])
    g_gt = sb("g_gt", [ROWS, H, T])
    g_le = sb("g_le", [ROWS, H, T])
    y = sb("y", [128, 2, 4, ROWS])
    sg = sb("sg", [128, 2, 4, ROWS])
    Q = sb("Q", [128, H, ROWS])
    K = sb("K", [128, PER, H, MICRO])
    V = sb("V", [128, PER, H, MICRO])
    sq = sb("sq", [128, H, ROWS])
    r2 = sb("r2", [MICRO, 4 * H])
    beta = sb("beta", [MICRO, PER * H])
    nbr2 = sb("nbr2", [MICRO, PER * H])
    rr = sb("rr", [MICRO, PER * H])
    br = sb("br", [MICRO, PER * H])
    dj = sb("dj", [MICRO, 2, H, T])
    dm = sb("dm", [MICRO, H, T])
    di = sb("di", [MICRO, 2, H, T])
    dmask = sb("dmask", [MICRO, 4, MICRO])
    N = sb("N", [MICRO, 2, 4, MICRO])
    X = sb("X", [MICRO, 2, 4, MICRO])
    Y = sb("Y", [MICRO, 2, 4, MICRO])
    Z = sb("Z", [MICRO, 2, 4, MICRO])
    C = sb("C", [MICRO, 2, 4, HD])
    EE = sb("EE", [MICRO, 2, 4, HD])
    W = sb("W", [MICRO, PER, H, HD])
    PT = sb("PT", [MICRO, PER, H, ROWS])
    gs = sb("gs", [ROWS, H * HD])
    gsig = sb("gsig", [ROWS, 512])
    osq = EE[:, :, :, :].rearrange("p a b c -> p (a b c)")
    O = C[:, :, :, :].rearrange("p a b c -> p (a b c)")
    hout = sb("hout", [ROWS, D])
    xTout = sb("xTout", [128, DC, ROWS])
    rms = sb("rms", [ROWS, 4, H])
    OT = sq
    lg = sb("lg", [ROWS, E])
    mx = sb("mx", [ROWS, 2])

    s = {n: sem("d_" + n) for n in """w_tok w_const w_small w_gate w_out
        x_loaded tok_full dve_chain var_ready rstd_ready xt_full xt_ready tok_used ab_full ab_read
        conv_full conv_init taps_done sig_done prod_done q_sq k_sq sq_used ks_full ks_read r2_ready
        rr_ready be_full be_sig br_ready gate_full gate_sig gate_mul gate_wt
        spl spl_ln g_ready gt_ready d_full d_exp dm_ready di_ready dmask_ready
        kk_full noff_ready n_ready x_pair kq_full pt_ready vt_full c_ready
        nt_full z_full z_ready x_full x_ready y_full y_ready e_full e_ready w_full wv_ready
        o_full o_sq o_mean o_pow o_read ot_full ot_ready wo_full h_ready h_stored xT_kept pool_chain act_chain
        x2t_full x2t_ready lg_full consts route_ready setup setup2""".split()}

    block = ctx.enter_context(nc.Block())
    IMG_B = 2
    IB = PER * IMG_B

    @block.sync
    def _(sp_):
        open_counts(sp_, s.values())
        sp_.dma_start(wlin[:, :, :], a["wlin"]).then_inc(s["w_tok"], 16)
        sp_.dma_start(xin[:, :, :], a["x"][0]).then_inc(s["x_loaded"], 16)
        sp_.dma_start(pos3[:, :], a["pos3"]).then_inc(s["w_tok"], 16)
        sp_.dma_start(addend[:, :], a["rowadd"]).then_inc(s["w_tok"], 16)
        small = [(wab, "wab"), (wrt, "wrt"), (taps, "taps"), (ident, "ident"), (m_low, "m_low"),
                 (m_pair, "m_pair"), (m_lvl, "m_lvl"), (s_gt, "s_gt"), (s_le, "s_le"),
                 (up_to, "up_to"), (after, "after"), (causal, "causal"), (spread, "spread"),
                 (countdown, "countdown")]
        for t, n in small:
            sp_.dma_start(t[tuple(slice(None) for _ in t.shape)], a[n]).then_inc(s["w_const"], 16)
        for t, n in ((dtb, "dtb"), (alog, "alog"), (rmsw, "rmsw"), (rbias, "rbias")):
            sp_.dma_start(t[:, :], a[n].partition_broadcast(ROWS)).then_inc(s["w_const"], 16)
        for c in range(DC):
            sp_.dma_start(wqkv[:, c, :], a["wqkv"][:, c, :]).then_inc(s["w_small"], 16)
        sp_.dma_start(wgate[:, :, :], a["wgate"]).then_inc(s["w_gate"], 16)
        sp_.dma_start(wout[:, :, :], a["wout"]).then_inc(s["w_out"], 16)
        with sp_.Fori(0, GROUPS) as gi:
            sp_.wait_ge(s["tok_full"], OPEN + gi + 1)
            sp_.dma_start(xin[:, :, :], a["x"][bass.ds(gi + 1, 1)].rearrange("a p c n -> p (a c) n"))\
                .then_inc(s["x_loaded"], 16)
            sp_.wait_ge(s["h_ready"], OPEN + gi + 1)
            sp_.dma_start(h_dram[:, bass.ds(gi, 1), :].rearrange("p a d -> p (a d)"), hout[:, :]).then_inc(s["h_stored"], 16)
            sp_.wait_ge(s["xT_kept"], OPEN + gi + 1)
            sp_.dma_start(xT_dram[:, :, bass.ds(gi * ROWS, ROWS)], xTout[:, :, :]).then_inc(s["h_stored"], 16)
        sp_.wait_ge(s["h_stored"], OPEN + 32 * GROUPS)
        sp_.wait_ge(s["x_loaded"], OPEN + 16 * (GROUPS + 1))
    CONST = 16 * 18

    @block.gpsimd
    def _(pool):
        nc.gpsimd.memset(phalf[:, :], 0.5).then_inc(s["consts"], 1)
        nc.gpsimd.memset(nhalf[:, :], -0.5).then_inc(s["consts"], 1)
        nc.gpsimd.memset(ones[:, :], 1.0).then_inc(s["consts"], 1)
        nc.gpsimd.memset(PT[:, :, :, :], 0.0).then_inc(s["consts"], 1)
        pool.wait_ge(s["w_const"], OPEN + CONST)
        with pool.Fori(0, GROUPS) as gi:
            ch = Chain(pool, s["pool_chain"], POOL_LINKS, gi)
            pool.wait_ge(s["var_ready"], OPEN + gi * 2 + 1)
            pool.tensor_tensor(rstd[:, :], ve[:, :], nhalf[:, 0:1], ALU.pow).then_inc(s["rstd_ready"], 1)
            for b in range(CQ):
                kind, i, hh = block_of(b)
                pool.wait_ge(s["sig_done"], OPEN + gi * CQ + b + 1)
                if kind == "q":
                    out = Q[:, hh:hh + 4, :]
                    i0, i1 = y[:, b % 2], sg[:, b % 2]
                    pool.tensor_tensor(out, i0, i1, ALU.mult).then_inc(s["prod_done"], 1)
                else:
                    dst = K if kind == "k" else V
                    for m in range(PER):
                        out = dst[:, m, hh:hh + 4, i:MICRO:NH]
                        c_ = slice(m * T, (m + 1) * T)
                        ins = pool.tensor_tensor(out, y[:, b % 2, :, c_], sg[:, b % 2, :, c_], ALU.mult)
                        if m == PER - 1:
                            ins.then_inc(s["prod_done"], 1)
                if b == 1:
                    pool.wait_ge(s["prod_done"], OPEN + gi * CQ + 2)
                    pool.wait_ge(s["ks_full"], OPEN + gi * 4)
                    pool.tensor_tensor(sq[:, :, :], Q[:, :, :], Q[:, :, :], ALU.mult).then_inc(s["q_sq"], 1)
            pool.wait_ge(s["prod_done"], OPEN + gi * CQ + CQ)
            for m in range(PER):
                pool.wait_ge(s["ks_full"], OPEN + gi * 4 + m + 1)
                pool.tensor_tensor(sq[:, :, :], K[:, m], K[:, m], ALU.mult).then_inc(s["k_sq"], 1)
            pool.wait_ge(s["r2_ready"], OPEN + gi + 1)
            pool.tensor_tensor(rr[:, :], r2[:, H:], phalf[:, 0:PER * H], ALU.pow).then_inc(s["rr_ready"], 1)
            pool.wait_ge(s["g_ready"], OPEN + gi + 1)
            pool.tensor_tensor(g_gt[:, :, :], bc(g[:, :], 2, T), bc(s_gt[:, :], 1, H), ALU.mult)\
                .then_inc(s["gt_ready"], 1)
            pool.tensor_tensor(g_le[:, :, :], bc(g[:, :], 2, T), bc(s_le[:, :], 1, H), ALU.mult)\
                .then_inc(s["gt_ready"], 1)
            pool.wait_ge(s["br_ready"], OPEN + gi + 1)
            for m in range(PER):
                pool.wait_ge(s["d_exp"], OPEN + gi * 2 * PER + 2 * m + 2)
                ch.link(pool.tensor_tensor(dm[:, :, :], dj[:, m % 2], bc(nbr2[:, m * H:(m + 1) * H], 2, T),
                                           ALU.mult))
                pool.tensor_tensor(di[:, m % 2], di[:, m % 2], bc(causal[:, :], 1, H), ALU.mult)\
                    .then_inc(s["di_ready"], 1)
                for b in range(IMG_B):
                    n = m * IMG_B + b
                    ch.wait()
                    pool.wait_ge(s["noff_ready"], OPEN + gi * IB + n)
                    pool.tensor_tensor(
                        dmask[:, :, :].rearrange("p h (t i) -> p h t i", i=NH),
                        bc(dm[:, 4 * b:4 * b + 4, :], 3, NH),
                        bc(m_low[:, :].rearrange("p (t i) -> p t i", i=NH), 1, 4), ALU.mult)\
                        .then_inc(s["dmask_ready"], 1)
                    pool.wait_ge(s["noff_ready"], OPEN + gi * IB + n + 1)
                    pool.tensor_tensor(N[:, b], N[:, b], bc(ident[0:MICRO, 0:MICRO], 1, 4), ALU.add)\
                        .then_inc(s["n_ready"], 1)
                    pool.wait_ge(s["n_ready"], OPEN + gi * IB + n + 1)
                    pool.tensor_tensor(X[:, b], N[:, b], bc(m_pair[:, :], 1, 4), ALU.mult)\
                        .then_inc(s["x_pair"], 1)
            pool.wait_ge(s["o_mean"], OPEN + gi + 1)
            pool.tensor_tensor(rms[:, 3], rms[:, 2], phalf[0:ROWS, 0:H], ALU.pow).then_inc(s["o_pow"], 1)
            pool.wait_ge(s["var_ready"], OPEN + gi * 2 + 2)
            pool.tensor_tensor(rstd[:, :], ve[:, :], nhalf[:, 0:1], ALU.pow).then_inc(s["rstd_ready"], 1)
            assert ch.n == POOL_LINKS, ch.n

    @block.tensor
    def _(pe):
        def wait_bank_free(gi, k):
            if k >= 6:
                pe.wait_ge(s["taps_done"], OPEN + gi * CQ + k - 5)

        pe.wait_ge(s["w_tok"], OPEN + 48)
        pe.wait_ge(s["w_const"], OPEN + CONST)
        pe.wait_ge(s["consts"], OPEN + 4)
        with pe.Fori(0, GROUPS) as gi:
            pe.wait_ge(s["x_loaded"], OPEN + gi * 16 + 16)
            pe.wait_ge(s["route_ready"], OPEN + gi)
            for c in range(FC):
                ins = pe.matmul(bank[6][0:ROWS, 0:D], xin[:, c, :], wlin[:, c, :], start=c == 0, stop=c == FC - 1)
            ins.then_inc(s["tok_full"], 1)
            pe.wait_ge(s["dve_chain"], OPEN + gi * DVE_LINKS + LINK_XN)
            for c in range(DC):
                ins = pe.transpose(bank[7][:, c * ROWS:(c + 1) * ROWS], xn[:, c * 128:(c + 1) * 128],
                                   ident[0:ROWS, 0:ROWS])
            ins.then_inc(s["xt_full"], 1)
            pe.wait_ge(s["xt_ready"], OPEN + gi + 1)
            for c in range(DC):
                ins = pe.matmul(bank[6][0:ROWS, 256:288], xnT[:, c, :], wab[:, c, :], start=c == 0, stop=c == DC - 1)
            ins.then_inc(s["ab_full"], 1)
            pe.wait_ge(s["w_small"], OPEN + 32)
            for k in range(CQ):
                wait_bank_free(gi, k)
                for j in range(4):
                    blk = 4 * k + j
                    for c in range(DC):
                        ins = pe.matmul(bank[k % 6][:, j * ROWS:(j + 1) * ROWS],
                                        wqkv[:, c, blk * 128:(blk + 1) * 128], xnT[:, c, :],
                                        start=c == 0, stop=c == DC - 1)
                ins.then_inc(s["conv_full"], 1)
            pe.wait_ge(s["w_gate"], OPEN + 16)
            for n in range(2):
                if n == 0:
                    pe.wait_ge(s["ab_read"], OPEN + gi * 2 + 2)
                for c in range(DC):
                    ins = pe.matmul(bank[6 + n][0:ROWS, :], xnT[:, c, :], wgate[:, c, n * 512:(n + 1) * 512],
                                    start=c == 0, stop=c == DC - 1)
                ins.then_inc(s["gate_full"], 1)
            for r in range(4):
                if r == 0:
                    pe.wait_ge(s["gate_mul"], OPEN + gi * 2 + 2)
                    pe.wait_ge(s["q_sq"], OPEN + gi + 1)
                else:
                    pe.wait_ge(s["k_sq"], OPEN + gi * PER + r)
                for hh in range(H):
                    ins = pe.matmul(bank[6][0:MICRO, r * H + hh:r * H + hh + 1], sq[:, hh, :], ones[:, :],
                                    start=True, stop=True)
                ins.then_inc(s["ks_full"], 1)
            for m in range(PER):
                for i in range(NH):
                    ins = pe.matmul(bank[7][0:MICRO, m * H:(m + 1) * H], spread[:, m * NH + i, :],
                                    blog[:, i * H:(i + 1) * H], start=i == 0, stop=i == NH - 1)
            ins.then_inc(s["be_full"], 1)
            pe.wait_ge(s["gt_ready"], OPEN + gi * 2 + 2)
            pe.wait_ge(s["prod_done"], OPEN + gi * CQ + CQ)
            pe.wait_ge(s["taps_done"], OPEN + gi * CQ + CQ)
            for m in range(PER):
                if m == 0:
                    pe.wait_ge(s["ks_read"], OPEN + gi + 1)
                    pe.wait_ge(s["be_sig"], OPEN + gi + 1)
                else:
                    pe.wait_ge(s["pt_ready"], OPEN + gi * PER + m)
                    pe.wait_ge(s["c_ready"], OPEN + gi * IB + 2 * m)
                for n, (lhs, rhs) in enumerate(((up_to, g_gt), (after, g_le))):
                    pe.matmul(bank[6 + n][0:MICRO, 0:H * T], lhs[:, m, :],
                              rhs[:, :, :].rearrange("p h t -> p (h t)"), start=True, stop=True)\
                        .then_inc(s["d_full"], 1)
                for b in range(IMG_B):
                    for j in range(4):
                        hh = 4 * b + j
                        ins = pe.matmul(bank[b][0:MICRO, j * MICRO:(j + 1) * MICRO], K[:, m, hh, :], K[:, m, hh, :],
                                        start=True, stop=True)
                    ins.then_inc(s["kk_full"], 1)
                pe.wait_ge(s["d_exp"], OPEN + gi * 2 * PER + 2 * m + 2)
                for hh in range(H):
                    ins = pe.matmul(bank[6][0:MICRO, hh * T:(hh + 1) * T], K[:, m, hh, :],
                                    Q[:, hh, m * T:(m + 1) * T], start=True, stop=True)
                ins.then_inc(s["kq_full"], 1)
                for b in range(IMG_B):
                    if b:
                        pe.wait_ge(s["c_ready"], OPEN + gi * IB + 2 * m + 1)
                    for j in range(4):
                        ins = pe.transpose(bank[7][0:MICRO, j * HD:(j + 1) * HD], V[:, m, 4 * b + j, :], ident[:, :])
                    ins.then_inc(s["vt_full"], 1)
                for b in range(IMG_B):
                    n = m * IMG_B + b
                    pe.wait_ge(s["n_ready"], OPEN + gi * IB + n + 1)
                    for j in range(4):
                        ins = pe.transpose(bank[b][0:MICRO, j * MICRO:(j + 1) * MICRO], N[:, b, j, :],
                                           ident[0:MICRO, 0:MICRO])
                    ins.then_inc(s["z_full"], 1)
                for l in range(1, len(LEVELS)):
                    last = l == len(LEVELS) - 1
                    for b in range(IMG_B):
                        n = (gi * PER + m) * IMG_B * (len(LEVELS) - 2)
                        nz = (gi * PER + m) * IMG_B * len(LEVELS)
                        if l == 1:
                            pe.wait_ge(s["z_ready"], OPEN + nz + b + 1)
                        else:
                            pe.wait_ge(s["y_ready"], OPEN + n + (l - 2) * IMG_B + b + 1)
                        for j in range(4):
                            rhs = (Z if l == 1 else Y)[:, b, j, :]
                            ins = pe.matmul(bank[b][0:MICRO, j * MICRO:(j + 1) * MICRO], N[:, b, j, :], rhs,
                                            start=True, stop=True)
                        ins.then_inc(s["z_full"], 1)
                        if last:
                            pe.wait_ge(s["c_ready"], OPEN + gi * IB + 2 * m + b + 1)
                            for j in range(4):
                                ins = pe.matmul(bank[2 + 2 * b][0:MICRO, j * HD:(j + 1) * HD], Y[:, b, j, :],
                                                C[:, b, j, :], start=True, stop=True)
                            ins.then_inc(s["e_full"], 1)
                    for b in range(IMG_B):
                        nz = (gi * PER + m) * IMG_B * len(LEVELS)
                        if last:
                            pe.wait_ge(s["z_ready"], OPEN + nz + l * IMG_B + b + 1)
                            pe.wait_ge(s["e_ready"], OPEN + (gi * PER + m) * IMG_B + b + 1)
                            for j in range(4):
                                ins = pe.matmul(bank[3 + 2 * b][0:MICRO, j * HD:(j + 1) * HD], Z[:, b, j, :],
                                                EE[:, b, j, :], start=True, stop=True)
                            ins.then_inc(s["w_full"], 1)
                            continue
                        pe.wait_ge(s["z_ready"], OPEN + nz + l * IMG_B + b + 1)
                        if l == 1:
                            pe.wait_ge(s["x_pair"], OPEN + gi * IB + m * IMG_B + b + 1)
                            if m:
                                pe.wait_ge(s["wv_ready"], OPEN + (gi * PER + m) * IMG_B)
                        else:
                            pe.wait_ge(s["x_ready"], OPEN + (gi * PER + m) * IMG_B * (len(LEVELS) - 3) + (l - 2) * IMG_B + b + 1)
                        for j in range(4):
                            ins = pe.matmul(bank[3 + 2 * b][0:MICRO, j * MICRO:(j + 1) * MICRO], X[:, b, j, :],
                                            Z[:, b, j, :], start=True, stop=True)
                        ins.then_inc(s["y_full"], 1)
                        if l == len(LEVELS) - 2:
                            continue
                        for j in range(4):
                            ins = pe.matmul(bank[2 + 2 * b][0:MICRO, j * MICRO:(j + 1) * MICRO], Z[:, b, j, :],
                                            X[:, b, j, :], start=True, stop=True)
                        ins.then_inc(s["x_full"], 1)
            pe.wait_ge(s["wv_ready"], OPEN + (gi + 1) * IB)
            pe.wait_ge(s["pt_ready"], OPEN + (gi + 1) * PER)
            for b in range(2):
                for j in range(4):
                    for m in range(PER):
                        ins = pe.matmul(bank[b][0:ROWS, j * HD:(j + 1) * HD], PT[:, m, 4 * b + j, :],
                                        W[:, m, 4 * b + j, :], start=m == 0, stop=m == PER - 1)
                ins.then_inc(s["o_full"], 1)
            for b in range(2):
                pe.wait_ge(s["o_read"], OPEN + gi * 2 + b + 1)
                for j in range(4):
                    ins = pe.transpose(bank[2 + b][:, j * ROWS:(j + 1) * ROWS],
                                       O[:, (4 * b + j) * HD:(4 * b + j + 1) * HD], ident[0:ROWS, 0:ROWS])
                ins.then_inc(s["ot_full"], 1)
            pe.wait_ge(s["ot_ready"], OPEN + gi * 2 + 2)
            pe.wait_ge(s["w_out"], OPEN + 16)
            for hh in range(H):
                ins = pe.matmul(bank[6][0:ROWS, 0:D], OT[:, hh, :], wout[:, hh, :], start=hh == 0, stop=hh == H - 1)
            ins.then_inc(s["wo_full"], 1)
            pe.wait_ge(s["dve_chain"], OPEN + gi * DVE_LINKS + LINK_XN2)
            for c in range(DC):
                ins = pe.transpose(bank[7][:, c * ROWS:(c + 1) * ROWS], xn[:, c * 128:(c + 1) * 128],
                                   ident[0:ROWS, 0:ROWS])
            ins.then_inc(s["x2t_full"], 1)
            pe.wait_ge(s["x2t_ready"], OPEN + gi + 1)
            for c in range(DC):
                ins = pe.matmul(bank[6][0:ROWS, 256:256 + E], xnT[:, c, :], wrt[:, c, :], start=c == 0, stop=c == DC - 1)
            ins.then_inc(s["lg_full"], 1)

    @block.scalar
    def _(act):
        act.wait_ge(s["w_const"], OPEN + CONST)
        act.activation(negA[:, :], alog[:, :], ACT.Exp).then_inc(s["setup"], 1)
        with act.Fori(0, GROUPS) as gi:
            act.wait_ge(s["xt_full"], OPEN + gi + 1)
            act.activation(xnT[:, :, :], bank[7][:, 0:DC * ROWS], ACT.Copy).then_inc(s["xt_ready"], 1)
            act.wait_ge(s["spl"], OPEN + gi + 1)
            act.activation(sp[:, 1], sp[:, 1], ACT.Sigmoid).then_inc(s["act_chain"], 1)
            for k in range(CQ):
                act.wait_ge(s["conv_full"], OPEN + gi * CQ + k + 1)
                if k >= 2:
                    act.wait_ge(s["prod_done"], OPEN + gi * CQ + k - 1)
                else:
                    act.wait_ge(s["prod_done"], OPEN + gi * CQ)
                for j in range(4):
                    ins = act.activation(y[:, k % 2, j, :], bank[k % 6][:, j * ROWS:(j + 1) * ROWS], ACT.Copy,
                                         scale=taps[:, 4 * k + j, TAPS - 1:TAPS])
                ins.then_inc(s["conv_init"], 1)
                if k >= 1:
                    act.wait_ge(s["taps_done"], OPEN + gi * CQ + k)
                    act.activation(sg[:, (k - 1) % 2], y[:, (k - 1) % 2], ACT.Sigmoid).then_inc(s["sig_done"], 1)
            act.wait_ge(s["taps_done"], OPEN + gi * CQ + CQ)
            act.activation(sg[:, (CQ - 1) % 2], y[:, (CQ - 1) % 2], ACT.Sigmoid).then_inc(s["sig_done"], 1)
            for n in range(2):
                act.wait_ge(s["gate_full"], OPEN + gi * 2 + n + 1)
                if n:
                    act.wait_ge(s["gate_mul"], OPEN + gi * 2 + n)
                act.activation(gsig[:, :], bank[6 + n][0:ROWS, :], ACT.Sigmoid).then_inc(s["gate_sig"], 1)
            act.wait_ge(s["be_full"], OPEN + gi + 1)
            act.activation(beta[:, :], bank[7][0:MICRO, 0:PER * H], ACT.Sigmoid).then_inc(s["be_sig"], 1)
            act.wait_ge(s["act_chain"], OPEN + gi + 1)
            act.activation(sp[:, 2], sp[:, 1], ACT.Ln).then_inc(s["spl_ln"], 1)
            for m in range(PER):
                if m >= 2:
                    act.wait_ge(s["pt_ready"], OPEN + gi * PER + m - 1)
                for n, dst in enumerate((dj, di)):
                    act.wait_ge(s["d_full"], OPEN + gi * 2 * PER + 2 * m + n + 1)
                    if m >= 2 and n == 0:
                        act.wait_ge(s["dmask_ready"], OPEN + gi * IB + 1)
                    act.activation(dst[:, m % 2], bank[6 + n][0:MICRO, 0:H * T], ACT.Exp).then_inc(s["d_exp"], 1)
                nl = (gi * PER + m) * IMG_B * (len(LEVELS) - 3)
                for l in range(1, len(LEVELS) - 2):
                    for b in range(IMG_B):
                        act.wait_ge(s["x_full"], OPEN + nl + (l - 1) * IMG_B + b + 1)
                        act.activation(X[:, b], bank[2 + 2 * b][0:MICRO, 0:4 * MICRO], ACT.Copy)\
                            .then_inc(s["x_ready"], 1)
                for b in range(IMG_B):
                    act.wait_ge(s["e_full"], OPEN + (gi * PER + m) * IMG_B + b + 1)
                    act.activation(EE[:, b], bank[2 + 2 * b][0:MICRO, 0:512], ACT.Copy).then_inc(s["e_ready"], 1)
                for b in range(IMG_B):
                    act.wait_ge(s["w_full"], OPEN + (gi * PER + m) * IMG_B + b + 1)
                    act.activation(W[:, m, 4 * b:4 * b + 4, :], bank[3 + 2 * b][0:MICRO, 0:512], ACT.Copy)\
                        .then_inc(s["wv_ready"], 1)
            for b in range(2):
                act.wait_ge(s["o_full"], OPEN + gi * 2 + b + 1)
                act.activation(osq[:, b * 512:(b + 1) * 512], bank[b][0:ROWS, :], ACT.Square).then_inc(s["o_sq"], 1)
            for b in range(2):
                act.wait_ge(s["ot_full"], OPEN + gi * 2 + b + 1)
                act.activation(OT[:, 4 * b:4 * b + 4, :], bank[2 + b][:, 0:4 * ROWS], ACT.Copy)\
                    .then_inc(s["ot_ready"], 1)
            act.wait_ge(s["x2t_full"], OPEN + gi + 1)
            act.activation(xnT[:, :, :], bank[7][:, 0:DC * ROWS], ACT.Copy).then_inc(s["x2t_ready"], 1)

    @block.vector
    def _(dve):
        dve.wait_ge(s["w_tok"], OPEN + 48)
        dve.tensor_tensor(addend[:, :], addend[:, :], pos3[:, :], ALU.add).then_inc(s["setup2"], 1)
        dve.wait_ge(s["setup"], OPEN + 1)
        dve.tensor_scalar(negA[:, :], negA[:, :], -1.0, None, ALU.mult).then_inc(s["setup2"], 1)
        dve.wait_ge(s["setup2"], OPEN + 2)
        dve.wait_ge(s["w_const"], OPEN + CONST)
        dve.wait_ge(s["consts"], OPEN + 4)
        with dve.Fori(0, GROUPS) as gi:
            ch = Chain(dve, s["dve_chain"], DVE_LINKS, gi)
            h = hcur[:, :]
            dve.wait_ge(s["tok_full"], OPEN + gi + 1)
            ch.link(dve.tensor_tensor(h, bank[6][0:ROWS, 0:D], addend[:, :], ALU.add))
            ch.wait()
            layer_norm(dve, ch, st[:, :], mv[:, :], ve[:, :], rstd[:, :], xn[:, :], h,
                       s["var_ready"], s["rstd_ready"], gi, 1, 2)
            assert ch.n == LINK_XN, ch.n
            dve.wait_ge(s["ab_full"], OPEN + gi + 1)
            dve.tensor_copy(blog[:, :], bank[6][0:ROWS, 256:256 + NH * H]).then_inc(s["ab_read"], 1)
            dve.tensor_tensor(sp[:, 0], bank[6][0:ROWS, 280:288], dtb[:, :], ALU.add).then_inc(s["ab_read"], 1)
            dve.wait_ge(s["ab_read"], OPEN + gi * 2 + 2)
            dve.scalar_tensor_tensor(sp[:, 1], sp[:, 0], -1.0, sp[:, 0], ALU.mult, ALU.max).then_inc(s["spl"], 1)
            for k in range(CQ):
                dve.wait_ge(s["conv_init"], OPEN + gi * CQ + k + 1)
                for tap in range(TAPS - 2, -1, -1):
                    sh = TAPS - 1 - tap
                    if sh > 1:
                        ch.wait()
                    for j in range(4):
                        yv = y[:, k % 2, j, :].rearrange("p (m t) -> p m t", t=T)[:, :, sh:T]
                        pv = bank[k % 6][:, j * ROWS:(j + 1) * ROWS].rearrange("p (m t) -> p m t", t=T)[:, :, 0:T - sh]
                        ins = dve.scalar_tensor_tensor(yv, pv, taps[:, 4 * k + j, tap:tap + 1], yv,
                                                       ALU.mult, ALU.add)
                        if j == 3:
                            if tap == 0:
                                ins.then_inc(s["taps_done"], 1)
                            else:
                                ch.link(ins)
            for n in range(2):
                dve.wait_ge(s["gate_sig"], OPEN + gi * 2 + n + 1)
                dve.tensor_tensor(gs[:, n * 512:(n + 1) * 512], bank[6 + n][0:ROWS, :], gsig[:, :],
                                  ALU.mult).then_inc(s["gate_mul"], 1)
            dve.wait_ge(s["gate_mul"], OPEN + gi * 2 + 2)
            gsv = gs[:, :].rearrange("p (h d) -> p h d", h=H)
            ch.link(dve.tensor_tensor(gsv, gsv, bc(rmsw[:, :], 1, H), ALU.mult))
            dve.wait_ge(s["ks_full"], OPEN + gi * 4 + 4)
            dve.tensor_scalar(r2[:, :], bank[6][0:MICRO, 0:4 * H], 1e-6, None, ALU.add).then_inc(s["ks_read"], 1)
            dve.wait_ge(s["ks_read"], OPEN + gi + 1)
            dve.reciprocal(r2[:, :], r2[:, :]).then_inc(s["r2_ready"], 1)
            dve.wait_ge(s["r2_ready"], OPEN + gi + 1)
            dve.wait_ge(s["be_sig"], OPEN + gi + 1)
            ch.link(dve.scalar_tensor_tensor(nbr2[:, :], beta[:, :], -2.0, r2[:, H:], ALU.mult, ALU.mult))
            dve.wait_ge(s["rr_ready"], OPEN + gi + 1)
            dve.scalar_tensor_tensor(br[:, :], beta[:, :], 2.0, rr[:, :], ALU.mult, ALU.mult)\
                .then_inc(s["br_ready"], 1)
            dve.wait_ge(s["spl_ln"], OPEN + gi + 1)
            ch.link(dve.scalar_tensor_tensor(sp[:, 3], sp[:, 0], 0.0, sp[:, 2], ALU.max, ALU.subtract))
            ch.wait()
            dve.tensor_tensor(g[:, :], sp[:, 3], negA[:, :], ALU.mult).then_inc(s["g_ready"], 1)
            for m in range(PER):
                for b in range(IMG_B):
                    n = m * IMG_B + b
                    dve.wait_ge(s["kk_full"], OPEN + gi * IB + n + 1)
                    dve.wait_ge(s["dmask_ready"], OPEN + gi * IB + n + 1)
                    dve.tensor_tensor(N[:, b], bank[b][0:MICRO, 0:4 * MICRO].rearrange("p (h c) -> p h c", h=4),
                                      dmask[:, :, :], ALU.mult).then_inc(s["noff_ready"], 1)
                dve.wait_ge(s["kq_full"], OPEN + gi * PER + m + 1)
                dve.wait_ge(s["di_ready"], OPEN + gi * PER + m + 1)
                dve.tensor_tensor(PT[:, m, :, m * T:(m + 1) * T],
                                  bank[6][0:MICRO, 0:H * T].rearrange("p (h t) -> p h t", h=H), di[:, m % 2],
                                  ALU.mult).then_inc(s["pt_ready"], 1)
                for b in range(IMG_B):
                    dve.wait_ge(s["vt_full"], OPEN + gi * IB + m * IMG_B + b + 1)
                    dve.tensor_tensor(C[:, b], bank[7][0:MICRO, :].rearrange("p (h d) -> p h d", h=4),
                                      bc(br[:, m * H + 4 * b:m * H + 4 * b + 4], 2, HD), ALU.mult)\
                        .then_inc(s["c_ready"], 1)
                nz = (gi * PER + m) * IMG_B * len(LEVELS)
                nl = (gi * PER + m) * IMG_B * (len(LEVELS) - 2)
                for l in range(len(LEVELS)):
                    for b in range(IMG_B):
                        dve.wait_ge(s["z_full"], OPEN + nz + l * IMG_B + b + 1)
                        dve.tensor_tensor(Z[:, b], bank[b][0:MICRO, 0:4 * MICRO].rearrange("p (h c) -> p h c", h=4),
                                          bc(m_lvl[:, l, :], 1, 4), ALU.mult).then_inc(s["z_ready"], 1)
                    if 1 <= l < len(LEVELS) - 1:
                        for b in range(IMG_B):
                            dve.wait_ge(s["y_full"], OPEN + nl + (l - 1) * IMG_B + b + 1)
                            dve.tensor_copy(Y[:, b], bank[3 + 2 * b][0:MICRO, 0:4 * MICRO]).then_inc(s["y_ready"], 1)
            dve.wait_ge(s["o_sq"], OPEN + gi * 2 + 2)
            ch.link(dve.tensor_reduce(rms[:, 0], osq.rearrange("p (h d) -> p h d", h=H), AX.X, ALU.add))
            ch.wait()
            ch.link(dve.scalar_tensor_tensor(rms[:, 1], rms[:, 0], 1.0 / (HD * HD), r2[0:ROWS, 0:H],
                                             ALU.mult, ALU.mult))
            ch.wait()
            ch.link(dve.tensor_scalar(rms[:, 0], rms[:, 1], 1e-5, None, ALU.add))
            ch.wait()
            ch.link(dve.reciprocal(rms[:, 1], rms[:, 0]))
            ch.wait()
            dve.scalar_tensor_tensor(rms[:, 2], r2[0:ROWS, 0:H], 1.0 / HD, rms[:, 1], ALU.mult, ALU.mult)\
                .then_inc(s["o_mean"], 1)
            for b in range(2):
                Ov = O[:, b * 512:(b + 1) * 512].rearrange("p (h d) -> p h d", h=4)
                dve.wait_ge(s["o_sq"], OPEN + gi * 2 + b + 1)
                ch.link(dve.tensor_tensor(Ov, bank[b][0:ROWS, :].rearrange("p (h d) -> p h d", h=4),
                                          gsv[:, 4 * b:4 * b + 4, :], ALU.mult))
            dve.wait_ge(s["o_pow"], OPEN + gi + 1)
            ch.wait()
            for b in range(2):
                Ov = O[:, b * 512:(b + 1) * 512].rearrange("p (h d) -> p h d", h=4)
                dve.tensor_tensor(Ov, Ov, bc(rms[:, 3, 4 * b:4 * b + 4], 2, HD), ALU.mult).then_inc(s["o_read"], 1)
            dve.wait_ge(s["wo_full"], OPEN + gi + 1)
            ch.link(dve.tensor_tensor(h, bank[6][0:ROWS, 0:D], h, ALU.add))
            ch.wait()
            dve.wait_ge(s["h_stored"], OPEN + gi * 32)
            dve.tensor_copy(hout[:, :], h).then_inc(s["h_ready"], 1)
            layer_norm(dve, ch, st[:, :], mv[:, :], ve[:, :], rstd[:, :], xn[:, :], h,
                       s["var_ready"], s["rstd_ready"], gi, 2, 2)
            assert ch.n == LINK_XN2, ch.n
            dve.wait_ge(s["x2t_ready"], OPEN + gi + 1)
            dve.tensor_copy(xTout[:, :, :], xnT[:, :, :]).then_inc(s["xT_kept"], 1)
            dve.wait_ge(s["lg_full"], OPEN + gi + 1)
            ch.link(dve.tensor_tensor(lg[:, :], bank[6][0:ROWS, 256:256 + E], rbias[:, :], ALU.add))
            choose(dve, ch, lg[:, :], mx, countdown[:, :],
                   route[:, bass.ds(gi, 1), :].rearrange("p a e -> p (a e)"), s["route_ready"])
            assert ch.n == DVE_LINKS, ch.n


def choose(dve, ch, lg, mx, countdown, out, ready):
    ch.wait()
    ch.link(dve.tensor_reduce(mx[:, 0:1], lg, AX.X, ALU.max))
    ch.wait()
    ch.link(dve.scalar_tensor_tensor(lg, lg, mx[:, 0:1], countdown, ALU.is_equal, ALU.mult))
    ch.wait()
    ch.link(dve.tensor_reduce(mx[:, 1:2], lg, AX.X, ALU.max))
    ch.wait()
    dve.tensor_scalar(out, lg, mx[:, 1:2], None, ALU.is_equal).then_inc(ready, 1)


def block_of(k):
    if k < 2:
        return "q", 0, 4 * k
    k -= 2
    kind = "k" if k < 6 else "v"
    k %= 6
    return kind, k // 2, 4 * (k % 2)


def host_layouts(i):
    f = np.float32
    x = np.asarray(i["x"])
    p = x.reshape(IMAGES, CHANNELS, GRID, PATCH, GRID, PATCH).transpose(0, 2, 4, 1, 3, 5).reshape(IMAGES, PATCHES, F)
    tok = np.zeros((IMAGES, T, F), f)
    tok[:, 1:] = p
    first = [min(PER * g, FIRST_OF_LAST) for g in range(GROUPS + 1)]
    xg = np.stack([tok[b:b + PER] for b in first]).reshape(-1, ROWS, FC, 128).transpose(0, 3, 2, 1)

    def rows(w):
        w = np.asarray(w)
        return np.ascontiguousarray(w.reshape(-1, 128, w.shape[1]).transpose(1, 0, 2))

    blin = np.asarray(i["L0_tok_b_lin"])
    one = np.concatenate([np.asarray(i["L0_tok_class_token"])[0], np.broadcast_to(blin, (PATCHES, D))])
    taps = np.concatenate([np.asarray(i[f"L0_attn_conv_{c}"]) for c in "qkv"])
    r, c = np.arange(MICRO)[:, None], np.arange(MICRO)[None]
    lvl = [((r // (2 * s)) == (c // (2 * s))) & ((r // s) % 2 == 1) & ((c // s) % 2 == 0) | (r == c) for s in LEVELS]
    tl = (np.arange(ROWS) % T)[:, None]
    im = (np.arange(ROWS) // T)[:, None]
    step_t = (np.arange(MICRO) // NH)[None]
    return dict(
        x=xg, wlin=rows(np.asarray(i["L0_tok_W_lin"]).T), pos3=np.tile(np.asarray(i["L0_tok_position_embeddings"])[0], (PER, 1)),
        rowadd=np.tile(one, (PER, 1)),
        wqkv=rows(np.concatenate([np.asarray(i[f"L0_attn_W{c}"]) for c in "qkv"], 1)),
        wgate=rows(i["L0_attn_Wg"]), wout=rows(i["L0_attn_Wo"]),
        wab=rows(np.concatenate([np.asarray(i["L0_attn_Wb"]), np.asarray(i["L0_attn_Wa"])], 1)),
        wrt=rows(i["L0_ffn_router_w"]), taps=taps.reshape(CB, 128, TAPS).transpose(1, 0, 2),
        dtb=np.asarray(i["L0_attn_dt_bias"]), alog=np.asarray(i["L0_attn_A_log"]),
        rmsw=np.asarray(i["L0_attn_rms_weight"]), rbias=np.asarray(i["L0_ffn_router_b"]),
        ident=np.eye(128, dtype=f), m_low=(r > c).astype(f), m_pair=lvl[0].astype(f),
        m_lvl=np.stack([m.T for m in lvl], 1).astype(f),
        s_gt=(tl > np.arange(T)[None]).astype(f), s_le=(tl <= np.arange(T)[None]).astype(f),
        up_to=np.stack([(im == m) & (tl <= step_t) for m in range(PER)], 1).astype(f),
        after=np.stack([(im == m) & (tl > step_t) for m in range(PER)], 1).astype(f),
        causal=(step_t.T <= np.arange(T)[None]).astype(f),
        spread=np.stack([(im == m) & (c == NH * tl + j) for m in range(PER) for j in range(NH)], 1).astype(f),
        countdown=np.tile(np.arange(E, 0, -1).astype(f), (ROWS, 1)),
    )


def attention_phase(nc, ctx, a, h_all, xT_all, route):
    def sb(name, shape, dt=F32):
        return ctx.enter_context(nc.sbuf_tensor("a_" + name, shape, dt))

    bank = [ctx.enter_context(nc.psum_tensor(f"a_bank{i}", [128, 512], F32)) for i in range(8)]
    AC = AH // 4
    wq = sb("wq", [128, DC, AC * 128])
    wk = sb("wk", [128, DC, AC * 128])
    wv = sb("wv", [128, DC, D])
    wo = sb("wo", [128, DC, D])
    wg = sb("wg", [128, DC, E])
    bq = sb("bq", [128, AC])
    bk = sb("bk", [128, AC])
    bv = sb("bv", [ROWS, D])
    bo = sb("bo", [ROWS, D])
    bg = sb("bg", [ROWS, E])
    ident = sb("ident", [128, 128])
    mask = sb("mask", [ROWS, ROWS])
    countdown = sb("countdown", [ROWS, E])
    nhalf = sb("nhalf", [ROWS, 1])
    st = sb("st", [ROWS, 6])
    mv = sb("mv", [ROWS, 2])
    ve = sb("ve", [ROWS, 1])
    rstd = sb("rstd", [ROWS, 1])
    hcur = sb("hcur", [ROWS, D])
    hb = sb("hb", [ROWS, D])
    xn = sb("xn", [ROWS, D])
    xnT = sb("xnT", [128, DC, ROWS])
    qT = sb("qT", [128, AC, ROWS])
    kT = sb("kT", [128, AC, ROWS])
    v = sb("v", [ROWS, D])
    S = sb("S", [ROWS, AC, 4, ROWS])
    mx = sb("mx", [ROWS, AH])
    sums = sb("sums", [ROWS, AH])
    rinv = sb("rinv", [ROWS, AH])
    PT = sb("PT", [ROWS, AC, 4, ROWS])
    yv = sb("yv", [ROWS, D])
    yT = sb("yT", [128, DC, ROWS])
    lg = sb("lg", [ROWS, E])
    lm = sb("lm", [ROWS, E])
    ex = sb("ex", [ROWS, E])
    gx = sb("gx", [ROWS, 4])
    hot = sb("hot", [ROWS, E])

    s = {n: ctx.enter_context(nc.semaphore("a_" + n)) for n in """weights consts scaled
        dve_chain var_ready rstd_ready xt_full xt_ready q_full k_full v_full q_ready k_ready v_ready
        hb_ready s_full masked max_ready shifted exp_done pt_full pt_ready y_full y_ready yt_full yt_ready
        wo_full x2t_full x2t_ready lg_full lg_shift lg_exp hot_ready route_ready""".split()}
    block = ctx.enter_context(nc.Block())
    LOADS = 12

    @block.sync
    def _(sp):
        open_counts(sp, s.values())
        for t, n in ((ident, "ident"), (wq, "awq"), (wk, "awk"), (wv, "awv"), (wo, "awo"), (wg, "awg"), (bq, "abq"),
                     (bk, "abk"), (mask, "amask"), (countdown, "countdown")):
            sp.dma_start(t[tuple(slice(None) for _ in t.shape)], a[n]).then_inc(s["weights"], 16)
        sp.dma_start(bv[:, :], a["abv"].partition_broadcast(ROWS)).then_inc(s["weights"], 16)
        sp.dma_start(bo[:, :], a["abo"].partition_broadcast(ROWS)).then_inc(s["weights"], 16)
        sp.dma_start(bg[:, :], a["abg"].partition_broadcast(ROWS)).then_inc(s["weights"], 16)
    LOADED = 16 * 13

    @block.gpsimd
    def _(pool):
        pool.memset(nhalf[:, :], -0.5).then_inc(s["consts"], 1)
        pool.wait_ge(s["weights"], OPEN + LOADED)
        pool.wait_ge(s["consts"], OPEN + 1)
        with pool.Fori(0, GROUPS) as gi:
            pool.wait_ge(s["var_ready"], OPEN + gi * 2 + 1)
            pool.tensor_tensor(rstd[:, :], ve[:, :], nhalf[:, :], ALU.pow).then_inc(s["rstd_ready"], 1)
            pool.tensor_tensor(hb[:, :], hcur[:, :], bo[:, :], ALU.add).then_inc(s["hb_ready"], 1)
            for c in range(AC):
                pool.wait_ge(s["max_ready"], OPEN + gi * AC + c + 1)
                pool.tensor_tensor(S[:, c], S[:, c], bc(mx[:, 4 * c:4 * c + 4], 2, ROWS), ALU.subtract)\
                    .then_inc(s["shifted"], 1)
            pool.wait_ge(s["var_ready"], OPEN + gi * 2 + 2)
            pool.tensor_tensor(rstd[:, :], ve[:, :], nhalf[:, :], ALU.pow).then_inc(s["rstd_ready"], 1)

    @block.tensor
    def _(pe):
        pe.wait_ge(s["weights"], OPEN + LOADED)
        pe.wait_ge(s["scaled"], OPEN + 1)
        with pe.Fori(0, GROUPS) as gi:
            pe.wait_ge(s["dve_chain"], OPEN + gi * A_LINKS + A_XN)
            for c in range(DC):
                ins = pe.transpose(bank[0][:, c * ROWS:(c + 1) * ROWS], xn[:, c * 128:(c + 1) * 128],
                                   ident[0:ROWS, 0:ROWS])
            ins.then_inc(s["xt_full"], 1)
            pe.wait_ge(s["xt_ready"], OPEN + gi + 1)
            for w, b, full in ((wq, 1, "q_full"), (wk, 2, "k_full")):
                for j in range(AC):
                    for c in range(DC):
                        ins = pe.matmul(bank[b][:, j * ROWS:(j + 1) * ROWS], w[:, c, j * 128:(j + 1) * 128],
                                        xnT[:, c, :], start=c == 0, stop=c == DC - 1)
                ins.then_inc(s[full], 1)
            for c in range(DC):
                ins = pe.matmul(bank[3][0:ROWS, 0:D], xnT[:, c, :], wv[:, c, :], start=c == 0, stop=c == DC - 1)
            ins.then_inc(s["v_full"], 1)
            pe.wait_ge(s["q_ready"], OPEN + gi + 1)
            pe.wait_ge(s["k_ready"], OPEN + gi + 1)
            for c in range(AC):
                for j in range(4):
                    ins = pe.matmul(bank[4 + j][0:ROWS, c * ROWS:(c + 1) * ROWS], qT[32 * j:32 * j + 32, c, :],
                                    kT[32 * j:32 * j + 32, c, :], start=True, stop=True)
                    if c == AC - 1:
                        ins.then_inc(s["s_full"], 1)
            for c in range(AC):
                pe.wait_ge(s["exp_done"], OPEN + gi * AC + c + 1)
                for j in range(4):
                    ins = pe.transpose(bank[4 + c][0:ROWS, j * ROWS:(j + 1) * ROWS], S[:, c, j, :],
                                       ident[0:ROWS, 0:ROWS])
                ins.then_inc(s["pt_full"], 1)
            pe.wait_ge(s["v_ready"], OPEN + gi + 1)
            for c in range(AC):
                pe.wait_ge(s["pt_ready"], OPEN + gi * AC + c + 1)
                for j in range(4):
                    hh = 4 * j + c
                    ins = pe.matmul(bank[1][0:ROWS, hh * AD:(hh + 1) * AD], PT[:, c, j, :], v[:, hh * AD:(hh + 1) * AD],
                                    start=True, stop=True)
            ins.then_inc(s["y_full"], 1)
            pe.wait_ge(s["y_ready"], OPEN + gi + 1)
            for c in range(DC):
                ins = pe.transpose(bank[2][:, c * ROWS:(c + 1) * ROWS], yv[:, c * 128:(c + 1) * 128],
                                   ident[0:ROWS, 0:ROWS])
            ins.then_inc(s["yt_full"], 1)
            pe.wait_ge(s["yt_ready"], OPEN + gi + 1)
            for c in range(DC):
                ins = pe.matmul(bank[3][0:ROWS, 0:D], yT[:, c, :], wo[:, c, :], start=c == 0, stop=c == DC - 1)
            ins.then_inc(s["wo_full"], 1)
            pe.wait_ge(s["dve_chain"], OPEN + gi * A_LINKS + A_XN2)
            for c in range(DC):
                ins = pe.transpose(bank[0][:, c * ROWS:(c + 1) * ROWS], xn[:, c * 128:(c + 1) * 128],
                                   ident[0:ROWS, 0:ROWS])
            ins.then_inc(s["x2t_full"], 1)
            pe.wait_ge(s["x2t_ready"], OPEN + gi + 1)
            for c in range(DC):
                ins = pe.matmul(bank[1][0:ROWS, 256:256 + E], xnT[:, c, :], wg[:, c, :], start=c == 0, stop=c == DC - 1)
            ins.then_inc(s["lg_full"], 1)
            pe.wait_ge(s["lg_shift"], OPEN + gi + 1)

    @block.scalar
    def _(act):
        act.wait_ge(s["weights"], OPEN + LOADED)
        with act.Fori(0, GROUPS) as gi:
            act.wait_ge(s["xt_full"], OPEN + gi + 1)
            act.activation(xnT[:, :, :], bank[0][:, 0:DC * ROWS], ACT.Copy).then_inc(s["xt_ready"], 1)
            act.wait_ge(s["k_full"], OPEN + gi + 1)
            for j in range(AC):
                ins = act.activation(kT[:, j, :], bank[2][:, j * ROWS:(j + 1) * ROWS], ACT.Identity,
                                     bias=bk[:, j:j + 1])
            ins.then_inc(s["k_ready"], 1)
            for c in range(AC):
                act.wait_ge(s["shifted"], OPEN + gi * AC + c + 1)
                act.activation(S[:, c], S[:, c], ACT.Exp).then_inc(s["exp_done"], 1)
            for c in range(AC):
                act.wait_ge(s["pt_full"], OPEN + gi * AC + c + 1)
                act.activation(PT[:, c], bank[4 + c][0:ROWS, 0:4 * ROWS], ACT.Copy).then_inc(s["pt_ready"], 1)
            act.wait_ge(s["yt_full"], OPEN + gi + 1)
            act.activation(yT[:, :, :], bank[2][:, 0:DC * ROWS], ACT.Copy).then_inc(s["yt_ready"], 1)
            act.wait_ge(s["x2t_full"], OPEN + gi + 1)
            act.activation(xnT[:, :, :], bank[0][:, 0:DC * ROWS], ACT.Copy).then_inc(s["x2t_ready"], 1)
            act.wait_ge(s["lg_shift"], OPEN + gi + 1)
            act.activation(ex[:, :], lm[:, :], ACT.Exp).then_inc(s["lg_exp"], 1)

    @block.vector
    def _(dve):
        dve.wait_ge(s["weights"], OPEN + LOADED)
        dve.tensor_scalar(bq[:, :], bq[:, :], AD ** -0.5, None, ALU.mult).then_inc(s["scaled"], 1)
        dve.wait_ge(s["scaled"], OPEN + 1)
        with dve.Fori(0, GROUPS) as gi:
            ch = Chain(dve, s["dve_chain"], A_LINKS, gi)
            row = h_all[:, bass.ds(gi, 1), :].rearrange("p a d -> p (a d)")
            dve.wait_ge(s["hb_ready"], OPEN + gi)
            ch.link(dve.tensor_scalar(hcur[:, :], row, 1.0, None, ALU.mult))
            ch.wait()
            layer_norm(dve, ch, st[:, :], mv[:, :], ve[:, :], rstd[:, :], xn[:, :], hcur[:, :],
                       s["var_ready"], s["rstd_ready"], gi, 1, 2)
            assert ch.n == A_XN, ch.n
            dve.wait_ge(s["q_full"], OPEN + gi + 1)
            for j in range(AC):
                ins = dve.tensor_scalar(qT[:, j, :], bank[1][:, j * ROWS:(j + 1) * ROWS], AD ** -0.5, bq[:, j:j + 1],
                                        ALU.mult, ALU.add)
            ins.then_inc(s["q_ready"], 1)
            dve.wait_ge(s["v_full"], OPEN + gi + 1)
            dve.tensor_tensor(v[:, :], bank[3][0:ROWS, 0:D], bv[:, :], ALU.add).then_inc(s["v_ready"], 1)
            for c in range(AC):
                dve.wait_ge(s["s_full"], OPEN + gi * AC + c + 1)
                dve.tensor_tensor(S[:, c], bank[4 + c][0:ROWS, 0:4 * ROWS].rearrange("p (h k) -> p h k", h=4),
                                  bc(mask[:, :], 1, 4), ALU.add).then_inc(s["masked"], 1)
                dve.wait_ge(s["masked"], OPEN + gi * AC + c + 1)
                dve.tensor_reduce(mx[:, 4 * c:4 * c + 4], S[:, c], AX.X, ALU.max).then_inc(s["max_ready"], 1)
            for c in range(AC):
                dve.wait_ge(s["exp_done"], OPEN + gi * AC + c + 1)
                ch.link(dve.tensor_reduce(sums[:, 4 * c:4 * c + 4], S[:, c], AX.X, ALU.add))
            ch.wait()
            ch.link(dve.reciprocal(rinv[:, :], sums[:, :]))
            ch.wait()
            dve.wait_ge(s["y_full"], OPEN + gi + 1)
            dve.tensor_tensor(yv[:, :].rearrange("p (c j d) -> p c j d", c=AC, j=4),
                              bank[1][0:ROWS, 0:D].rearrange("p (c j d) -> p c j d", c=AC, j=4),
                              bc(rinv[:, :].rearrange("p (j c) -> p c j", j=4), 3, AD), ALU.mult).then_inc(s["y_ready"], 1)
            dve.wait_ge(s["wo_full"], OPEN + gi + 1)
            dve.wait_ge(s["hb_ready"], OPEN + gi + 1)
            ch.link(dve.tensor_tensor(hcur[:, :], bank[3][0:ROWS, 0:D], hb[:, :], ALU.add))
            ch.wait()
            ch.link(dve.tensor_scalar(row, hcur[:, :], 1.0, None, ALU.mult))
            layer_norm(dve, ch, st[:, :], mv[:, :], ve[:, :], rstd[:, :], xn[:, :], hcur[:, :],
                       s["var_ready"], s["rstd_ready"], gi, 2, 2)
            assert ch.n == A_XN2, ch.n
            dve.wait_ge(s["x2t_ready"], OPEN + gi + 1)
            ch.link(dve.tensor_scalar(xT_all[:, :, bass.ds(gi * ROWS, ROWS)], xnT[:, :, :], 1.0, None, ALU.mult))
            dve.wait_ge(s["lg_full"], OPEN + gi + 1)
            ch.link(dve.tensor_tensor(lg[:, :], bank[1][0:ROWS, 256:256 + E], bg[:, :], ALU.add))
            ch.wait()
            ch.link(dve.tensor_reduce(gx[:, 2:3], lg[:, :], AX.X, ALU.max))
            ch.wait()
            dve.tensor_scalar(lm[:, :], lg[:, :], gx[:, 2:3], None, ALU.subtract).then_inc(s["lg_shift"], 1)
            choose(dve, ch, lg[:, :], gx, countdown[:, :], hot[:, :], s["hot_ready"])
            dve.wait_ge(s["lg_exp"], OPEN + gi + 1)
            ch.link(dve.tensor_reduce(gx[:, 2:3], ex[:, :], AX.X, ALU.add))
            ch.wait()
            ch.link(dve.reciprocal(gx[:, 3:4], gx[:, 2:3]))
            ch.wait()
            dve.wait_ge(s["hot_ready"], OPEN + gi + 1)
            dve.tensor_scalar(route[:, bass.ds(gi, 1), :].rearrange("p a e -> p (a e)"), hot[:, :], gx[:, 3:4], None,
                              ALU.mult).then_inc(s["route_ready"], 1)
            assert ch.n == A_LINKS, ch.n


def mixture_phase(nc, ctx, tag, w1_dram, b1_dram, w2_dram, b2_dram, gated, h_all, xT_all, route, out=None):
    def sb(name, shape, dt=F32):
        return ctx.enter_context(nc.sbuf_tensor(tag + name, shape, dt))

    bank = [ctx.enter_context(nc.psum_tensor(f"{tag}bank{i}", [128, 512], F32)) for i in range(8)]
    WIDE = 2 * HID if gated else HID
    FB = HID // 128
    TILE = 2 * ROWS
    TILES = GROUPS // 2
    w1 = sb("w1", [128, 2, DC, WIDE])
    w2 = sb("w2", [128, 2, FB, D])
    b1 = sb("b1", [128, 2, WIDE // 128])
    b2 = sb("b2", [1, 2, D])
    ones = sb("ones", [1, ROWS])
    sig = sb("sig", [128, 2, TILE])
    hid = sb("hid", [128, FB, TILE])
    rt = sb("rt", [ROWS, 2])
    s = {n: ctx.enter_context(nc.semaphore(tag + n)) for n in """weights0 weights1 consts up_full sig_done
        hid_ready y_full y_read rt_ready stored""".split()}
    block = ctx.enter_context(nc.Block())
    loaded = [s["weights0"], s["weights1"]]

    @block.sync
    def _(sp):
        open_counts(sp, s.values())
        def load(e, eb):
            e = bass.ds(e, 1)
            sp.dma_start(w1[:, eb], w1_dram[e].rearrange("a p c n -> p (a c) n")).then_inc(loaded[eb], 16)
            sp.dma_start(b1[:, eb], b1_dram[e].rearrange("a p n -> p (a n)")).then_inc(loaded[eb], 16)
            sp.dma_start(w2[:, eb], w2_dram[e].rearrange("a p c n -> p (a c) n")).then_inc(loaded[eb], 16)
            sp.dma_start(b2[:, eb], b2_dram[e]).then_inc(loaded[eb], 16)

        load(0, 0)
        load(1, 1)
        with sp.Fori(0, E // 2 - 1) as pair:
            for eb in range(2):
                sp.wait_ge(s["y_full"], OPEN + (2 * pair + eb + 1) * (2 * TILES))
                load(2 * pair + eb + 2, eb)
        if out is not None:
            sp.wait_ge(s["y_read"], OPEN + 2 * E * TILES)
            full = ROWS * (GROUPS - 1)
            sp.dma_start(out[0:full, :].rearrange("(g p) d -> p g d", p=ROWS), h_all[:, 0:GROUPS - 1, :])\
                .then_inc(s["stored"], 16)
            sp.dma_start(out[full:full + NEW_ROWS_OF_LAST, :], h_all[ROWS - NEW_ROWS_OF_LAST:ROWS, GROUPS - 1, :])\
                .then_inc(s["stored"], 16)
            sp.wait_ge(s["stored"], OPEN + 32)

    @block.gpsimd
    def _(pool):
        pool.memset(ones[:, :], 1.0).then_inc(s["consts"], 1)

    @block.tensor
    def _(pe):
        pe.wait_ge(s["consts"], OPEN + 1)
        with pe.Fori(0, E // 2) as pair:
            for eb in range(2):
                with pe.Fori(0, TILES) as ti:
                    pe.wait_ge(loaded[eb], OPEN + (pair + 1) * 64)
                    n = (2 * pair + eb) * TILES + ti
                    for f in range(FB):
                        pe.wait_ge(s["hid_ready"], OPEN + n * FB + max(f - 2, 0))
                        for up in range(2 if gated else 1):
                            for c in range(DC):
                                col = up * HID + f * 128
                                ins = pe.matmul(bank[(f % 3) * 2 + up][:, 0:TILE], w1[:, eb, c, col:col + 128],
                                                xT_all[:, c, bass.ds(ti * TILE, TILE)], start=c == 0, stop=c == DC - 1)
                        ins.then_inc(s["up_full"], 1)
                    pe.wait_ge(s["hid_ready"], OPEN + n * FB + FB)
                    pe.wait_ge(s["y_read"], OPEN + n * 2)
                    for half in range(2):
                        y = bank[6 + half][0:ROWS, 0:D]
                        for f in range(FB):
                            pe.matmul(y, hid[:, f, half * ROWS:(half + 1) * ROWS], w2[:, eb, f, :], start=f == 0,
                                      stop=False)
                        pe.matmul(y, ones[:, :], b2[:, eb, :], start=False, stop=True).then_inc(s["y_full"], 1)

    @block.scalar
    def _(act):
        with act.Fori(0, E // 2) as pair:
            for eb in range(2):
                with act.Fori(0, TILES) as ti:
                    act.wait_ge(loaded[eb], OPEN + (pair + 1) * 64)
                    n = (2 * pair + eb) * TILES + ti
                    if not gated:
                        act.wait_ge(s["y_full"], OPEN + n * 2)
                    for f in range(FB):
                        act.wait_ge(s["up_full"], OPEN + n * FB + f + 1)
                        if gated:
                            act.wait_ge(s["hid_ready"], OPEN + n * FB + max(f - 1, 0))
                            act.activation(sig[:, f % 2, :], bank[(f % 3) * 2 + 1][:, 0:TILE], ACT.Sigmoid,
                                           bias=b1[:, eb, FB + f:FB + f + 1]).then_inc(s["sig_done"], 1)
                        else:
                            act.activation(hid[:, f, :], bank[(f % 3) * 2][:, 0:TILE], ACT.Relu,
                                           bias=b1[:, eb, f:f + 1]).then_inc(s["hid_ready"], 1)

    @block.vector
    def _(dve):
        with dve.Fori(0, E // 2) as pair:
            for eb in range(2):
                with dve.Fori(0, TILES) as ti:
                    if gated:
                        dve.wait_ge(loaded[eb], OPEN + (pair + 1) * 64)
                    n = (2 * pair + eb) * TILES + ti
                    if gated:
                        dve.wait_ge(s["y_full"], OPEN + n * 2)
                        for f in range(FB):
                            dve.wait_ge(s["sig_done"], OPEN + n * FB + f + 1)
                            dve.scalar_tensor_tensor(hid[:, f, :], bank[(f % 3) * 2][:, 0:TILE], b1[:, eb, f:f + 1],
                                                     sig[:, f % 2, :], ALU.add, ALU.mult).then_inc(s["hid_ready"], 1)
                    dve.wait_ge(s["y_read"], OPEN + n * 2)
                    dve.tensor_copy(rt[:, :], route[:, bass.ds(2 * ti, 2), bass.ds(2 * pair + eb, 1)]
                                    .rearrange("p a b -> p (a b)")).then_inc(s["rt_ready"], 1)
                    dve.wait_ge(s["rt_ready"], OPEN + n + 1)
                    for half in range(2):
                        dve.wait_ge(s["y_full"], OPEN + n * 2 + half + 1)
                        h = h_all[:, bass.ds(2 * ti + half, 1), :].rearrange("p a d -> p (a d)")
                        dve.scalar_tensor_tensor(h, bank[6 + half][0:ROWS, 0:D], rt[:, half:half + 1], h,
                                                 ALU.mult, ALU.add).then_inc(s["y_read"], 1)


def host_layouts_rest(i):
    f = np.float32

    def rows(w):
        w = np.asarray(w)
        return np.ascontiguousarray(w.reshape(-1, 128, w.shape[1]).transpose(1, 0, 2))

    def pad_heads(w):
        w = np.asarray(w).reshape(-1, AH, AD)
        o = np.zeros((w.shape[0], AH, 32), f)
        o[:, :, :AD] = w
        return o.reshape(-1, AH * 32)

    def per_expert(w):
        w = np.asarray(w)
        return np.ascontiguousarray(w.reshape(E, -1, 128, w.shape[2]).transpose(0, 2, 1, 3))

    def bias(b):
        b = np.asarray(b)
        return np.ascontiguousarray(b.reshape(E, -1, 128).transpose(0, 2, 1))

    r = np.arange(ROWS)
    ok = (r[:, None] // T == r[None] // T) & (r[None] <= r[:, None])
    return dict(
        awq=rows(pad_heads(i["L1_attn_Wq"])), awk=rows(pad_heads(i["L1_attn_Wk"])), awv=rows(i["L1_attn_Wv"]),
        awo=rows(i["L1_attn_Wo"]), awg=rows(i["L1_ffn_w_gate"]),
        abq=pad_heads(np.asarray(i["L1_attn_bq"])[None]).reshape(-1, 128).T,
        abk=pad_heads(np.asarray(i["L1_attn_bk"])[None]).reshape(-1, 128).T,
        abv=np.asarray(i["L1_attn_bv"]), abo=np.asarray(i["L1_attn_bo"]), abg=np.asarray(i["L1_ffn_b_gate"]),
        amask=np.where(ok, 0.0, -1e30).astype(f),
        m0w1=per_expert(i["L0_ffn_w1"]), m0b1=bias(i["L0_ffn_b1"]), m0w2=per_expert(i["L0_ffn_w2"]),
        m0b2=np.asarray(i["L0_ffn_b2"]),
        m1w1=per_expert(i["L1_ffn_W1"]), m1b1=bias(i["L1_ffn_b1"]), m1w2=per_expert(i["L1_ffn_W2"]),
        m1b2=np.asarray(i["L1_ffn_b2"]),
    )


def build(nc, a, out):
    h_dram = nc.dram_tensor("h_rows", (ROWS, GROUPS, D), F32, kind="Internal").ap()
    xT_dram = nc.dram_tensor("normed_t", (128, DC, TOKENS), F32, kind="Internal").ap()
    with ExitStack() as kept:
        route = kept.enter_context(nc.sbuf_tensor("route", [ROWS, GROUPS, E], F32))
        with ExitStack() as ctx:
            delta_phase(nc, ctx, a, h_dram, xT_dram, route)
        h_all = kept.enter_context(nc.sbuf_tensor("h_all", [ROWS, GROUPS, D], F32))
        xT_all = kept.enter_context(nc.sbuf_tensor("xT_all", [128, DC, TOKENS], F32))
        reloaded = kept.enter_context(nc.semaphore("reloaded"))
        with nc.Block() as block:
            @block.sync
            def _(sp):
                sp.dma_start(h_all[:, :, :], h_dram).then_inc(reloaded, 16)
                sp.dma_start(xT_all[:, :, :], xT_dram).then_inc(reloaded, 16)
                sp.wait_ge(reloaded, 32)
        with ExitStack() as ctx:
            mixture_phase(nc, ctx, "m0_", a["m0w1"], a["m0b1"], a["m0w2"], a["m0b2"], True, h_all, xT_all, route)
        with ExitStack() as ctx:
            attention_phase(nc, ctx, a, h_all, xT_all, route)
        with ExitStack() as ctx:
            mixture_phase(nc, ctx, "m1_", a["m1w1"], a["m1b1"], a["m1w2"], a["m1b2"], False, h_all, xT_all, route,
                          out.rearrange("b t d -> (b t) d"))


def kernel(**inputs):
    import concourse.bacc as bacc
    from concourse.bass_utils import run_bass_kernel_spmd as run

    nc = bacc.Bacc("TRN2", target_bir_lowering=False, num_devices=1)
    arrays, a = {}, {}
    for name, v in {**host_layouts(inputs), **host_layouts_rest(inputs)}.items():
        v = np.ascontiguousarray(v)
        arrays["in_" + name] = v
        a[name] = nc.dram_tensor("in_" + name, v.shape, F32, kind="ExternalInput").ap()
    out = nc.dram_tensor("out", (IMAGES, T, D), F32, kind="ExternalOutput").ap()
    build(nc, a, out)
    return run(nc, [arrays], core_ids=[0]).results[0]["out"]
```

```python
import numpy as np
import concourse.bass as bass
from concourse import mybir
from contextlib import ExitStack

F32 = mybir.dt.float32
I32 = mybir.dt.int32
ALU = mybir.AluOpType
ACT = mybir.ActivationFunctionType
AX = mybir.AxisListType

A_LINKS = 25
A_XN = 3
A_XN2 = 13
TAIL_LINKS = 10

IMAGES, CHANNELS, SIDE, PATCH = 64, 3, 96, 16
GRID = SIDE // PATCH
PATCHES = GRID * GRID
T = PATCHES + 1
F = CHANNELS * PATCH * PATCH
FC = F // 128
D = 256
DC = D // 128
PER = 3
ROWS = PER * T
GROUPS = -(-IMAGES // PER)
FIRST_OF_LAST = IMAGES - PER
NEW_ROWS_OF_LAST = (IMAGES - PER * (GROUPS - 1)) * T
TOKENS = GROUPS * ROWS

H, HD, NH, TAPS = 8, 128, 3, 4
MICRO = NH * T
QB, KB, VB = H, NH * H, NH * H
CB = QB + KB + VB
CQ = CB // 4
LEVELS = [1, 2, 4, 8, 16, 32, 64]
E = 8
HID = 1024
AH, AD = 16, 16


def bc(ap, axis, n):
    shape = list(ap.shape)
    shape.insert(axis, n)
    return ap.unsqueeze(axis).to_broadcast(shape)


OPEN = 1


def open_counts(eng, sems):
    for x in sems:
        eng.sem_inc(x, OPEN)


class Chain:

    def __init__(self, eng, sem, per_turn, turn):
        self.eng, self.sem, self.per, self.turn, self.n = eng, sem, per_turn, turn, 0

    def link(self, ins):
        ins.then_inc(self.sem, 1)
        self.n += 1

    def wait(self):
        self.eng.wait_ge(self.sem, OPEN + self.turn * self.per + self.n)


def layer_norm(dve, chain, st, mv, ve, rstd, xn, h, var_ready, rstd_ready, turn, nth, per):
    chain.link(dve.bn_stats(st, h))
    chain.wait()
    dve.memset(ve, 0.0)
    chain.link(dve.bn_aggr(mv, st))
    chain.wait()
    dve.tensor_scalar(ve, mv[:, 1:2], 1e-5, None, ALU.add).then_inc(var_ready, 1)
    dve.wait_ge(rstd_ready, OPEN + turn * per + nth)
    chain.link(dve.tensor_scalar(xn, h, mv[:, 0:1], rstd, ALU.subtract, ALU.mult))


def delta_phase(nc, ctx, a, h_dram, sorted_x, taken):
    def sb(name, shape, dt=F32):
        return ctx.enter_context(nc.sbuf_tensor("d_" + name, shape, dt))

    bank = [ctx.enter_context(nc.psum_tensor(f"d_bank{i}", [128, 512], F32)) for i in range(8)]
    L = len(LEVELS)
    HT = 4
    NB = H // HT
    GRAM = MICRO + T
    TRIPLES = [(0, 3), (3, 3), (6, 2)]

    wlin = sb("wlin", [128, FC, D])
    wqkv = sb("wqkv", [128, DC, CB * 128])
    wgate = sb("wgate", [128, DC, H * HD])
    wout = sb("wout", [128, H, D])
    wab = sb("wab", [128, DC, 32])
    wrt = sb("wrt", [128, DC, E])
    taps = sb("taps", [128, CB, TAPS])
    ident = sb("ident", [128, 128])
    addend = sb("addend", [ROWS, D])
    dtb = sb("dtb", [ROWS, H])
    negA = sb("negA", [ROWS, H])
    rmsw = sb("rmsw", [HD, 1])
    rbias = sb("rbias", [ROWS, E])
    countdown = sb("countdown", [ROWS, E])
    phalf = sb("phalf", [ROWS, PER * H])
    nhalf = sb("nhalf", [ROWS, 1])
    ones = sb("ones", [128, 1])
    all_ones = sb("all_ones", [ROWS, ROWS])
    before = sb("before", [ROWS, ROWS])
    m_low = sb("m_low", [MICRO, MICRO])
    m_lvl = sb("m_lvl", [MICRO, L, MICRO])
    s_gt = sb("s_gt", [ROWS, T])
    s_le = sb("s_le", [ROWS, T])
    up_to = sb("up_to", [ROWS, PER, MICRO])
    after = sb("after", [ROWS, PER, MICRO])
    causal = sb("causal", [MICRO, T])
    spread = sb("spread", [ROWS, PER, MICRO])
    sub_step = sb("sub_step", [MICRO, NH])

    xin = sb("xin", [128, FC, ROWS])
    h1 = sb("h1", [ROWS, D])
    st, mv, ve, rstd = sb("st", [ROWS, 6]), sb("mv", [ROWS, 2]), sb("ve", [ROWS, 1]), sb("rstd", [ROWS, 1])
    xn = sb("xn", [ROWS, D])
    xnT = sb("xnT", [128, DC, ROWS])
    blog = sb("blog", [ROWS, NH * H])
    sp = sb("sp", [ROWS, 4, H])
    g = sb("g", [ROWS, H])
    g_gt = sb("g_gt", [ROWS, H, T])
    g_le = sb("g_le", [ROWS, H, T])
    y = sb("y", [128, 3, 4, ROWS])
    sg = sb("sg", [128, 2, 4, ROWS])
    KQ = sb("KQ", [128, PER, H, GRAM])
    V = sb("V", [128, PER, H, MICRO])
    sq = sb("sq", [128, H, ROWS])
    r2 = sb("r2", [MICRO, 4, H])
    bs = sb("bs", [MICRO, PER, NH, H])
    beta = sb("beta", [MICRO, PER, H])
    nbr2 = sb("nbr2", [MICRO, PER, H])
    rr = sb("rr", [MICRO, PER, H])
    br = sb("br", [MICRO, PER, H])
    dj = sb("dj", [MICRO, PER, H, T])
    di = sb("di", [MICRO, PER, H, T])
    dmask = sb("dmask", [MICRO, 2, H, MICRO])
    N = sb("N", [MICRO, PER, H, MICRO])
    X = sb("X", [MICRO, NB, HT, MICRO])
    Y = sb("Y", [MICRO, NB, HT, MICRO])
    Z = sb("Z", [MICRO, NB, HT, MICRO])
    C = sb("C", [MICRO, PER, H, HD])
    EE = sb("EE", [MICRO, NB, HT, HD])
    PT = sb("PT", [MICRO, PER, H, ROWS])
    gs = sb("gs", [ROWS, H, HD])
    gsig = sb("gsig", [ROWS, 512])
    r2_kept = sb("r2_kept", [ROWS, H])
    h_kept = sb("h_kept", [ROWS, D])
    h2 = sb("h2", [ROWS, D])
    O = y[0:ROWS, :, :, :].rearrange("p a b c -> p (a b c)")[:, 0:H * HD].rearrange("p (h c) -> p h c", h=H)
    osq = EE[:, :, :, :].rearrange("p a b c -> p (a b) c")
    rms = sb("rms", [ROWS, 4, H])
    OT = sq
    st2, mv2, ve2, rstd2 = sb("st2", [ROWS, 6]), sb("mv2", [ROWS, 2]), sb("ve2", [ROWS, 1]), sb("rstd2", [ROWS, 1])
    xrow = sb("xrow", [ROWS, D + 1])
    row_number = sb("row_number", [ROWS, GROUPS])
    carrier = sb("carrier", [1, 1])
    xrT = sb("xrT", [128, DC, ROWS])
    lg = sb("lg", [ROWS, E])
    mx = sb("mx", [ROWS, 2])
    hot = sb("hot", [ROWS, E])
    place = sb("place", [ROWS, E])
    slotf = sb("slotf", [ROWS, 1])
    slot = sb("slot", [ROWS, 1], I32)

    s = {n: nc.alloc_semaphore("d_" + n) for n in """w_tok w_const w_qkv w_gate w_out w_scaled consts setup setup2
        x_loaded tok_full group_kept group_moved var_ready rstd_ready xn_ready xt_full xt_ready ab_full ab_read spl spl_sig spl_ln g_ready
        gt_ready conv_full conv_init taps_done sig_done prod_done q_sq k_sq ks_full ks_read r2_ready rr_ready
        be_full be_sig be_sel br_ready nbr2_ready d_full d_exp di_ready gate_full gate_sig gate_mul
        dmask_ready kk_full n_off pt_ready n_ready vt_full c_ready
        z_full z_ready pairs_ready xt2_full x_ready y_full y0_ready y1_ready e_full e_ready w_full w_ready
        o_full o_gated o_sq o_mean o_pow o_ready ot_full ot_ready wo_full h2_ready h2_stored var2_ready rstd2_ready
        xrow_ready x2t_full x2t_ready lg_full hot_ready rank_full slot_ready numbered scattered
        pool_chain head_chain tail_chain norm_chain""".split()}
    block = ctx.enter_context(nc.Block())
    W_CONST = 16 * 20

    QUAD0 = 3
    assert QUAD0 + CQ + 1 <= 18 and PER * L == 21

    @block.sync
    def _(sync):
        open_counts(sync, [x for n, x in s.items() if n != "scattered"])
        sync.dma_start(xin[:, :, :], a["x"][0]).then_inc(s["x_loaded"], 16)
        sync.dma_start(wlin[:, :, :], a["wlin"]).then_inc(s["w_tok"], 16)
        sync.dma_start(h1[:, :], a["pos3"]).then_inc(s["w_tok"], 16)
        sync.dma_start(addend[:, :], a["rowadd"]).then_inc(s["w_tok"], 16)
        for t, n in ((wab, "wab"), (wrt, "wrt"), (taps, "taps"), (ident, "ident"), (m_low, "m_low"), (m_lvl, "m_lvl"),
                     (s_gt, "s_gt"), (s_le, "s_le"), (up_to, "up_to"), (after, "after"), (causal, "causal"),
                     (spread, "spread"), (countdown, "countdown"), (before, "before"), (sub_step, "sub_step"),
                     (row_number, "row_number"), (rmsw, "rmsw")):
            sync.dma_start(t[tuple(slice(None) for _ in t.shape)], a[n]).then_inc(s["w_const"], 16)
        for t, n in ((dtb, "dtb"), (negA, "alog"), (rbias, "rbias")):
            sync.dma_start(t[:, :], a[n].partition_broadcast(ROWS)).then_inc(s["w_const"], 16)
        for c in range(DC):
            sync.dma_start(wqkv[:, c, :], a["wqkv"][:, c, :]).then_inc(s["w_qkv"], 16)
        sync.dma_start(wgate[:, :, :], a["wgate"]).then_inc(s["w_gate"], 16)
        sync.dma_start(wout[:, :, :], a["wout"]).then_inc(s["w_out"], 16)

        def load_patches(n):
            sync.wait_ge(s["tok_full"], OPEN + n)
            x = a["x"][n] if isinstance(n, int) else a["x"][bass.ds(n, 1)].rearrange("a p c n -> p (a c) n")
            sync.dma_start(xin[:, :, :], x).then_inc(s["x_loaded"], 16)

        def store_rows(t):
            sync.wait_ge(s["h2_ready"], OPEN + t + 1)
            sync.dma_start(h_dram[:, bass.ds(t, 1), :].rearrange("p a d -> p (a d)"), h2[:, :])\
                .then_inc(s["h2_stored"], 16)

        load_patches(1)
        load_patches(2)
        with sync.Fori(1, GROUPS - 1) as gi:
            load_patches(gi + 2)
            store_rows(gi - 1)
        store_rows(GROUPS - 2)
        store_rows(GROUPS - 1)
        sync.wait_ge(s["h2_stored"], OPEN + 16 * GROUPS)
        sync.wait_ge(s["x_loaded"], OPEN + 16 * (GROUPS + 1))

    def tail_pe(pe, step, t, begun):
        if step == 2:
            for b in range(2):
                pe.wait_ge(s["o_ready"], OPEN + t * 2 + b + 1)
                if b == 0:
                    pe.wait_ge(s["xt_ready"], OPEN + begun)
                for j in range(4):
                    ins = pe.transpose(bank[6 + b][:, j * ROWS:(j + 1) * ROWS], O[:, 4 * b + j, :],
                                       ident[0:ROWS, 0:ROWS])
                ins.then_inc(s["ot_full"], 1)
        if step == 3:
            pe.wait_ge(s["ot_ready"], OPEN + t * 2 + 2)
            for hh in range(H):
                ins = pe.matmul(bank[6][0:ROWS, 0:D], OT[:, hh, :], wout[:, hh, :], start=hh == 0, stop=hh == H - 1)
            ins.then_inc(s["wo_full"], 1)
        if step == 5:
            pe.wait_ge(s["xrow_ready"], OPEN + t + 1)
            for c in range(DC):
                ins = pe.transpose(bank[7][:, c * ROWS:(c + 1) * ROWS], xrow[:, c * 128:(c + 1) * 128],
                                   ident[0:ROWS, 0:ROWS])
            ins.then_inc(s["x2t_full"], 1)
        if step == 6:
            pe.wait_ge(s["x2t_ready"], OPEN + t + 1)
            for c in range(DC):
                ins = pe.matmul(bank[6][0:ROWS, 0:E], xrT[:, c, :], wrt[:, c, :], start=c == 0, stop=c == DC - 1)
            ins.then_inc(s["lg_full"], 1)
        if step == 7:
            pe.wait_ge(s["hot_ready"], OPEN + t + 1)
            pe.matmul(bank[7][0:ROWS, 0:E], before[:, :], hot[:, :], start=True, stop=True)
            pe.matmul(bank[7][0:ROWS, E:2 * E], all_ones[:, :], hot[:, :], start=True, stop=True)\
                .then_inc(s["rank_full"], 1)

    def tail_act(act, step, t):
        if step == 1:
            act.wait_ge(s["o_pow"], OPEN + t + 1)
            act.wait_ge(s["o_gated"], OPEN + 2 * t + 2)
            for b in range(2):
                for j in range(4 * b, 4 * b + 4):
                    ins = act.activation(O[:, j, :], O[:, j, :], ACT.Copy, scale=rms[:, 3, j:j + 1])
                ins.then_inc(s["o_ready"], 1)
        if step == 2:
            for b in range(2):
                act.wait_ge(s["ot_full"], OPEN + t * 2 + b + 1)
                act.activation(OT[:, 4 * b:4 * b + 4, :], bank[6 + b][:, 0:4 * ROWS], ACT.Copy)\
                    .then_inc(s["ot_ready"], 1)
        if step == 5:
            act.wait_ge(s["x2t_full"], OPEN + t + 1)
            act.activation(xrT[:, :, :], bank[7][:, 0:DC * ROWS], ACT.Copy).then_inc(s["x2t_ready"], 1)

    def tail_dve(dve, step, t, ch):
        if step == 3:
            dve.wait_ge(s["wo_full"], OPEN + t + 1)
            dve.wait_ge(s["group_moved"], OPEN + t + 1)
            dve.tensor_tensor(h2[:, :], bank[6][0:ROWS, 0:D], h2[:, :], ALU.add).then_inc(s["h2_ready"], 1)
            dve.wait_ge(s["h2_ready"], OPEN + t + 1)
            ch.link(dve.bn_stats(st2[:, :], h2[:, :]))
            ch.wait()
            dve.memset(ve2[:, :], 0.0)
            ch.link(dve.bn_aggr(mv2[:, :], st2[:, :]))
            ch.wait()
            dve.tensor_scalar(ve2[:, :], mv2[:, 1:2], 1e-5, None, ALU.add).then_inc(s["var2_ready"], 1)
        if step == 4:
            dve.wait_ge(s["rstd2_ready"], OPEN + t + 1)
            dve.wait_ge(s["scattered"], 16 * t + 16)
            dve.tensor_scalar(xrow[:, D:D + 1], row_number[:, bass.ds(t, 1)], 1.0, None, ALU.mult)\
                .then_inc(s["numbered"], 1)
            dve.tensor_scalar(xrow[:, 0:D], h2[:, :], mv2[:, 0:1], rstd2[:, :], ALU.subtract, ALU.mult)\
                .then_inc(s["xrow_ready"], 1)
        if step == 6:
            dve.wait_ge(s["lg_full"], OPEN + t + 1)
            ch.link(dve.tensor_tensor(lg[:, :], bank[6][0:ROWS, 0:E], rbias[:, :], ALU.add))
            choose(dve, ch, lg[:, :], mx, countdown[:, :], hot[:, :], s["hot_ready"])
        if step == 7:
            place_rows(dve, ch, bank[7][0:ROWS, 0:E], bank[7][0:ROWS, E:2 * E], hot, place, slotf, slot,
                       taken, t, s["rank_full"], s["slot_ready"], s["scattered"])

    def tail_pool(pool, step, t):
        if step == 3:
            pool.wait_ge(s["var2_ready"], OPEN + t + 1)
            pool.tensor_tensor(rstd2[:, :], ve2[:, :], nhalf[:, :], ALU.pow).then_inc(s["rstd2_ready"], 1)
        if step == 7:
            pool.wait_ge(s["slot_ready"], OPEN + t + 1)
            pool.tensor_tensor(carrier[:, :], nhalf[0:1, 0:1], nhalf[0:1, 0:1], ALU.mult)
            pool.indirect_dma_start(sorted_x, bass.IndirectOffsetOnAxis(slot[:, 0:1], 0), xrow[:, :], None)\
                .then_inc(s["scattered"], 16)

    d_bank = [bank[4], bank[5], bank[7]]

    def head_pe(pe, step, n, beside=True):
        if step == 1:
            pe.wait_ge(s["x_loaded"], OPEN + n * 16 + 16)
            for c in range(FC):
                ins = pe.matmul(bank[6][0:ROWS, 0:D], xin[:, c, :], wlin[:, c, :], start=c == 0, stop=c == FC - 1)
            ins.then_inc(s["tok_full"], 1)
        if step == 2:
            pe.wait_ge(s["xn_ready"], OPEN + n + 1)
            for c in range(DC):
                ins = pe.transpose(bank[7][:, c * ROWS:(c + 1) * ROWS], xn[:, c * 128:(c + 1) * 128],
                                   ident[0:ROWS, 0:ROWS])
            ins.then_inc(s["xt_full"], 1)
        if step == 3:
            pe.wait_ge(s["xt_ready"], OPEN + n + 1)
            if beside:
                pe.wait_ge(s["ot_ready"], OPEN + 2 * (n - 1))
            for c in range(DC):
                ins = pe.matmul(bank[7][0:ROWS, 0:32], xnT[:, c, :], wab[:, c, :], start=c == 0, stop=c == DC - 1)
            ins.then_inc(s["ab_full"], 1)
        if QUAD0 <= step < QUAD0 + CQ:
            k = step - QUAD0
            if k >= 2:
                pe.wait_ge(s["taps_done"], OPEN + n * CQ + k - 1)
            for j in range(4):
                blk = 4 * k + j
                for c in range(DC):
                    ins = pe.matmul(bank[4 + k % 2][:, j * ROWS:(j + 1) * ROWS], wqkv[:, c, blk * 128:(blk + 1) * 128],
                                    xnT[:, c, :], start=c == 0, stop=c == DC - 1)
            ins.then_inc(s["conv_full"], 1)
        if step == 8:
            pe.wait_ge(s["ab_read"], OPEN + n * 2 + 2)
            for m in range(PER):
                ins = pe.matmul(bank[6][0:MICRO, m * NH * H:(m + 1) * NH * H], spread[:, m, :], blog[:, :],
                                start=True, stop=True)
            ins.then_inc(s["be_full"], 1)
        if step in (9, 14, 16, 18):
            r = (9, 14, 16, 18).index(step)
            if r == 0:
                pe.wait_ge(s["be_sig"], OPEN + n + 1)
                pe.wait_ge(s["q_sq"], OPEN + n + 1)
            else:
                pe.wait_ge(s["k_sq"], OPEN + n * PER + r)
            for hh in range(H):
                ins = pe.matmul(bank[6][0:MICRO, r * H + hh:r * H + hh + 1], sq[:, hh, :], ones[:, :],
                                start=True, stop=True)
            ins.then_inc(s["ks_full"], 1)
        if step in (19, 20):
            for k in range(3 * (step - 19), 3 * (step - 18)):
                if k == 0:
                    pe.wait_ge(s["gt_ready"], OPEN + n * 2 + 2)
                    pe.wait_ge(s["taps_done"], OPEN + n * CQ + CQ)
                if k >= 3:
                    pe.wait_ge(s["d_exp"], OPEN + n * PER * 2 + k - 2)
                lhs, rhs = ((up_to, g_gt), (after, g_le))[k % 2]
                pe.matmul(d_bank[k % 3][0:MICRO, 0:H * T], lhs[:, k // 2, :],
                          rhs[:, :, :].rearrange("p h t -> p (h t)"), start=True, stop=True)\
                    .then_inc(s["d_full"], 1)

    def head_act(act, step, n):
        if step == 2:
            act.wait_ge(s["xt_full"], OPEN + n + 1)
            act.activation(xnT[:, :, :], bank[7][:, 0:DC * ROWS], ACT.Copy).then_inc(s["xt_ready"], 1)
        if step == 4:
            act.wait_ge(s["spl"], OPEN + n + 1)
            act.activation(sp[:, 2], sp[:, 1], ACT.Sigmoid).then_inc(s["spl_sig"], 1)
        if QUAD0 + 2 <= step < QUAD0 + CQ + 2:
            k = step - QUAD0 - 2
            act.wait_ge(s["taps_done"], OPEN + n * CQ + k + 1)
            act.wait_ge(s["prod_done"], OPEN + n * CQ + max(k - 1, 0))
            act.activation(sg[:, k % 2], y[:, k % 3], ACT.Sigmoid).then_inc(s["sig_done"], 1)
        if QUAD0 <= step < QUAD0 + CQ:
            k = step - QUAD0
            act.wait_ge(s["conv_full"], OPEN + n * CQ + k + 1)
            act.wait_ge(s["prod_done"], OPEN + n * CQ + max(k - 2, 0))
            for j in range(4):
                ins = act.activation(y[:, k % 3, j, :], bank[4 + k % 2][:, j * ROWS:(j + 1) * ROWS], ACT.Copy,
                                     scale=taps[:, 4 * k + j, TAPS - 1:TAPS])
            ins.then_inc(s["conv_init"], 1)
        if step == 8:
            act.wait_ge(s["be_full"], OPEN + n + 1)
            act.activation(bs[:, :, :, :].rearrange("p m i h -> p (m i h)"), bank[6][0:MICRO, 0:PER * NH * H],
                           ACT.Sigmoid).then_inc(s["be_sig"], 1)
        if step == 18:
            act.wait_ge(s["spl_sig"], OPEN + n + 1)
            act.activation(sp[:, 2], sp[:, 2], ACT.Ln).then_inc(s["spl_ln"], 1)
        if step in (19, 20):
            for k in range(3 * (step - 19), 3 * (step - 18)):
                act.wait_ge(s["d_full"], OPEN + n * PER * 2 + k + 1)
                act.activation((dj, di)[k % 2][:, k // 2], d_bank[k % 3][0:MICRO, 0:H * T].rearrange("p (h t) -> p h t", h=H),
                               ACT.Exp).then_inc(s["d_exp"], 1)

    def head_dve(dve, step, n, ch):
        if step == 1:
            dve.wait_ge(s["tok_full"], OPEN + n + 1)
            dve.wait_ge(s["group_kept"], OPEN + n)
            ch.link(dve.tensor_tensor(h1[:, :], bank[6][0:ROWS, 0:D], addend[:, :], ALU.add))
            ch.wait()
            ch.link(dve.bn_stats(st[:, :], h1[:, :]))
            ch.wait()
            dve.memset(ve[:, :], 0.0)
            ch.link(dve.bn_aggr(mv[:, :], st[:, :]))
            ch.wait()
            dve.tensor_scalar(ve[:, :], mv[:, 1:2], 1e-5, None, ALU.add).then_inc(s["var_ready"], 1)
        if step == 2:
            dve.wait_ge(s["rstd_ready"], OPEN + n + 1)
            dve.tensor_scalar(xn[:, :], h1[:, :], mv[:, 0:1], rstd[:, :], ALU.subtract, ALU.mult)\
                .then_inc(s["xn_ready"], 1)
        if step == 3:
            dve.wait_ge(s["ab_full"], OPEN + n + 1)
            dve.tensor_copy(blog[:, :], bank[7][0:ROWS, 0:NH * H]).then_inc(s["ab_read"], 1)
            dve.tensor_tensor(sp[:, 0], bank[7][0:ROWS, NH * H:NH * H + H], dtb[:, :], ALU.add)\
                .then_inc(s["ab_read"], 1)
            dve.wait_ge(s["ab_read"], OPEN + n * 2 + 2)
            dve.scalar_tensor_tensor(sp[:, 1], sp[:, 0], -1.0, sp[:, 0], ALU.mult, ALU.max).then_inc(s["spl"], 1)
        if QUAD0 < step <= QUAD0 + CQ:
            k = step - QUAD0 - 1
            dve.wait_ge(s["conv_init"], OPEN + n * CQ + k + 1)
            for tap in range(TAPS - 2, -1, -1):
                sh = TAPS - 1 - tap
                if sh > 1:
                    ch.wait()
                for j in range(4):
                    yv = y[:, k % 3, j, :].rearrange("p (m t) -> p m t", t=T)[:, :, sh:T]
                    pv = bank[4 + k % 2][:, j * ROWS:(j + 1) * ROWS].rearrange("p (m t) -> p m t", t=T)[:, :, 0:T - sh]
                    ins = dve.scalar_tensor_tensor(yv, pv, taps[:, 4 * k + j, tap:tap + 1], yv, ALU.mult, ALU.add)
                if tap:
                    ch.link(ins)
                else:
                    ins.then_inc(s["taps_done"], 1)
        if step == 9:
            dve.wait_ge(s["be_sig"], OPEN + n + 1)
            for m in range(PER):
                ins = dve.tensor_tensor(bs[:, m], bs[:, m], bc(sub_step[:, :], 2, H), ALU.mult)
            ch.link(ins)
            ch.wait()
            ch.link(dve.tensor_reduce(beta[:, :, :], bs[:, :, :, :].rearrange("p m i h -> p m h i"), AX.X, ALU.add))
        if step == 18:
            dve.wait_ge(s["spl_ln"], OPEN + n + 1)
            ch.link(dve.scalar_tensor_tensor(sp[:, 3], sp[:, 0], 0.0, sp[:, 2], ALU.max, ALU.subtract))
            ch.wait()
            dve.tensor_tensor(g[:, :], sp[:, 3], negA[:, :], ALU.mult).then_inc(s["g_ready"], 1)
        if step == 19:
            dve.wait_ge(s["ks_full"], OPEN + n * 4 + 4)
            dve.tensor_scalar(r2[:, :, :].rearrange("p a h -> p (a h)"), bank[6][0:MICRO, 0:4 * H], 1e-6, None,
                              ALU.add).then_inc(s["ks_read"], 1)
            dve.wait_ge(s["ks_read"], OPEN + n + 1)
            dve.reciprocal(r2[:, :, :], r2[:, :, :]).then_inc(s["r2_ready"], 1)
            dve.wait_ge(s["r2_ready"], OPEN + n + 1)
            dve.scalar_tensor_tensor(nbr2[:, :, :], beta[:, :, :], -2.0, r2[:, 1:4], ALU.mult, ALU.mult)\
                .then_inc(s["nbr2_ready"], 1)

    def head_pool(pool, step, n, beside=True):
        if step == 1:
            pool.wait_ge(s["var_ready"], OPEN + n + 1)
            pool.tensor_tensor(rstd[:, :], ve[:, :], nhalf[:, :], ALU.pow).then_inc(s["rstd_ready"], 1)
        if QUAD0 + 2 <= step < QUAD0 + CQ + 2:
            k = step - QUAD0 - 2
            kind, i, hh = block_of(k)
            pool.wait_ge(s["sig_done"], OPEN + n * CQ + k + 1)
            for m in range(PER):
                c_ = slice(m * T, (m + 1) * T)
                if kind == "q":
                    to = KQ[:, m, hh:hh + 4, MICRO:GRAM]
                else:
                    to = (KQ if kind == "k" else V)[:, m, hh:hh + 4, i:MICRO:NH]
                ins = pool.tensor_tensor(to, y[:, k % 3, :, c_], sg[:, k % 2, :, c_], ALU.mult)
            ins.then_inc(s["prod_done"], 1)
        if step == 7:
            pool.wait_ge(s["prod_done"], OPEN + n * CQ + 2)
            pool.wait_ge(s["ks_full"], OPEN + n * 4)
            if beside:
                pool.wait_ge(s["wo_full"], OPEN + n - 1)
            for m in range(PER):
                q = KQ[:, m, :, MICRO:GRAM]
                ins = pool.tensor_tensor(sq[:, :, m * T:(m + 1) * T], q, q, ALU.mult)
            ins.then_inc(s["q_sq"], 1)
        if step in (13, 15, 17):
            m = (step - 13) // 2
            if m == 0:
                pool.wait_ge(s["prod_done"], OPEN + n * CQ + 8)
            pool.wait_ge(s["ks_full"], OPEN + n * 4 + m + 1)
            k_ = KQ[:, m, :, 0:MICRO]
            pool.tensor_tensor(sq[:, :, :], k_, k_, ALU.mult).then_inc(s["k_sq"], 1)
        if step == 18:
            pool.wait_ge(s["g_ready"], OPEN + n + 1)
            pool.tensor_tensor(g_gt[:, :, :], bc(g[:, :], 2, T), bc(s_gt[:, :], 1, H), ALU.mult)\
                .then_inc(s["gt_ready"], 1)
            pool.tensor_tensor(g_le[:, :, :], bc(g[:, :], 2, T), bc(s_le[:, :], 1, H), ALU.mult)\
                .then_inc(s["gt_ready"], 1)
        if step == 19:
            pool.wait_ge(s["r2_ready"], OPEN + n + 1)
            pool.tensor_tensor(rr[:, :, :], r2[:, 1:4], phalf[:, :].rearrange("p (a h) -> p a h", h=H), ALU.pow)\
                .then_inc(s["rr_ready"], 1)

    @block.gpsimd
    def _(pool):
        pool.memset(phalf[:, :], 0.5).then_inc(s["consts"], 1)
        pool.memset(nhalf[:, :], -0.5).then_inc(s["consts"], 1)
        pool.memset(ones[:, :], 1.0).then_inc(s["consts"], 1)
        pool.memset(all_ones[:, :], 1.0).then_inc(s["consts"], 1)
        pool.memset(PT[:, :, :, :], 0.0).then_inc(s["consts"], 1)
        pool.dma_start(taken[:, :], a["regions"]).then_inc(s["scattered"], 16)
        pool.wait_ge(s["w_const"], OPEN + W_CONST)
        pool.wait_ge(s["consts"], OPEN + 5)
        for step in range(21):
            head_pool(pool, step, 0, beside=False)

        def turn(gi, first, last):
            ch = Chain(pool, s["pool_chain"], PER, gi)
            for m in range(PER):
                pool.wait_ge(s["d_exp"], OPEN + (gi * PER + m) * 2 + 2)
                pool.wait_ge(s["nbr2_ready"], OPEN + gi + 1)
                ch.link(pool.tensor_tensor(dj[:, m], dj[:, m], bc(nbr2[:, m], 2, T), ALU.mult))
                pool.tensor_tensor(di[:, m], di[:, m], bc(causal[:, :], 1, H), ALU.mult).then_inc(s["di_ready"], 1)
                ch.wait()
                if m == 2:
                    unit_diagonal(gi, 0)
                for hh in range(0, H, 4):
                    ins = pool.tensor_tensor(
                        dmask[:, m % 2, hh:hh + 4, :].rearrange("p h (t i) -> p h t i", i=NH),
                        bc(dj[:, m, hh:hh + 4, :], 3, NH),
                        bc(m_low[:, :].rearrange("p (t i) -> p t i", i=NH), 1, 4), ALU.mult)
                ins.then_inc(s["dmask_ready"], 1)
            unit_diagonal(gi, 1)
            unit_diagonal(gi, 2)
            pool.tensor_copy(r2_kept[:, :], r2[0:ROWS, 0, :])
            pool.tensor_copy(h_kept[:, :], h1[:, :]).then_inc(s["group_kept"], 1)
            for step in range(PER * L):
                if step == 8:
                    pool.wait_ge(s["group_kept"], OPEN + gi + 1)
                    if not first:
                        pool.wait_ge(s["h2_stored"], OPEN + 16 * gi)
                    pool.tensor_tensor(h2[:, :], h_kept[:, :], bc(ones[0:ROWS, 0], 1, D), ALU.mult).then_inc(s["group_moved"], 1)
                if not first:
                    tail_pool(pool, step, gi - 1)
                if not last:
                    head_pool(pool, step, gi + 1)
            pool.wait_ge(s["o_mean"], OPEN + gi + 1)
            pool.tensor_tensor(rms[:, 3], rms[:, 2], phalf[0:ROWS, 0:H], ALU.pow).then_inc(s["o_pow"], 1)

        def unit_diagonal(gi, m):
            pool.wait_ge(s["n_off"], OPEN + (gi * PER + m) * 3 + 3)
            for b in range(NB):
                nv = N[:, m, HT * b:HT * b + HT, :]
                pool.tensor_tensor(nv, nv, bc(ident[0:MICRO, 0:MICRO], 1, HT), ALU.add).then_inc(s["n_ready"], 1)

        turn(0, True, False)
        with pool.Fori(1, GROUPS - 1) as gi:
            turn(gi, False, False)
        turn(GROUPS - 1, False, True)
        for step in range(8):
            tail_pool(pool, step, GROUPS - 1)
        pool.wait_ge(s["scattered"], 16 * GROUPS + 16)

    @block.tensor
    def _(pe):
        pe.wait_ge(s["w_tok"], OPEN + 48)
        pe.wait_ge(s["w_const"], OPEN + W_CONST)
        pe.wait_ge(s["consts"], OPEN + 5)
        for step in range(21):
            if step == QUAD0:
                pe.wait_ge(s["w_qkv"], OPEN + 32)
            head_pe(pe, step, 0, beside=False)
        pe.wait_ge(s["w_gate"], OPEN + 16)
        pe.wait_ge(s["w_scaled"], OPEN + 1)

        def turn(gi, first, last):
            for n in range(2):
                for c in range(DC):
                    ins = pe.matmul(bank[n][0:ROWS, :], xnT[:, c, :], wgate[:, c, n * 512:(n + 1) * 512],
                                    start=c == 0, stop=c == DC - 1)
                ins.then_inc(s["gate_full"], 1)
            pe.wait_ge(s["prod_done"], OPEN + (gi + 1) * CQ)
            pe.wait_ge(s["ks_read"], OPEN + gi + 1)
            pe.wait_ge(s["d_exp"], OPEN + (gi + 1) * PER * 2)
            for m in range(PER):
                for q, (h0, nh) in enumerate(TRIPLES):
                    if m:
                        pe.wait_ge(s["pt_ready"], OPEN + (gi * PER + m - 1) * 3 + q + 1)
                    for j in range(nh):
                        ins = pe.matmul(bank[4 + q][0:MICRO, j * GRAM:(j + 1) * GRAM], KQ[:, m, h0 + j, 0:MICRO],
                                        KQ[:, m, h0 + j, :], start=True, stop=True)
                    ins.then_inc(s["kk_full"], 1)
                for b in range(NB):
                    if m:
                        pe.wait_ge(s["c_ready"], OPEN + (gi * PER + m - 1) * NB + b + 1)
                    elif not first:
                        pe.wait_ge(s["o_gated"], OPEN + gi * 2)
                    for j in range(HT):
                        ins = pe.transpose(bank[2 + b][0:MICRO, j * HD:(j + 1) * HD], V[:, m, HT * b + j, :], ident[:, :])
                    ins.then_inc(s["vt_full"], 1)
            pe.wait_ge(s["c_ready"], OPEN + (gi + 1) * PER * NB)
            pe.wait_ge(s["gate_mul"], OPEN + gi * 2 + 2)
            pe.wait_ge(s["pt_ready"], OPEN + (gi + 1) * PER * 3)
            for m in range(PER):
                for l in range(L):
                    u = (gi * PER + m) * NB
                    zn = u * L + l * NB
                    yn = (gi * PER + m) * (L - 2) + l - 1
                    for b in range(NB):
                        if l == 0:
                            if m:
                                pe.wait_ge(s["w_ready"], OPEN + u - NB + b + 1)
                            pe.wait_ge(s["n_ready"], OPEN + u + b + 1)
                            for j in range(HT):
                                ins = pe.transpose(bank[b][0:MICRO, j * MICRO:(j + 1) * MICRO], N[:, m, HT * b + j, :],
                                                   ident[0:MICRO, 0:MICRO])
                        else:
                            if l == 1:
                                pe.wait_ge(s["pairs_ready"], OPEN + u + b + 1)
                            else:
                                pe.wait_ge(s[f"y{b}_ready"], OPEN + yn)
                            for j in range(HT):
                                ins = pe.matmul(bank[b][0:MICRO, j * MICRO:(j + 1) * MICRO], N[:, m, HT * b + j, :],
                                                Y[:, b, j, :], start=True, stop=True)
                        ins.then_inc(s["z_full"], 1)
                    for b in range(NB):
                        if 1 <= l <= L - 2:
                            for j in range(HT):
                                ins = pe.transpose(bank[2 + b][0:MICRO, j * MICRO:(j + 1) * MICRO], Y[:, b, j, :],
                                                   ident[0:MICRO, 0:MICRO])
                            ins.then_inc(s["xt2_full"], 1)
                        if l == L - 1:
                            for j in range(HT):
                                ins = pe.matmul(bank[2 + b][0:MICRO, j * HD:(j + 1) * HD], Y[:, b, j, :],
                                                C[:, m, HT * b + j, :], start=True, stop=True)
                            ins.then_inc(s["e_full"], 1)
                    if not last:
                        head_pe(pe, m * L + l, gi + 1)
                    if not first:
                        tail_pe(pe, m * L + l, gi - 1, GROUPS if last else gi + 2)
                    for b in range(NB):
                        if l == 0:
                            continue
                        pe.wait_ge(s["z_ready"], OPEN + u * (L - 1) + (l - 1) * NB + b + 1)
                        if l < L - 1:
                            pe.wait_ge(s["x_ready"], OPEN + u * (L - 2) + (l - 1) * NB + b + 1)
                            for j in range(HT):
                                ins = pe.matmul(bank[2 + b][0:MICRO, j * MICRO:(j + 1) * MICRO], X[:, b, j, :],
                                                Z[:, b, j, :], start=True, stop=True)
                            ins.then_inc(s["y_full"], 1)
                        else:
                            pe.wait_ge(s["e_ready"], OPEN + u + b + 1)
                            for j in range(HT):
                                ins = pe.matmul(bank[b][0:MICRO, j * HD:(j + 1) * HD], Z[:, b, j, :], EE[:, b, j, :],
                                                start=True, stop=True)
                            ins.then_inc(s["w_full"], 1)
            pe.wait_ge(s["w_ready"], OPEN + (gi + 1) * PER * NB)
            for b in range(2):
                for j in range(4):
                    for m in range(PER):
                        ins = pe.matmul(bank[2 + b][0:ROWS, j * HD:(j + 1) * HD], PT[:, m, 4 * b + j, :],
                                        C[:, m, 4 * b + j, :], start=m == 0, stop=m == PER - 1)
                ins.then_inc(s["o_full"], 1)

        turn(0, True, False)
        with pe.Fori(1, GROUPS - 1) as gi:
            turn(gi, False, False)
        turn(GROUPS - 1, False, True)
        for step in range(8):
            tail_pe(pe, step, GROUPS - 1, GROUPS)

    @block.scalar
    def _(act):
        act.wait_ge(s["w_const"], OPEN + W_CONST)
        act.activation(negA[:, :], negA[:, :], ACT.Exp).then_inc(s["setup"], 1)
        act.wait_ge(s["w_out"], OPEN + 16)
        act.activation(wout[:, :, :], wout[:, :, :], ACT.Copy, scale=rmsw[:, 0:1]).then_inc(s["w_scaled"], 1)
        for step in range(21):
            head_act(act, step, 0)

        def turn(gi, first, last):
            for n in range(2):
                act.wait_ge(s["gate_full"], OPEN + gi * 2 + n + 1)
                if n:
                    act.wait_ge(s["gate_mul"], OPEN + gi * 2 + 1)
                elif not first:
                    act.wait_ge(s["gate_mul"], OPEN + gi * 2)
                act.activation(gsig[:, :], bank[n][0:ROWS, :], ACT.Sigmoid).then_inc(s["gate_sig"], 1)
            act.wait_ge(s["br_ready"], OPEN + gi + 1)
            for m in range(PER):
                for b in range(NB):
                    act.wait_ge(s["vt_full"], OPEN + (gi * PER + m) * NB + b + 1)
                    for j in range(HT):
                        ins = act.activation(C[:, m, HT * b + j, :], bank[2 + b][0:MICRO, j * HD:(j + 1) * HD], ACT.Copy,
                                             scale=br[:, m, HT * b + j:HT * b + j + 1])
                    ins.then_inc(s["c_ready"], 1)
            for m in range(PER):
                for l in range(L):
                    u = (gi * PER + m) * NB
                    for b in range(NB):
                        if 1 <= l <= L - 2:
                            act.wait_ge(s["xt2_full"], OPEN + u * (L - 2) + (l - 1) * NB + b + 1)
                            act.activation(X[:, b], bank[2 + b][0:MICRO, 0:HT * MICRO].rearrange("p (h c) -> p h c", h=HT),
                                           ACT.Copy).then_inc(s["x_ready"], 1)
                        if l == L - 1:
                            act.wait_ge(s["e_full"], OPEN + u + b + 1)
                            act.activation(EE[:, b], bank[2 + b][0:MICRO, :].rearrange("p (h c) -> p h c", h=HT),
                                           ACT.Copy).then_inc(s["e_ready"], 1)
                    if not last:
                        head_act(act, m * L + l, gi + 1)
                    if not first:
                        tail_act(act, m * L + l, gi - 1)
                    if 1 <= l <= L - 2:
                        act.wait_ge(s["y_full"], OPEN + u * (L - 2) + (l - 1) * NB + 2)
                        act.activation(Y[:, 1], bank[3][0:MICRO, 0:HT * MICRO].rearrange("p (h c) -> p h c", h=HT),
                                       ACT.Copy).then_inc(s["y1_ready"], 1)
                    if l == L - 1:
                        for b in range(NB):
                            act.wait_ge(s["w_full"], OPEN + u + b + 1)
                            act.activation(C[:, m, HT * b:HT * b + HT, :],
                                           bank[b][0:MICRO, :].rearrange("p (h c) -> p h c", h=HT), ACT.Copy)\
                                .then_inc(s["w_ready"], 1)
            for b in range(2):
                act.wait_ge(s["o_full"], OPEN + gi * 2 + b + 1)
                act.activation(osq[:, 4 * b:4 * b + 4, :], bank[2 + b][0:ROWS, :].rearrange("p (h c) -> p h c", h=4),
                               ACT.Square).then_inc(s["o_sq"], 1)

        turn(0, True, False)
        with act.Fori(1, GROUPS - 1) as gi:
            turn(gi, False, False)
        turn(GROUPS - 1, False, True)
        for step in range(8):
            tail_act(act, step, GROUPS - 1)

    @block.vector
    def _(dve):
        dve.wait_ge(s["w_tok"], OPEN + 48)
        dve.tensor_tensor(addend[:, :], addend[:, :], h1[:, :], ALU.add).then_inc(s["setup2"], 1)
        dve.wait_ge(s["setup"], OPEN + 1)
        dve.tensor_scalar(negA[:, :], negA[:, :], -1.0, None, ALU.mult).then_inc(s["setup2"], 1)
        dve.wait_ge(s["setup2"], OPEN + 2)
        dve.wait_ge(s["w_const"], OPEN + W_CONST)
        dve.wait_ge(s["consts"], OPEN + 5)
        ch0 = Chain(dve, s["head_chain"], 0, 0)
        for step in range(21):
            head_dve(dve, step, 0, ch0)
        HEAD = ch0.n
        ch0 = None

        def turn(gi, first, last):
            head = Chain(dve, s["head_chain"], HEAD, gi + 1)
            tail = Chain(dve, s["tail_chain"], TAIL_LINKS, gi - 1)
            norm = Chain(dve, s["norm_chain"], 4, gi)
            dve.wait_ge(s["rr_ready"], OPEN + gi + 1)
            dve.scalar_tensor_tensor(br[:, :, :], beta[:, :, :], 2.0, rr[:, :, :], ALU.mult, ALU.mult)\
                .then_inc(s["br_ready"], 1)
            for n in range(2):
                dve.wait_ge(s["gate_sig"], OPEN + gi * 2 + n + 1)
                dve.tensor_tensor(gs[:, 4 * n:4 * n + 4, :], bank[n][0:ROWS, :].rearrange("p (h c) -> p h c", h=4),
                                  gsig[:, :].rearrange("p (h c) -> p h c", h=4), ALU.mult).then_inc(s["gate_mul"], 1)
            for m in range(PER):
                dve.wait_ge(s["dmask_ready"], OPEN + gi * PER + m + 1)
                for q, (h0, nh) in enumerate(TRIPLES):
                    dve.wait_ge(s["kk_full"], OPEN + (gi * PER + m) * 3 + q + 1)
                    pv = bank[4 + q][0:MICRO, 0:nh * GRAM].rearrange("p (h c) -> p h c", h=nh)
                    dve.tensor_tensor(N[:, m, h0:h0 + nh, :], pv[:, :, 0:MICRO], dmask[:, m % 2, h0:h0 + nh, :], ALU.mult)\
                        .then_inc(s["n_off"], 1)
                    if q == 0:
                        dve.wait_ge(s["di_ready"], OPEN + gi * PER + m + 1)
                    dve.tensor_tensor(PT[:, m, h0:h0 + nh, m * T:(m + 1) * T], pv[:, :, MICRO:GRAM],
                                      di[:, m, h0:h0 + nh, :], ALU.mult).then_inc(s["pt_ready"], 1)
            for m in range(PER):
                for l in range(L):
                    u = (gi * PER + m) * NB
                    for b in range(NB):
                        dve.wait_ge(s["z_full"], OPEN + u * L + l * NB + b + 1)
                        to, done = (Y, "pairs_ready") if l == 0 else (Z, "z_ready")
                        dve.tensor_tensor(to[:, b], bank[b][0:MICRO, 0:HT * MICRO].rearrange("p (h c) -> p h c", h=HT),
                                          bc(m_lvl[:, l, :], 1, HT), ALU.mult).then_inc(s[done], 1)
                    if not last:
                        head_dve(dve, m * L + l, gi + 1, head)
                    if not first:
                        tail_dve(dve, m * L + l, gi - 1, tail)
                    if 1 <= l <= L - 2:
                        dve.wait_ge(s["y_full"], OPEN + u * (L - 2) + (l - 1) * NB + 1)
                        dve.tensor_copy(Y[:, 0], bank[2][0:MICRO, 0:HT * MICRO].rearrange("p (h c) -> p h c", h=HT))\
                            .then_inc(s["y0_ready"], 1)
            assert head.n in (0, HEAD) and tail.n in (0, TAIL_LINKS), (tail.n, head.n)
            for b in range(2):
                dve.wait_ge(s["o_sq"], OPEN + gi * 2 + b + 1)
                dve.tensor_tensor(O[:, 4 * b:4 * b + 4, :], bank[2 + b][0:ROWS, :].rearrange("p (h d) -> p h d", h=4),
                                  gs[:, 4 * b:4 * b + 4, :], ALU.mult).then_inc(s["o_gated"], 1)
            dve.wait_ge(s["group_kept"], OPEN + gi + 1)
            norm.link(dve.tensor_reduce(rms[:, 0], osq, AX.X, ALU.add))
            norm.wait()
            norm.link(dve.scalar_tensor_tensor(rms[:, 1], rms[:, 0], 1.0 / (HD * HD), r2_kept[:, :], ALU.mult, ALU.mult))
            norm.wait()
            norm.link(dve.tensor_scalar(rms[:, 0], rms[:, 1], 1e-5, None, ALU.add))
            norm.wait()
            norm.link(dve.reciprocal(rms[:, 1], rms[:, 0]))
            norm.wait()
            dve.scalar_tensor_tensor(rms[:, 2], r2_kept[:, :], 1.0 / HD, rms[:, 1], ALU.mult, ALU.mult)\
                .then_inc(s["o_mean"], 1)

        turn(0, True, False)
        with dve.Fori(1, GROUPS - 1) as gi:
            turn(gi, False, False)
        turn(GROUPS - 1, False, True)
        tail = Chain(dve, s["tail_chain"], TAIL_LINKS, GROUPS - 1)
        for step in range(8):
            tail_dve(dve, step, GROUPS - 1, tail)


def choose(dve, ch, lg, mx, countdown, out, ready):
    ch.wait()
    ch.link(dve.tensor_reduce(mx[:, 0:1], lg, AX.X, ALU.max))
    ch.wait()
    ch.link(dve.scalar_tensor_tensor(lg, lg, mx[:, 0:1], countdown, ALU.is_equal, ALU.mult))
    ch.wait()
    ch.link(dve.tensor_reduce(mx[:, 1:2], lg, AX.X, ALU.max))
    ch.wait()
    dve.tensor_scalar(out, lg, mx[:, 1:2], None, ALU.is_equal).then_inc(ready, 1)


def block_of(k):
    if k < 2:
        return "q", 0, 4 * k
    k -= 2
    kind = "k" if k < 6 else "v"
    k %= 6
    return kind, k // 2, 4 * (k % 2)


def host_layouts(i):
    f = np.float32
    x = np.asarray(i["x"])
    p = x.reshape(IMAGES, CHANNELS, GRID, PATCH, GRID, PATCH).transpose(0, 2, 4, 1, 3, 5).reshape(IMAGES, PATCHES, F)
    tok = np.zeros((IMAGES, T, F), f)
    tok[:, 1:] = p
    first = [min(PER * g, FIRST_OF_LAST) for g in range(GROUPS + 1)]
    xg = np.stack([tok[b:b + PER] for b in first]).reshape(-1, ROWS, FC, 128).transpose(0, 3, 2, 1)

    def rows(w):
        w = np.asarray(w)
        return np.ascontiguousarray(w.reshape(-1, 128, w.shape[1]).transpose(1, 0, 2))

    blin = np.asarray(i["L0_tok_b_lin"])
    one = np.concatenate([np.asarray(i["L0_tok_class_token"])[0], np.broadcast_to(blin, (PATCHES, D))])
    taps = np.concatenate([np.asarray(i[f"L0_attn_conv_{c}"]) for c in "qkv"])
    r, c = np.arange(MICRO)[:, None], np.arange(MICRO)[None]
    lvl = [((r // (2 * s)) == (c // (2 * s))) & ((r // s) % 2 == 1) & ((c // s) % 2 == 0) | (r == c) for s in LEVELS]
    tl = (np.arange(ROWS) % T)[:, None]
    im = (np.arange(ROWS) // T)[:, None]
    step_t = (np.arange(MICRO) // NH)[None]
    return dict(
        x=xg, wlin=rows(np.asarray(i["L0_tok_W_lin"]).T), pos3=np.tile(np.asarray(i["L0_tok_position_embeddings"])[0], (PER, 1)),
        rowadd=np.tile(one, (PER, 1)),
        wqkv=rows(np.concatenate([np.asarray(i[f"L0_attn_W{c}"]) for c in "qkv"], 1)),
        wgate=rows(i["L0_attn_Wg"]), wout=rows(i["L0_attn_Wo"]),
        wab=rows(np.concatenate([np.asarray(i["L0_attn_Wb"]), np.asarray(i["L0_attn_Wa"])], 1)),
        wrt=rows(i["L0_ffn_router_w"]), taps=taps.reshape(CB, 128, TAPS).transpose(1, 0, 2),
        dtb=np.asarray(i["L0_attn_dt_bias"]), alog=np.asarray(i["L0_attn_A_log"]),
        rmsw=np.asarray(i["L0_attn_rms_weight"])[:, None], rbias=np.asarray(i["L0_ffn_router_b"]),
        ident=np.eye(128, dtype=f), m_low=(r > c).astype(f),
        m_lvl=np.stack([m.T for m in lvl], 1).astype(f),
        s_gt=(tl > np.arange(T)[None]).astype(f), s_le=(tl <= np.arange(T)[None]).astype(f),
        up_to=np.stack([(im == m) & (tl <= step_t) for m in range(PER)], 1).astype(f),
        after=np.stack([(im == m) & (tl > step_t) for m in range(PER)], 1).astype(f),
        causal=(step_t.T <= np.arange(T)[None]).astype(f),
        spread=np.stack([(im == m) & (tl == step_t) for m in range(PER)], 1).astype(f),
        sub_step=(r % NH == np.arange(NH)[None]).astype(f),
        countdown=np.tile(np.arange(E, 0, -1).astype(f), (ROWS, 1)),
    )


SLOTS = 256
REGION = (-(-TOKENS // SLOTS) + 1) * SLOTS
EMPTY = E * REGION
SORTED_ROWS = EMPTY + SLOTS
MAX_TILES = (TOKENS + E * (SLOTS - 1)) // SLOTS
PER_EXPERT = -(-TOKENS // SLOTS)


def mixture_phase(nc, ctx, tag, w1_dram, b1_dram, w2_dram, b2_dram, gated, a, taken, sorted_x, y_dram):
    def sb(name, shape, dt=F32):
        return ctx.enter_context(nc.sbuf_tensor(tag + name, shape, dt))

    bank = [ctx.enter_context(nc.psum_tensor(f"{tag}bank{i}", [128, 512], F32)) for i in range(8)]
    WIDE = 2 * HID if gated else HID
    FB = HID // 128
    NT = MAX_TILES
    PAIRS = (NT - 1) // 2
    assert NT % 2 == 1
    w1 = sb("w1", [128, 2, DC, WIDE])
    w2 = sb("w2", [128, 2, FB, D])
    b1 = sb("b1", [128, 2, WIDE // 128])
    b2 = sb("b2", [1, 2, D])
    ones = sb("ones", [1, 128])
    ident = sb("ident", [128, 128])
    zero = sb("zero", [128, 2, D + 1])
    xr = sb("xr", [128, 2, 2, D + 1])
    to_row = sb("to_row", [128, 2, 2], I32)
    carrier = sb("carrier", [1, 1])
    xT = sb("xT", [128, 2, DC, SLOTS])
    sig = sb("sig", [128, 2, SLOTS])
    hid = sb("hid", [128, FB, SLOTS])
    yo = sb("yo", [128, 2, 2, D])
    region = sb("region", [1, E])
    full = sb("full", [1, E, PER_EXPERT])
    upto = sb("upto", [1, E, E])
    number = sb("number", [1, NT + 1, E])
    t_e = sb("t_e", [1, 6, E])
    t_ek = sb("t_ek", [1, E, PER_EXPERT])
    t_ee = sb("t_ee", [1, E, E])
    t_te = sb("t_te", [1, 2, NT + 1, E])
    t_t = sb("t_t", [1, 6, NT + 1])
    table = sb("table", [1, 2, NT + 1], I32)
    tails = sb("tails", [1, E], I32)
    s = {n: nc.alloc_semaphore(tag + n) for n in """consts weights0 weights1 rows0 rows1 zeroed
        chain table_ready xt_full xt_ready up_full sig_done hid_ready y_full y_ready sent carried to_row_ready loads""".split()}
    loaded, rows_in = [s["weights0"], s["weights1"]], [s["rows0"], s["rows1"]]
    block = ctx.enter_context(nc.Block())

    @block.sync
    def _(sync):
        open_counts(sync, [x for n, x in s.items() if n != "sent"])
        for t, n in ((region, "region"), (full, "full"), (upto, "upto"), (number, "number"), (ident, "ident")):
            sync.dma_start(t[tuple(slice(None) for _ in t.shape)], a[n]).then_inc(s["loads"], 16)
        sync.wait_ge(s["sent"], 16)
        sync.dma_start(sorted_x[EMPTY:EMPTY + SLOTS, :].rearrange("(h p) d -> p h d", p=128), zero[:, :, :])\
            .then_inc(s["zeroed"], 16)

        def load_weights(n, b):
            e = sync.value_load(table[0:1, 0:1, bass.ds(n, 1)].rearrange("p a b -> p (a b)"), min_val=0, max_val=E - 1)
            e = bass.ds(e, 1)
            sync.dma_start(w1[:, b], w1_dram[e].rearrange("a p c n -> p (a c) n")).then_inc(loaded[b], 16)
            sync.dma_start(b1[:, b], b1_dram[e].rearrange("a p n -> p (a n)")).then_inc(loaded[b], 16)
            sync.dma_start(w2[:, b], w2_dram[e].rearrange("a p c n -> p (a c) n")).then_inc(loaded[b], 16)
            sync.dma_start(b2[:, b], b2_dram[e]).then_inc(loaded[b], 16)

        def rows_of(n):
            r = sync.value_load(table[0:1, 1:2, bass.ds(n, 1)].rearrange("p a b -> p (a b)"), min_val=0, max_val=EMPTY)
            return bass.ds(r, SLOTS)

        def load_rows(n, b):
            sync.dma_start(xr[:, b], sorted_x[rows_of(n), :].rearrange("(h p) d -> p h d", p=128))\
                .then_inc(rows_in[b], 16)

        sync.wait_ge(s["table_ready"], OPEN + 3)
        for e in range(E):
            r = sync.value_load(tails[0:1, e:e + 1], min_val=e * REGION, max_val=e * REGION + TOKENS)
            sync.dma_start(sorted_x[bass.ds(r, SLOTS), :].rearrange("(h p) d -> p h d", p=128), zero[:, :, :])\
                .then_inc(s["zeroed"], 16)
        load_weights(0, 0)
        sync.wait_ge(s["zeroed"], OPEN + 16 * (E + 1))
        load_rows(0, 0)
        load_rows(1, 1)
        load_weights(1, 1)
        with sync.Fori(0, PAIRS) as pair:
            for b in range(2):
                n = 2 * pair + b
                sync.wait_ge(s["xt_full"], OPEN + n + 1)
                sync.wait_ge(s["to_row_ready"], OPEN + n + 1)
                load_rows(n + 2, b)
                sync.wait_ge(s["y_full"], OPEN + n + 1)
                load_weights(n + 2, b)
        sync.wait_ge(rows_in[1], OPEN + 16 * (PAIRS + 1))
        sync.wait_ge(loaded[1], OPEN + 64 * (PAIRS + 1))

    @block.gpsimd
    def _(pool):
        pool.memset(ones[:, :], 1.0).then_inc(s["consts"], 1)

        def send_rows(n, b, nb):
            pool.wait_ge(s["y_ready"], OPEN + n + 1)
            pool.tensor_tensor(carrier[:, :], ones[:, 0:1], ones[:, 0:1], ALU.mult).then_inc(s["carried"], 1)
            for half in range(2):
                pool.indirect_dma_start(y_dram, bass.IndirectOffsetOnAxis(to_row[:, b, half:half + 1], 0),
                                        yo[:, b, half, :], None).then_inc(s["sent"], 16)

        pool.dma_start(zero[:, :, :], a["zero_rows"]).then_inc(s["sent"], 16)
        with pool.Fori(0, PAIRS) as pair:
            for b in range(2):
                send_rows(2 * pair + b, b, pair)
        send_rows(NT - 1, 0, PAIRS)
        pool.wait_ge(s["sent"], 32 * NT + 16)

    @block.tensor
    def _(pe):
        pe.wait_ge(s["consts"], OPEN + 1)
        pe.wait_ge(s["loads"], OPEN + 80)

        def turn(n, b, nb):
            pe.wait_ge(rows_in[b], OPEN + 16 * (nb + 1))
            for c in range(DC):
                for h in range(2):
                    ins = pe.transpose(bank[7][:, c * SLOTS + h * 128:c * SLOTS + (h + 1) * 128],
                                       xr[:, b, h, c * 128:(c + 1) * 128], ident[:, :])
            ins.then_inc(s["xt_full"], 1)

        def tile(n, b, nb, last=False):
            pe.wait_ge(loaded[b], OPEN + (nb + 1) * 64)
            pe.wait_ge(s["xt_ready"], OPEN + n + 1)
            for f in range(FB):
                pe.wait_ge(s["hid_ready"], OPEN + n * FB + max(f - 2, 0))
                for up in range(2 if gated else 1):
                    for c in range(DC):
                        col = up * HID + f * 128
                        ins = pe.matmul(bank[(f % 3) * 2 + up][:, 0:SLOTS], w1[:, b, c, col:col + 128], xT[:, b, c, :],
                                        start=c == 0, stop=c == DC - 1)
                ins.then_inc(s["up_full"], 1)
            if not last:
                turn(n + 1, 1 - b, nb + b)
            pe.wait_ge(s["hid_ready"], OPEN + n * FB + FB)
            pe.wait_ge(s["y_ready"], OPEN + n)
            for half in range(2):
                y = bank[6][:, half * D:(half + 1) * D]
                for f in range(FB):
                    pe.matmul(y, hid[:, f, half * 128:(half + 1) * 128], w2[:, b, f, :], start=f == 0, stop=False)
                ins = pe.matmul(y, ones[:, :], b2[:, b, :], start=False, stop=True)
            ins.then_inc(s["y_full"], 1)

        turn(0, 0, 0)
        with pe.Fori(0, PAIRS) as pair:
            for b in range(2):
                tile(2 * pair + b, b, pair)
        tile(NT - 1, 0, PAIRS, last=True)

    @block.scalar
    def _(act):
        def turned(n, b):
            act.wait_ge(s["xt_full"], OPEN + n + 1)
            act.activation(xT[:, b], bank[7][:, :].rearrange("p (c n) -> p c n", c=DC), ACT.Copy)\
                .then_inc(s["xt_ready"], 1)

        def tile(n, b, nb, last=False):
            act.wait_ge(loaded[b], OPEN + (nb + 1) * 64)
            if not gated:
                act.wait_ge(s["y_full"], OPEN + n)
            for f in range(FB):
                act.wait_ge(s["up_full"], OPEN + n * FB + f + 1)
                if gated:
                    act.wait_ge(s["hid_ready"], OPEN + n * FB + max(f - 1, 0))
                    act.activation(sig[:, f % 2, :], bank[(f % 3) * 2 + 1][:, 0:SLOTS], ACT.Sigmoid,
                                   bias=b1[:, b, FB + f:FB + f + 1]).then_inc(s["sig_done"], 1)
                else:
                    act.activation(hid[:, f, :], bank[(f % 3) * 2][:, 0:SLOTS], ACT.Relu,
                                   bias=b1[:, b, f:f + 1]).then_inc(s["hid_ready"], 1)
            if not last:
                turned(n + 1, 1 - b)

        turned(0, 0)
        with act.Fori(0, PAIRS) as pair:
            for b in range(2):
                tile(2 * pair + b, b, pair)
        tile(NT - 1, 0, PAIRS, last=True)

    @block.vector
    def _(dve):
        ch = Chain(dve, s["chain"], 0, 0)
        TT, RED = dve.tensor_tensor, dve.tensor_reduce
        dve.wait_ge(s["loads"], OPEN + 80)
        cnt, nt, cum = t_e[:, 0], t_e[:, 1], t_e[:, 2]
        ch.link(TT(cnt, taken[0:1, :], region[:, :], ALU.subtract))
        ch.wait()
        ch.link(TT(t_ek[:, :, :], bc(cnt, 2, PER_EXPERT), full[:, :, :], ALU.is_gt))
        ch.wait()
        ch.link(RED(nt, t_ek[:, :, :], AX.X, ALU.add))
        ch.wait()
        ch.link(TT(t_ee[:, :, :], bc(nt, 1, E), upto[:, :, :], ALU.mult))
        ch.wait()
        ch.link(RED(cum, t_ee[:, :, :], AX.X, ALU.add))
        ch.wait()
        ch.link(TT(t_te[:, 0], number[:, :, :], bc(cum, 1, NT + 1), ALU.is_ge))
        ch.wait()
        ch.link(RED(t_t[:, 0], t_te[:, 0], AX.X, ALU.add))
        ch.link(TT(t_te[:, 1], t_te[:, 0], bc(nt, 1, NT + 1), ALU.mult))
        ch.wait()
        ch.link(RED(t_t[:, 1], t_te[:, 1], AX.X, ALU.add))
        ch.wait()
        ch.link(TT(t_t[:, 2], number[:, :, 0], t_t[:, 1], ALU.subtract))
        ch.link(dve.tensor_scalar(t_t[:, 3], t_t[:, 0], float(E), float(SLOTS), ALU.is_lt, ALU.mult))
        ch.wait()
        ch.link(TT(t_t[:, 4], t_t[:, 2], t_t[:, 3], ALU.mult))
        ch.wait()
        dve.scalar_tensor_tensor(table[:, 1], t_t[:, 0], float(REGION), t_t[:, 4], ALU.mult, ALU.add)\
            .then_inc(s["table_ready"], 1)
        dve.tensor_scalar(table[:, 0], t_t[:, 0], float(E - 1), None, ALU.min).then_inc(s["table_ready"], 1)
        dve.tensor_copy(tails[:, :], taken[0:1, :]).then_inc(s["table_ready"], 1)

        def tile(n, b, nb):
            if gated:
                dve.wait_ge(loaded[b], OPEN + (nb + 1) * 64)
                dve.wait_ge(s["y_full"], OPEN + n)
                for f in range(FB):
                    dve.wait_ge(s["sig_done"], OPEN + n * FB + f + 1)
                    dve.scalar_tensor_tensor(hid[:, f, :], bank[(f % 3) * 2][:, 0:SLOTS], b1[:, b, f:f + 1],
                                             sig[:, f % 2, :], ALU.add, ALU.mult).then_inc(s["hid_ready"], 1)
            dve.wait_ge(s["y_full"], OPEN + n + 1)
            dve.wait_ge(s["carried"], OPEN + n)
            dve.wait_ge(s["sent"], 32 * n + 16)
            dve.wait_ge(rows_in[b], OPEN + 16 * (nb + 1))
            dve.tensor_copy(to_row[:, b, :], xr[:, b, :, D]).then_inc(s["to_row_ready"], 1)
            dve.tensor_copy(yo[:, b], bank[6][:, :].rearrange("p (h d) -> p h d", h=2)).then_inc(s["y_ready"], 1)

        with dve.Fori(0, PAIRS) as pair:
            for b in range(2):
                tile(2 * pair + b, b, pair)
        tile(NT - 1, 0, PAIRS)


def attention_phase(nc, ctx, a, h_dram, y_dram, h_all, sorted_x, taken, prob):
    def sb(name, shape, dt=F32):
        return ctx.enter_context(nc.sbuf_tensor("a_" + name, shape, dt))

    bank = [ctx.enter_context(nc.psum_tensor(f"a_bank{i}", [128, 512], F32)) for i in range(8)]
    AC = AH // 4
    wq = sb("wq", [128, DC, AC * 128])
    wk = sb("wk", [128, DC, AC * 128])
    wv = sb("wv", [128, DC, D])
    wo = sb("wo", [128, DC, D])
    wg = sb("wg", [128, DC, E])
    bq = sb("bq", [128, AC])
    bk = sb("bk", [128, AC])
    bv = sb("bv", [ROWS, D])
    bo = sb("bo", [ROWS, D])
    bg = sb("bg", [ROWS, E])
    ident = sb("ident", [128, 128])
    mask = sb("mask", [ROWS, ROWS])
    countdown = sb("countdown", [ROWS, E])
    nhalf = sb("nhalf", [ROWS, 1])
    st = sb("st", [ROWS, 6])
    mv = sb("mv", [ROWS, 2])
    ve = sb("ve", [ROWS, 1])
    rstd = sb("rstd", [ROWS, 1])
    hcur = sb("hcur", [ROWS, D])
    hb = sb("hb", [ROWS, D])
    xn = sb("xn", [ROWS, D])
    xnT = sb("xnT", [128, DC, ROWS])
    qT = sb("qT", [128, AC, ROWS])
    kT = sb("kT", [128, AC, ROWS])
    v = sb("v", [ROWS, D])
    S = sb("S", [ROWS, AC, 4, ROWS])
    mx = sb("mx", [ROWS, AH])
    sums = sb("sums", [ROWS, AH])
    rinv = sb("rinv", [ROWS, AH])
    PT = sb("PT", [ROWS, AC, 4, ROWS])
    yv = sb("yv", [ROWS, D])
    yT = sb("yT", [128, DC, ROWS])
    lg = sb("lg", [ROWS, E])
    lm = sb("lm", [ROWS, E])
    ex = sb("ex", [ROWS, E])
    gx = sb("gx", [ROWS, 4])
    hot = sb("hot", [ROWS, E])
    place = sb("place", [ROWS, E])
    slotf = sb("slotf", [ROWS, 1])
    slot = sb("slot", [ROWS, 1], I32)
    yg = sb("yg", [ROWS, D])
    h_in = sb("h_in", [ROWS, D])
    xrow = sb("xrow", [ROWS, D + 1])
    row_number = sb("row_number", [ROWS, GROUPS])
    carrier = sb("carrier", [1, 1])
    before = sb("before", [ROWS, ROWS])
    all_ones = sb("all_ones", [ROWS, ROWS])

    s = {n: nc.alloc_semaphore("a_" + n) for n in """weights consts scaled
        dve_chain var_ready rstd_ready xt_full xt_ready q_full k_full v_full q_ready k_ready v_ready
        hb_ready s_full masked max_ready shifted exp_done pt_full pt_ready y_full y_ready yt_full yt_ready
        wo_full x2t_full x2t_ready lg_full lg_shift lg_exp hot_ready route_ready
        h_loaded merged rank_full slot_ready numbered scattered""".split()}
    block = ctx.enter_context(nc.Block())
    @block.sync
    def _(sp):
        open_counts(sp, [x for n, x in s.items() if n != "scattered"])
        for t, n in ((ident, "ident"), (wq, "awq"), (wk, "awk"), (wv, "awv"), (wo, "awo"), (wg, "awg"), (bq, "abq"),
                     (bk, "abk"), (mask, "amask"), (countdown, "countdown"), (before, "before"),
                     (row_number, "row_number")):
            sp.dma_start(t[tuple(slice(None) for _ in t.shape)], a[n]).then_inc(s["weights"], 16)
        sp.dma_start(bv[:, :], a["abv"].partition_broadcast(ROWS)).then_inc(s["weights"], 16)
        sp.dma_start(bo[:, :], a["abo"].partition_broadcast(ROWS)).then_inc(s["weights"], 16)
        sp.dma_start(bg[:, :], a["abg"].partition_broadcast(ROWS)).then_inc(s["weights"], 16)
        with sp.Fori(0, GROUPS) as gi:
            sp.wait_ge(s["merged"], OPEN + gi)
            sp.dma_start(h_in[:, :], h_dram[:, bass.ds(gi, 1), :].rearrange("p a d -> p (a d)"))\
                .then_inc(s["h_loaded"], 16)
            sp.dma_start(yg[:, :], y_dram[bass.ds(gi * ROWS, ROWS), :]).then_inc(s["h_loaded"], 16)
    LOADED = 16 * 15

    @block.gpsimd
    def _(pool):
        pool.memset(nhalf[:, :], -0.5).then_inc(s["consts"], 1)
        pool.wait_ge(s["weights"], OPEN + LOADED)
        pool.memset(all_ones[:, :], 1.0).then_inc(s["consts"], 1)
        pool.wait_ge(s["consts"], OPEN + 2)
        pool.dma_start(taken[:, :], a["regions"]).then_inc(s["scattered"], 16)
        with pool.Fori(0, GROUPS) as gi:
            pool.wait_ge(s["var_ready"], OPEN + gi * 2 + 1)
            pool.tensor_tensor(rstd[:, :], ve[:, :], nhalf[:, :], ALU.pow).then_inc(s["rstd_ready"], 1)
            pool.tensor_tensor(hb[:, :], hcur[:, :], bo[:, :], ALU.add).then_inc(s["hb_ready"], 1)
            for c in range(AC):
                pool.wait_ge(s["max_ready"], OPEN + gi * AC + c + 1)
                pool.tensor_tensor(S[:, c], S[:, c], bc(mx[:, 4 * c:4 * c + 4], 2, ROWS), ALU.subtract)\
                    .then_inc(s["shifted"], 1)
            pool.wait_ge(s["var_ready"], OPEN + gi * 2 + 2)
            pool.tensor_tensor(rstd[:, :], ve[:, :], nhalf[:, :], ALU.pow).then_inc(s["rstd_ready"], 1)
            pool.wait_ge(s["slot_ready"], OPEN + gi + 1)
            pool.tensor_tensor(carrier[:, :], nhalf[0:1, 0:1], nhalf[0:1, 0:1], ALU.mult)
            pool.indirect_dma_start(sorted_x, bass.IndirectOffsetOnAxis(slot[:, 0:1], 0), xrow[:, :], None)\
                .then_inc(s["scattered"], 16)
        pool.wait_ge(s["scattered"], 16 * GROUPS + 16)

    @block.tensor
    def _(pe):
        pe.wait_ge(s["weights"], OPEN + LOADED)
        pe.wait_ge(s["scaled"], OPEN + 1)
        with pe.Fori(0, GROUPS) as gi:
            pe.wait_ge(s["dve_chain"], OPEN + gi * A_LINKS + A_XN)
            for c in range(DC):
                ins = pe.transpose(bank[0][:, c * ROWS:(c + 1) * ROWS], xn[:, c * 128:(c + 1) * 128],
                                   ident[0:ROWS, 0:ROWS])
            ins.then_inc(s["xt_full"], 1)
            pe.wait_ge(s["xt_ready"], OPEN + gi + 1)
            for w, b, full in ((wq, 1, "q_full"), (wk, 2, "k_full")):
                for j in range(AC):
                    for c in range(DC):
                        ins = pe.matmul(bank[b][:, j * ROWS:(j + 1) * ROWS], w[:, c, j * 128:(j + 1) * 128],
                                        xnT[:, c, :], start=c == 0, stop=c == DC - 1)
                ins.then_inc(s[full], 1)
            for c in range(DC):
                ins = pe.matmul(bank[3][0:ROWS, 0:D], xnT[:, c, :], wv[:, c, :], start=c == 0, stop=c == DC - 1)
            ins.then_inc(s["v_full"], 1)
            pe.wait_ge(s["q_ready"], OPEN + gi + 1)
            pe.wait_ge(s["k_ready"], OPEN + gi + 1)
            for c in range(AC):
                for j in range(4):
                    ins = pe.matmul(bank[4 + j][0:ROWS, c * ROWS:(c + 1) * ROWS], qT[32 * j:32 * j + 32, c, :],
                                    kT[32 * j:32 * j + 32, c, :], start=True, stop=True)
                    if c == AC - 1:
                        ins.then_inc(s["s_full"], 1)
            for c in range(AC):
                pe.wait_ge(s["exp_done"], OPEN + gi * AC + c + 1)
                for j in range(4):
                    ins = pe.transpose(bank[4 + c][0:ROWS, j * ROWS:(j + 1) * ROWS], S[:, c, j, :],
                                       ident[0:ROWS, 0:ROWS])
                ins.then_inc(s["pt_full"], 1)
            pe.wait_ge(s["v_ready"], OPEN + gi + 1)
            for c in range(AC):
                pe.wait_ge(s["pt_ready"], OPEN + gi * AC + c + 1)
                for j in range(4):
                    hh = 4 * j + c
                    ins = pe.matmul(bank[1][0:ROWS, hh * AD:(hh + 1) * AD], PT[:, c, j, :], v[:, hh * AD:(hh + 1) * AD],
                                    start=True, stop=True)
            ins.then_inc(s["y_full"], 1)
            pe.wait_ge(s["y_ready"], OPEN + gi + 1)
            for c in range(DC):
                ins = pe.transpose(bank[2][:, c * ROWS:(c + 1) * ROWS], yv[:, c * 128:(c + 1) * 128],
                                   ident[0:ROWS, 0:ROWS])
            ins.then_inc(s["yt_full"], 1)
            pe.wait_ge(s["yt_ready"], OPEN + gi + 1)
            for c in range(DC):
                ins = pe.matmul(bank[3][0:ROWS, 0:D], yT[:, c, :], wo[:, c, :], start=c == 0, stop=c == DC - 1)
            ins.then_inc(s["wo_full"], 1)
            pe.wait_ge(s["dve_chain"], OPEN + gi * A_LINKS + A_XN2)
            for c in range(DC):
                ins = pe.transpose(bank[0][:, c * ROWS:(c + 1) * ROWS], xrow[:, c * 128:(c + 1) * 128],
                                   ident[0:ROWS, 0:ROWS])
            ins.then_inc(s["x2t_full"], 1)
            pe.wait_ge(s["x2t_ready"], OPEN + gi + 1)
            for c in range(DC):
                ins = pe.matmul(bank[1][0:ROWS, 256:256 + E], xnT[:, c, :], wg[:, c, :], start=c == 0, stop=c == DC - 1)
            ins.then_inc(s["lg_full"], 1)
            pe.wait_ge(s["hot_ready"], OPEN + gi + 1)
            pe.matmul(bank[2][0:ROWS, 256:256 + E], before[:, :], hot[:, :], start=True, stop=True)
            pe.matmul(bank[2][0:ROWS, 264:264 + E], all_ones[:, :], hot[:, :], start=True, stop=True)\
                .then_inc(s["rank_full"], 1)

    @block.scalar
    def _(act):
        act.wait_ge(s["weights"], OPEN + LOADED)
        with act.Fori(0, GROUPS) as gi:
            act.wait_ge(s["xt_full"], OPEN + gi + 1)
            act.activation(xnT[:, :, :], bank[0][:, 0:DC * ROWS], ACT.Copy).then_inc(s["xt_ready"], 1)
            act.wait_ge(s["k_full"], OPEN + gi + 1)
            for j in range(AC):
                ins = act.activation(kT[:, j, :], bank[2][:, j * ROWS:(j + 1) * ROWS], ACT.Identity,
                                     bias=bk[:, j:j + 1])
            ins.then_inc(s["k_ready"], 1)
            for c in range(AC):
                act.wait_ge(s["shifted"], OPEN + gi * AC + c + 1)
                act.activation(S[:, c], S[:, c], ACT.Exp).then_inc(s["exp_done"], 1)
            for c in range(AC):
                act.wait_ge(s["pt_full"], OPEN + gi * AC + c + 1)
                act.activation(PT[:, c], bank[4 + c][0:ROWS, 0:4 * ROWS], ACT.Copy).then_inc(s["pt_ready"], 1)
            act.wait_ge(s["yt_full"], OPEN + gi + 1)
            act.activation(yT[:, :, :], bank[2][:, 0:DC * ROWS], ACT.Copy).then_inc(s["yt_ready"], 1)
            act.wait_ge(s["x2t_full"], OPEN + gi + 1)
            act.activation(xnT[:, :, :], bank[0][:, 0:DC * ROWS], ACT.Copy).then_inc(s["x2t_ready"], 1)
            act.wait_ge(s["lg_shift"], OPEN + gi + 1)
            act.activation(ex[:, :], lm[:, :], ACT.Exp).then_inc(s["lg_exp"], 1)

    @block.vector
    def _(dve):
        dve.wait_ge(s["weights"], OPEN + LOADED)
        dve.tensor_scalar(bq[:, :], bq[:, :], AD ** -0.5, None, ALU.mult).then_inc(s["scaled"], 1)
        dve.wait_ge(s["scaled"], OPEN + 1)
        with dve.Fori(0, GROUPS) as gi:
            ch = Chain(dve, s["dve_chain"], A_LINKS, gi)
            dve.wait_ge(s["hb_ready"], OPEN + gi)
            dve.wait_ge(s["h_loaded"], OPEN + 32 * gi + 32)
            dve.tensor_tensor(hcur[:, :], h_in[:, :], yg[:, :], ALU.add).then_inc(s["merged"], 1)
            dve.wait_ge(s["merged"], OPEN + gi + 1)
            layer_norm(dve, ch, st[:, :], mv[:, :], ve[:, :], rstd[:, :], xn[:, :], hcur[:, :],
                       s["var_ready"], s["rstd_ready"], gi, 1, 2)
            assert ch.n == A_XN, ch.n
            dve.wait_ge(s["q_full"], OPEN + gi + 1)
            for j in range(AC):
                ins = dve.tensor_scalar(qT[:, j, :], bank[1][:, j * ROWS:(j + 1) * ROWS], AD ** -0.5, bq[:, j:j + 1],
                                        ALU.mult, ALU.add)
            ins.then_inc(s["q_ready"], 1)
            dve.wait_ge(s["v_full"], OPEN + gi + 1)
            dve.tensor_tensor(v[:, :], bank[3][0:ROWS, 0:D], bv[:, :], ALU.add).then_inc(s["v_ready"], 1)
            for c in range(AC):
                dve.wait_ge(s["s_full"], OPEN + gi * AC + c + 1)
                dve.tensor_tensor(S[:, c], bank[4 + c][0:ROWS, 0:4 * ROWS].rearrange("p (h k) -> p h k", h=4),
                                  bc(mask[:, :], 1, 4), ALU.add).then_inc(s["masked"], 1)
                dve.wait_ge(s["masked"], OPEN + gi * AC + c + 1)
                dve.tensor_reduce(mx[:, 4 * c:4 * c + 4], S[:, c], AX.X, ALU.max).then_inc(s["max_ready"], 1)
            for c in range(AC):
                dve.wait_ge(s["exp_done"], OPEN + gi * AC + c + 1)
                ch.link(dve.tensor_reduce(sums[:, 4 * c:4 * c + 4], S[:, c], AX.X, ALU.add))
            ch.wait()
            ch.link(dve.reciprocal(rinv[:, :], sums[:, :]))
            ch.wait()
            dve.wait_ge(s["y_full"], OPEN + gi + 1)
            dve.tensor_tensor(yv[:, :].rearrange("p (c j d) -> p c j d", c=AC, j=4),
                              bank[1][0:ROWS, 0:D].rearrange("p (c j d) -> p c j d", c=AC, j=4),
                              bc(rinv[:, :].rearrange("p (j c) -> p c j", j=4), 3, AD), ALU.mult).then_inc(s["y_ready"], 1)
            dve.wait_ge(s["wo_full"], OPEN + gi + 1)
            dve.wait_ge(s["hb_ready"], OPEN + gi + 1)
            ch.link(dve.tensor_tensor(hcur[:, :], bank[3][0:ROWS, 0:D], hb[:, :], ALU.add))
            ch.wait()
            ch.link(dve.tensor_scalar(h_all[:, bass.ds(gi, 1), :].rearrange("p a d -> p (a d)"), hcur[:, :], 1.0, None,
                                      ALU.mult))
            dve.wait_ge(s["scattered"], 16 * gi + 16)
            layer_norm(dve, ch, st[:, :], mv[:, :], ve[:, :], rstd[:, :], xrow[:, 0:D], hcur[:, :],
                       s["var_ready"], s["rstd_ready"], gi, 2, 2)
            dve.tensor_scalar(xrow[:, D:D + 1], row_number[:, bass.ds(gi, 1)], 1.0, None, ALU.mult)\
                .then_inc(s["numbered"], 1)
            assert ch.n == A_XN2, ch.n
            dve.wait_ge(s["lg_full"], OPEN + gi + 1)
            ch.link(dve.tensor_tensor(lg[:, :], bank[1][0:ROWS, 256:256 + E], bg[:, :], ALU.add))
            ch.wait()
            ch.link(dve.tensor_reduce(gx[:, 2:3], lg[:, :], AX.X, ALU.max))
            ch.wait()
            dve.tensor_scalar(lm[:, :], lg[:, :], gx[:, 2:3], None, ALU.subtract).then_inc(s["lg_shift"], 1)
            choose(dve, ch, lg[:, :], gx, countdown[:, :], hot[:, :], s["hot_ready"])
            dve.wait_ge(s["lg_exp"], OPEN + gi + 1)
            ch.link(dve.tensor_reduce(gx[:, 2:3], ex[:, :], AX.X, ALU.add))
            ch.wait()
            ch.link(dve.reciprocal(gx[:, 3:4], gx[:, 2:3]))
            ch.wait()
            ch.link(dve.tensor_copy(prob[:, bass.ds(gi, 1)], gx[:, 3:4]))
            place_rows(dve, ch, bank[2][0:ROWS, 256:256 + E], bank[2][0:ROWS, 264:264 + E], hot, place, slotf, slot,
                       taken, gi, s["rank_full"], s["slot_ready"], s["scattered"])
            assert ch.n == A_LINKS, ch.n


def place_rows(dve, ch, ranks, totals, hot, place, slotf, slot, taken, gi, rank_full, slot_ready, scattered):
    dve.wait_ge(scattered, 16 * gi + 16)
    dve.wait_ge(rank_full, OPEN + gi + 1)
    ch.link(dve.tensor_tensor(place[:, :], ranks, taken[:, :], ALU.add))
    ch.link(dve.tensor_tensor(taken[:, :], totals, taken[:, :], ALU.add))
    ch.wait()
    ch.link(dve.tensor_tensor(place[:, :], place[:, :], hot[:, :], ALU.mult))
    ch.wait()
    ch.link(dve.tensor_reduce(slotf[:, :], place[:, :], AX.X, ALU.add))
    ch.wait()
    dve.tensor_copy(slot[:, :], slotf[:, :]).then_inc(slot_ready, 1)


def output_phase(nc, ctx, h_all, y_dram, prob, out):
    DEEP = 3
    TURNS = (GROUPS - 1) // DEEP
    assert (GROUPS - 1) % DEEP == 0
    y = ctx.enter_context(nc.sbuf_tensor("o_y", [ROWS, DEEP, D], F32))
    share = ctx.enter_context(nc.sbuf_tensor("o_share", [ROWS, DEEP], F32))
    res = ctx.enter_context(nc.sbuf_tensor("o_res", [ROWS, DEEP, D], F32))
    s = {n: nc.alloc_semaphore("o_" + n) for n in
         "loaded0 loaded1 loaded2 added0 added1 added2 stored0 stored1 stored2 share_ready".split()}
    block = ctx.enter_context(nc.Block())

    @block.sync
    def _(sync):
        open_counts(sync, s.values())

        def load(g, b):
            sync.dma_start(y[:, b, :], y_dram[bass.ds(g * ROWS, ROWS), :]).then_inc(s[f"loaded{b}"], 16)

        for b in range(DEEP):
            load(b, b)
        with sync.Fori(0, TURNS - 1) as t:
            for b in range(DEEP):
                sync.wait_ge(s[f"added{b}"], OPEN + t + 1)
                sync.dma_start(out[bass.ds((t * DEEP + b) * ROWS, ROWS), :], res[:, b, :]).then_inc(s[f"stored{b}"], 16)
                load((t + 1) * DEEP + b, b)
        for b in range(DEEP):
            sync.wait_ge(s[f"added{b}"], OPEN + TURNS)
            sync.dma_start(out[((TURNS - 1) * DEEP + b) * ROWS:((TURNS - 1) * DEEP + b + 1) * ROWS, :], res[:, b, :])\
                .then_inc(s[f"stored{b}"], 16)
            if b == 0:
                load(GROUPS - 1, 0)
        sync.wait_ge(s["added0"], OPEN + TURNS + 1)
        sync.dma_start(out[(GROUPS - 1) * ROWS:(GROUPS - 1) * ROWS + NEW_ROWS_OF_LAST, :],
                       res[ROWS - NEW_ROWS_OF_LAST:ROWS, 0, :]).then_inc(s["stored0"], 16)
        sync.wait_ge(s["stored0"], OPEN + 16 * TURNS + 16)
        sync.wait_ge(s["stored1"], OPEN + 16 * TURNS)
        sync.wait_ge(s["stored2"], OPEN + 16 * TURNS)

    @block.vector
    def _(dve):
        def add(g, b, t):
            dve.wait_ge(s[f"loaded{b}"], OPEN + 16 * t + 16)
            dve.wait_ge(s[f"stored{b}"], OPEN + 16 * t)
            dve.scalar_tensor_tensor(res[:, b, :], y[:, b, :], share[:, b:b + 1],
                                     h_all[:, bass.ds(g, 1), :].rearrange("p a d -> p (a d)"), ALU.mult, ALU.add)\
                .then_inc(s[f"added{b}"], 1)

        with dve.Fori(0, TURNS) as t:
            for b in range(DEEP):
                dve.wait_ge(s[f"added{b}"], OPEN + t)
                dve.tensor_scalar(share[:, b:b + 1], prob[:, bass.ds(t * DEEP + b, 1)], 1.0, None, ALU.mult)\
                    .then_inc(s["share_ready"], 1)
            dve.wait_ge(s["share_ready"], OPEN + (t + 1) * DEEP)
            for b in range(DEEP):
                add(t * DEEP + b, b, t)
        dve.wait_ge(s["added0"], OPEN + TURNS)
        dve.tensor_copy(share[:, 0:1], prob[:, GROUPS - 1:GROUPS]).then_inc(s["share_ready"], 1)
        dve.wait_ge(s["share_ready"], OPEN + GROUPS)
        add(GROUPS - 1, 0, TURNS)


def host_layouts_rest(i):
    f = np.float32

    def rows(w):
        w = np.asarray(w)
        return np.ascontiguousarray(w.reshape(-1, 128, w.shape[1]).transpose(1, 0, 2))

    def pad_heads(w):
        w = np.asarray(w).reshape(-1, AH, AD)
        o = np.zeros((w.shape[0], AH, 32), f)
        o[:, :, :AD] = w
        return o.reshape(-1, AH * 32)

    def per_expert(w):
        w = np.asarray(w)
        return np.ascontiguousarray(w.reshape(E, -1, 128, w.shape[2]).transpose(0, 2, 1, 3))

    def bias(b):
        b = np.asarray(b)
        return np.ascontiguousarray(b.reshape(E, -1, 128).transpose(0, 2, 1))

    r = np.arange(ROWS)
    ok = (r[:, None] // T == r[None] // T) & (r[None] <= r[:, None])
    return dict(
        awq=rows(pad_heads(i["L1_attn_Wq"])), awk=rows(pad_heads(i["L1_attn_Wk"])), awv=rows(i["L1_attn_Wv"]),
        awo=rows(i["L1_attn_Wo"]), awg=rows(i["L1_ffn_w_gate"]),
        abq=pad_heads(np.asarray(i["L1_attn_bq"])[None]).reshape(-1, 128).T,
        abk=pad_heads(np.asarray(i["L1_attn_bk"])[None]).reshape(-1, 128).T,
        abv=np.asarray(i["L1_attn_bv"]), abo=np.asarray(i["L1_attn_bo"]), abg=np.asarray(i["L1_ffn_b_gate"]),
        amask=np.where(ok, 0.0, -1e30).astype(f),
        m0w1=per_expert(i["L0_ffn_w1"]), m0b1=bias(i["L0_ffn_b1"]), m0w2=per_expert(i["L0_ffn_w2"]),
        m0b2=np.asarray(i["L0_ffn_b2"]),
        m1w1=per_expert(i["L1_ffn_W1"]), m1b1=bias(i["L1_ffn_b1"]), m1w2=per_expert(i["L1_ffn_W2"]),
        m1b2=np.asarray(i["L1_ffn_b2"]),
    )


def host_layouts_mixtures():
    f = np.float32
    e = np.arange(E)
    return dict(
        region=(e * REGION).astype(f)[None],
        full=np.broadcast_to(np.arange(PER_EXPERT) * SLOTS, (1, E, PER_EXPERT)).astype(f),
        upto=(e[None] <= e[:, None]).astype(f)[None],
        number=np.broadcast_to(np.arange(MAX_TILES + 1)[:, None], (1, MAX_TILES + 1, E)).astype(f),
        zero_rows=np.concatenate([np.zeros((SLOTS, D), f), np.arange(TOKENS, TOKENS + SLOTS, dtype=f)[:, None]], 1)
        .reshape(2, 128, D + 1).transpose(1, 0, 2),
        row_number=np.arange(TOKENS, dtype=f).reshape(GROUPS, ROWS).T,
        before=(np.arange(ROWS)[:, None] < np.arange(ROWS)[None]).astype(f),
        regions=np.tile((e * REGION).astype(f), (ROWS, 1)),
    )


def build(nc, a, out):
    h_dram = nc.dram_tensor("h_kept", (ROWS, GROUPS, D), F32, kind="Internal").ap()
    sorted_x = nc.dram_tensor("sorted_x", (SORTED_ROWS, D + 1), F32, kind="Internal").ap()
    y_dram = nc.dram_tensor("y_rows", (TOKENS + SLOTS, D), F32, kind="Internal").ap()
    with ExitStack() as kept:
        taken = kept.enter_context(nc.sbuf_tensor("taken", [ROWS, E], F32))
        with nc.cleanup_on_exit(), ExitStack() as ctx:
            delta_phase(nc, ctx, a, h_dram, sorted_x, taken)
        with nc.cleanup_on_exit(), ExitStack() as ctx:
            mixture_phase(nc, ctx, "m0_", a["m0w1"], a["m0b1"], a["m0w2"], a["m0b2"], True, a, taken, sorted_x, y_dram)
        h_all = kept.enter_context(nc.sbuf_tensor("h_all", [ROWS, GROUPS, D], F32))
        prob = kept.enter_context(nc.sbuf_tensor("prob", [ROWS, GROUPS], F32))
        with nc.cleanup_on_exit(), ExitStack() as ctx:
            attention_phase(nc, ctx, a, h_dram, y_dram, h_all, sorted_x, taken, prob)
        with nc.cleanup_on_exit(), ExitStack() as ctx:
            mixture_phase(nc, ctx, "m1_", a["m1w1"], a["m1b1"], a["m1w2"], a["m1b2"], False, a, taken, sorted_x, y_dram)
        with nc.cleanup_on_exit(), ExitStack() as ctx:
            output_phase(nc, ctx, h_all, y_dram, prob, out.rearrange("b t d -> (b t) d"))


def kernel(**inputs):
    import concourse.bacc as bacc
    from concourse.bass_utils import run_bass_kernel_spmd as run

    nc = bacc.Bacc("TRN2", target_bir_lowering=False, num_devices=1)
    arrays, a = {}, {}
    for name, v in {**host_layouts(inputs), **host_layouts_rest(inputs), **host_layouts_mixtures()}.items():
        v = np.ascontiguousarray(v)
        arrays["in_" + name] = v
        a[name] = nc.dram_tensor("in_" + name, v.shape, F32, kind="ExternalInput").ap()
    out = nc.dram_tensor("out", (IMAGES, T, D), F32, kind="ExternalOutput").ap()
    build(nc, a, out)
    return run(nc, [arrays], core_ids=[0]).results[0]["out"]
```

```python
import numpy as np
import concourse.bass as bass
from concourse import mybir
from contextlib import ExitStack

F32 = mybir.dt.float32
I32 = mybir.dt.int32
ALU = mybir.AluOpType
ACT = mybir.ActivationFunctionType
AX = mybir.AxisListType

ROUTE_LINKS = 11
TAIL_LINKS = 10

IMAGES, CHANNELS, SIDE, PATCH = 64, 3, 96, 16
GRID = SIDE // PATCH
PATCHES = GRID * GRID
T = PATCHES + 1
F = CHANNELS * PATCH * PATCH
FC = F // 128
D = 256
DC = D // 128
PER = 3
ROWS = PER * T
GROUPS = -(-IMAGES // PER)
FIRST_OF_LAST = IMAGES - PER
NEW_ROWS_OF_LAST = (IMAGES - PER * (GROUPS - 1)) * T
TOKENS = GROUPS * ROWS

H, HD, NH, TAPS = 8, 128, 3, 4
MICRO = NH * T
QB, KB, VB = H, NH * H, NH * H
CB = QB + KB + VB
CQ = CB // 4
LEVELS = [1, 2, 4, 8, 16, 32, 64]
E = 8
HID = 1024
AH, AD = 16, 16


def bc(ap, axis, n):
    shape = list(ap.shape)
    shape.insert(axis, n)
    return ap.unsqueeze(axis).to_broadcast(shape)


OPEN = 1


def open_counts(eng, sems):
    for x in sems:
        eng.sem_inc(x, OPEN)


class Chain:

    def __init__(self, eng, sem, per_turn, turn):
        self.eng, self.sem, self.per, self.turn, self.n = eng, sem, per_turn, turn, 0

    def link(self, ins):
        ins.then_inc(self.sem, 1)
        self.n += 1

    def wait(self):
        self.eng.wait_ge(self.sem, OPEN + self.turn * self.per + self.n)


def delta_phase(nc, ctx, a, h_dram, sorted_x, taken):
    def sb(name, shape, dt=F32):
        return ctx.enter_context(nc.sbuf_tensor("d_" + name, shape, dt))

    bank = [ctx.enter_context(nc.psum_tensor(f"d_bank{i}", [128, 512], F32)) for i in range(8)]
    L = len(LEVELS)
    HT = 4
    NB = H // HT
    GRAM = MICRO + T
    TRIPLES = [(0, 3), (3, 3), (6, 2)]

    wlin = sb("wlin", [128, FC, D])
    wqkv = sb("wqkv", [128, DC, CB * 128])
    wgate = sb("wgate", [128, DC, H * HD])
    wout = sb("wout", [128, H, D])
    wab = sb("wab", [128, DC, 32])
    wrt = sb("wrt", [128, DC, E])
    taps = sb("taps", [128, CB, TAPS])
    ident = sb("ident", [128, 128])
    addend = sb("addend", [ROWS, D])
    dtb = sb("dtb", [ROWS, H])
    negA = sb("negA", [ROWS, H])
    rmsw = sb("rmsw", [HD, 1])
    rbias = sb("rbias", [ROWS, E])
    countdown = sb("countdown", [ROWS, E])
    phalf = sb("phalf", [ROWS, PER * H])
    nhalf = sb("nhalf", [ROWS, 1])
    ones = sb("ones", [128, 1])
    all_ones = sb("all_ones", [ROWS, ROWS])
    before = sb("before", [ROWS, ROWS])
    m_low = sb("m_low", [MICRO, MICRO])
    m_lvl = sb("m_lvl", [MICRO, L, MICRO])
    s_gt = sb("s_gt", [ROWS, T])
    s_le = sb("s_le", [ROWS, T])
    up_to = sb("up_to", [ROWS, PER, MICRO])
    after = sb("after", [ROWS, PER, MICRO])
    causal = sb("causal", [MICRO, T])
    spread = sb("spread", [ROWS, PER, MICRO])
    sub_step = sb("sub_step", [MICRO, NH])

    xin = sb("xin", [128, FC, ROWS])
    h1 = sb("h1", [ROWS, D])
    st, mv, ve, rstd = sb("st", [ROWS, 6]), sb("mv", [ROWS, 2]), sb("ve", [ROWS, 1]), sb("rstd", [ROWS, 1])
    xn = sb("xn", [ROWS, D])
    xnT = sb("xnT", [128, DC, ROWS])
    blog = sb("blog", [ROWS, NH * H])
    sp = sb("sp", [ROWS, 4, H])
    g = sb("g", [ROWS, H])
    g_gt = sb("g_gt", [ROWS, H, T])
    g_le = sb("g_le", [ROWS, H, T])
    y = sb("y", [128, 3, 4, ROWS])
    sg = sb("sg", [128, 2, 4, ROWS])
    KQ = sb("KQ", [128, PER, H, GRAM])
    V = sb("V", [128, PER, H, MICRO])
    sq = sb("sq", [128, H, ROWS])
    r2 = sb("r2", [MICRO, 4, H])
    bs = sb("bs", [MICRO, PER, NH, H])
    beta = sb("beta", [MICRO, PER, H])
    nbr2 = sb("nbr2", [MICRO, PER, H])
    rr = sb("rr", [MICRO, PER, H])
    br = sb("br", [MICRO, PER, H])
    dj = sb("dj", [MICRO, PER, H, T])
    di = sb("di", [MICRO, PER, H, T])
    dmask2 = sb("dmask2", [MICRO, 2, H, MICRO])
    dmask = [dmask2[:, 0], dmask2[:, 1], sq[0:MICRO]]
    N = sb("N", [MICRO, PER, H, MICRO])
    X = sb("X", [MICRO, NB, HT, MICRO])
    Y = sb("Y", [MICRO, NB, HT, MICRO])
    Z = sb("Z", [MICRO, NB, HT, MICRO])
    C = sb("C", [MICRO, PER, H, HD])
    EE = sb("EE", [MICRO, NB, HT, HD])
    PT = sb("PT", [MICRO, PER, H, ROWS])
    gs = sb("gs", [ROWS, H, HD])
    gsig = sb("gsig", [ROWS, 512])
    r2_kept = sb("r2_kept", [ROWS, H])
    h_kept = sb("h_kept", [ROWS, D])
    h2 = sb("h2", [ROWS, D])
    O = y[0:ROWS, :, :, :].rearrange("p a b c -> p (a b c)")[:, 0:H * HD].rearrange("p (h c) -> p h c", h=H)
    osq = EE[:, :, :, :].rearrange("p a b c -> p (a b) c")
    rms = sb("rms", [ROWS, 4, H])
    OT = sq
    st2, mv2, ve2, rstd2 = sb("st2", [ROWS, 6]), sb("mv2", [ROWS, 2]), sb("ve2", [ROWS, 1]), sb("rstd2", [ROWS, 1])
    xrow = sb("xrow", [ROWS, D + 1])
    row_number = sb("row_number", [ROWS, GROUPS])
    carrier = sb("carrier", [1, 1])
    xrT = sb("xrT", [128, DC, ROWS])
    lg = sb("lg", [ROWS, E])
    mx = sb("mx", [ROWS, 2])
    hot = sb("hot", [ROWS, E])
    place = sb("place", [ROWS, E])
    slotf = sb("slotf", [ROWS, 1])
    slot = sb("slot", [ROWS, 1], I32)

    s = {n: nc.alloc_semaphore("d_" + n) for n in """w_tok w_const w_qkv w_gate w_out w_scaled consts setup setup2
        x_loaded tok_full group_kept group_moved var_ready rstd_ready xn_ready xt_full xt_ready ab_full ab_read spl spl_sig spl_ln g_ready
        gt_ready conv_full conv_init taps_done sig_done prod_done q_sq k_sq ks_full ks_read r2_ready rr_ready
        be_full be_sig be_sel br_ready nbr2_ready d_full d_exp di_ready gate_full gate_sig gate_mul
        dmask_ready kk_full n_off pt_ready n_ready vt_full c_ready
        z_full z_ready pairs_ready xt2_full x_ready y_full y0_ready y1_ready e_full e_ready w_full w_ready
        o_full o_gated o_sq o_mean o_pow o_ready ot_full ot_ready wo_full h2_ready h2_stored var2_ready rstd2_ready
        xrow_ready x2t_full x2t_ready lg_full hot_ready rank_full slot_ready numbered scattered
        pool_chain head_chain tail_chain norm_chain""".split()}
    block = ctx.enter_context(nc.Block())
    W_CONST = 16 * 20

    QUAD0 = 3
    assert QUAD0 + CQ + 1 <= 18 and PER * L == 21

    @block.sync
    def _(sync):
        open_counts(sync, [x for n, x in s.items() if n != "scattered"])
        sync.dma_start(xin[:, :, :], a["x"][0]).then_inc(s["x_loaded"], 16)
        sync.dma_start(wlin[:, :, :], a["wlin"]).then_inc(s["w_tok"], 16)
        sync.dma_start(h1[:, :], a["pos3"]).then_inc(s["w_tok"], 16)
        sync.dma_start(addend[:, :], a["rowadd"]).then_inc(s["w_tok"], 16)
        for t, n in ((wab, "wab"), (wrt, "wrt"), (taps, "taps"), (ident, "ident"), (m_low, "m_low"), (m_lvl, "m_lvl"),
                     (s_gt, "s_gt"), (s_le, "s_le"), (up_to, "up_to"), (after, "after"), (causal, "causal"),
                     (spread, "spread"), (countdown, "countdown"), (before, "before"), (sub_step, "sub_step"),
                     (row_number, "row_number"), (rmsw, "rmsw")):
            sync.dma_start(t[tuple(slice(None) for _ in t.shape)], a[n]).then_inc(s["w_const"], 16)
        for t, n in ((dtb, "dtb"), (negA, "alog"), (rbias, "rbias")):
            sync.dma_start(t[:, :], a[n].partition_broadcast(ROWS)).then_inc(s["w_const"], 16)
        for c in range(DC):
            sync.dma_start(wqkv[:, c, :], a["wqkv"][:, c, :]).then_inc(s["w_qkv"], 16)
        sync.dma_start(wgate[:, :, :], a["wgate"]).then_inc(s["w_gate"], 16)
        sync.dma_start(wout[:, :, :], a["wout"]).then_inc(s["w_out"], 16)

        def load_patches(n):
            sync.wait_ge(s["tok_full"], OPEN + n)
            x = a["x"][n] if isinstance(n, int) else a["x"][bass.ds(n, 1)].rearrange("a p c n -> p (a c) n")
            sync.dma_start(xin[:, :, :], x).then_inc(s["x_loaded"], 16)

        def store_rows(t):
            sync.wait_ge(s["h2_ready"], OPEN + t + 1)
            sync.dma_start(h_dram[:, bass.ds(t, 1), :].rearrange("p a d -> p (a d)"), h2[:, :])\
                .then_inc(s["h2_stored"], 16)

        load_patches(1)
        load_patches(2)
        with sync.Fori(1, GROUPS - 1) as gi:
            load_patches(gi + 2)
            store_rows(gi - 1)
        store_rows(GROUPS - 2)
        store_rows(GROUPS - 1)
        sync.wait_ge(s["h2_stored"], OPEN + 16 * GROUPS)
        sync.wait_ge(s["x_loaded"], OPEN + 16 * (GROUPS + 1))

    def tail_pe(pe, step, t, begun):
        if step == 2:
            for b in range(2):
                pe.wait_ge(s["o_ready"], OPEN + t * 2 + b + 1)
                if b == 0:
                    pe.wait_ge(s["xt_ready"], OPEN + begun)
                for j in range(4):
                    ins = pe.transpose(bank[6 + b][:, j * ROWS:(j + 1) * ROWS], O[:, 4 * b + j, :],
                                       ident[0:ROWS, 0:ROWS])
                ins.then_inc(s["ot_full"], 1)
        if step == 3:
            pe.wait_ge(s["ot_ready"], OPEN + t * 2 + 2)
            for hh in range(H):
                ins = pe.matmul(bank[6][0:ROWS, 0:D], OT[:, hh, :], wout[:, hh, :], start=hh == 0, stop=hh == H - 1)
            ins.then_inc(s["wo_full"], 1)
        if step == 5:
            pe.wait_ge(s["xrow_ready"], OPEN + t + 1)
            for c in range(DC):
                ins = pe.transpose(bank[7][:, c * ROWS:(c + 1) * ROWS], xrow[:, c * 128:(c + 1) * 128],
                                   ident[0:ROWS, 0:ROWS])
            ins.then_inc(s["x2t_full"], 1)
        if step == 6:
            pe.wait_ge(s["x2t_ready"], OPEN + t + 1)
            for c in range(DC):
                ins = pe.matmul(bank[6][0:ROWS, 0:E], xrT[:, c, :], wrt[:, c, :], start=c == 0, stop=c == DC - 1)
            ins.then_inc(s["lg_full"], 1)
        if step == 7:
            pe.wait_ge(s["hot_ready"], OPEN + t + 1)
            pe.matmul(bank[7][0:ROWS, 0:E], before[:, :], hot[:, :], start=True, stop=True)
            pe.matmul(bank[7][0:ROWS, E:2 * E], all_ones[:, :], hot[:, :], start=True, stop=True)\
                .then_inc(s["rank_full"], 1)

    def tail_act(act, step, t):
        if step == 1:
            act.wait_ge(s["o_pow"], OPEN + t + 1)
            act.wait_ge(s["o_gated"], OPEN + 2 * t + 2)
            for b in range(2):
                for j in range(4 * b, 4 * b + 4):
                    ins = act.activation(O[:, j, :], O[:, j, :], ACT.Copy, scale=rms[:, 3, j:j + 1])
                ins.then_inc(s["o_ready"], 1)
        if step == 2:
            for b in range(2):
                act.wait_ge(s["ot_full"], OPEN + t * 2 + b + 1)
                act.activation(OT[:, 4 * b:4 * b + 4, :], bank[6 + b][:, 0:4 * ROWS], ACT.Copy)\
                    .then_inc(s["ot_ready"], 1)
        if step == 5:
            act.wait_ge(s["x2t_full"], OPEN + t + 1)
            act.activation(xrT[:, :, :], bank[7][:, 0:DC * ROWS], ACT.Copy).then_inc(s["x2t_ready"], 1)

    def tail_dve(dve, step, t, ch):
        if step == 3:
            dve.wait_ge(s["wo_full"], OPEN + t + 1)
            dve.wait_ge(s["group_moved"], OPEN + t + 1)
            dve.tensor_tensor(h2[:, :], bank[6][0:ROWS, 0:D], h2[:, :], ALU.add).then_inc(s["h2_ready"], 1)
            dve.wait_ge(s["h2_ready"], OPEN + t + 1)
            ch.link(dve.bn_stats(st2[:, :], h2[:, :]))
            ch.wait()
            dve.memset(ve2[:, :], 0.0)
            ch.link(dve.bn_aggr(mv2[:, :], st2[:, :]))
            ch.wait()
            dve.tensor_scalar(ve2[:, :], mv2[:, 1:2], 1e-5, None, ALU.add).then_inc(s["var2_ready"], 1)
        if step == 4:
            dve.wait_ge(s["rstd2_ready"], OPEN + t + 1)
            dve.wait_ge(s["scattered"], 16 * t + 16)
            dve.tensor_scalar(xrow[:, D:D + 1], row_number[:, bass.ds(t, 1)], 1.0, None, ALU.mult)\
                .then_inc(s["numbered"], 1)
            dve.tensor_scalar(xrow[:, 0:D], h2[:, :], mv2[:, 0:1], rstd2[:, :], ALU.subtract, ALU.mult)\
                .then_inc(s["xrow_ready"], 1)
        if step == 6:
            dve.wait_ge(s["lg_full"], OPEN + t + 1)
            ch.link(dve.tensor_tensor(lg[:, :], bank[6][0:ROWS, 0:E], rbias[:, :], ALU.add))
            choose(dve, ch, lg[:, :], mx, countdown[:, :], hot[:, :], s["hot_ready"])
        if step == 7:
            place_rows(dve, ch, bank[7][0:ROWS, 0:E], bank[7][0:ROWS, E:2 * E], hot, place, slotf, slot,
                       taken, t, s["rank_full"], s["slot_ready"], s["scattered"], 16 * t + 16)

    def tail_pool(pool, step, t):
        if step == 3:
            pool.wait_ge(s["var2_ready"], OPEN + t + 1)
            pool.tensor_tensor(rstd2[:, :], ve2[:, :], nhalf[:, :], ALU.pow).then_inc(s["rstd2_ready"], 1)
        if step == 7:
            pool.wait_ge(s["slot_ready"], OPEN + t + 1)
            pool.tensor_tensor(carrier[:, :], nhalf[0:1, 0:1], nhalf[0:1, 0:1], ALU.mult)
            pool.indirect_dma_start(sorted_x, bass.IndirectOffsetOnAxis(slot[:, 0:1], 0), xrow[:, :], None)\
                .then_inc(s["scattered"], 16)

    d_bank = [bank[4], bank[5], bank[7]]

    def half_quad(pe, step, n, half):
        k = step - QUAD0
        if not 0 <= k < CQ:
            return
        if half == 0 and k >= 2:
            pe.wait_ge(s["taps_done"], OPEN + n * CQ + k - 1)
        for j in (2 * half, 2 * half + 1):
            blk = 4 * k + j
            for c in range(DC):
                ins = pe.matmul(bank[4 + k % 2][:, j * ROWS:(j + 1) * ROWS], wqkv[:, c, blk * 128:(blk + 1) * 128],
                                xnT[:, c, :], start=c == 0, stop=c == DC - 1)
        if half == 1:
            ins.then_inc(s["conv_full"], 1)

    def head_pe(pe, step, n, beside=True):
        if step == 1:
            pe.wait_ge(s["x_loaded"], OPEN + n * 16 + 16)
            for c in range(FC):
                ins = pe.matmul(bank[6][0:ROWS, 0:D], xin[:, c, :], wlin[:, c, :], start=c == 0, stop=c == FC - 1)
            ins.then_inc(s["tok_full"], 1)
        if step == 2:
            pe.wait_ge(s["xn_ready"], OPEN + n + 1)
            for c in range(DC):
                ins = pe.transpose(bank[7][:, c * ROWS:(c + 1) * ROWS], xn[:, c * 128:(c + 1) * 128],
                                   ident[0:ROWS, 0:ROWS])
            ins.then_inc(s["xt_full"], 1)
        if step == 3:
            pe.wait_ge(s["xt_ready"], OPEN + n + 1)
            if beside:
                pe.wait_ge(s["ot_ready"], OPEN + 2 * (n - 1))
            for c in range(DC):
                ins = pe.matmul(bank[7][0:ROWS, 0:32], xnT[:, c, :], wab[:, c, :], start=c == 0, stop=c == DC - 1)
            ins.then_inc(s["ab_full"], 1)
        if QUAD0 <= step < QUAD0 + CQ:
            half_quad(pe, step, n, 0)
        if step == 8:
            pe.wait_ge(s["ab_read"], OPEN + n * 2 + 2)
            for m in range(PER):
                ins = pe.matmul(bank[6][0:MICRO, m * NH * H:(m + 1) * NH * H], spread[:, m, :], blog[:, :],
                                start=True, stop=True)
            ins.then_inc(s["be_full"], 1)
        if step in (9, 14, 16, 18):
            r = (9, 14, 16, 18).index(step)
            if r == 0:
                pe.wait_ge(s["be_sig"], OPEN + n + 1)
                pe.wait_ge(s["q_sq"], OPEN + n + 1)
            else:
                pe.wait_ge(s["k_sq"], OPEN + n * PER + r)
            for hh in range(H):
                ins = pe.matmul(bank[6][0:MICRO, r * H + hh:r * H + hh + 1], sq[:, hh, :], ones[:, :],
                                start=True, stop=True)
            ins.then_inc(s["ks_full"], 1)
        if step in (19, 20):
            for k in range(3 * (step - 19), 3 * (step - 18)):
                if k == 0:
                    pe.wait_ge(s["gt_ready"], OPEN + n * 2 + 2)
                    pe.wait_ge(s["taps_done"], OPEN + n * CQ + CQ)
                if k >= 3:
                    pe.wait_ge(s["d_exp"], OPEN + n * PER * 2 + k - 2)
                lhs, rhs = ((up_to, g_gt), (after, g_le))[k % 2]
                pe.matmul(d_bank[k % 3][0:MICRO, 0:H * T], lhs[:, k // 2, :],
                          rhs[:, :, :].rearrange("p h t -> p (h t)"), start=True, stop=True)\
                    .then_inc(s["d_full"], 1)

    def head_act(act, step, n):
        if step == 2:
            act.wait_ge(s["xt_full"], OPEN + n + 1)
            act.activation(xnT[:, :, :], bank[7][:, 0:DC * ROWS], ACT.Copy).then_inc(s["xt_ready"], 1)
        if step == 4:
            act.wait_ge(s["spl"], OPEN + n + 1)
            act.activation(sp[:, 2], sp[:, 1], ACT.Sigmoid).then_inc(s["spl_sig"], 1)
        if QUAD0 + 2 <= step < QUAD0 + CQ + 2:
            k = step - QUAD0 - 2
            act.wait_ge(s["taps_done"], OPEN + n * CQ + k + 1)
            act.wait_ge(s["prod_done"], OPEN + n * CQ + max(k - 1, 0))
            act.activation(sg[:, k % 2], y[:, k % 3], ACT.Sigmoid).then_inc(s["sig_done"], 1)
        if step == 8:
            act.wait_ge(s["be_full"], OPEN + n + 1)
            act.activation(bs[:, :, :, :].rearrange("p m i h -> p (m i h)"), bank[6][0:MICRO, 0:PER * NH * H],
                           ACT.Sigmoid).then_inc(s["be_sig"], 1)
        if step == 20:
            exponentials(act, n, 3)

    def exponentials(act, n, k0):
        for k in range(k0, k0 + 3):
            act.wait_ge(s["d_full"], OPEN + n * PER * 2 + k + 1)
            act.activation((dj, di)[k % 2][:, k // 2], d_bank[k % 3][0:MICRO, 0:H * T].rearrange("p (h t) -> p h t", h=H),
                           ACT.Exp).then_inc(s["d_exp"], 1)

    def head_act_late(act, step, n):
        if QUAD0 <= step < QUAD0 + CQ:
            k = step - QUAD0
            act.wait_ge(s["conv_full"], OPEN + n * CQ + k + 1)
            act.wait_ge(s["prod_done"], OPEN + n * CQ + max(k - 2, 0))
            for j in range(4):
                ins = act.activation(y[:, k % 3, j, :], bank[4 + k % 2][:, j * ROWS:(j + 1) * ROWS], ACT.Copy,
                                     scale=taps[:, 4 * k + j, TAPS - 1:TAPS])
            ins.then_inc(s["conv_init"], 1)
        if step == 18:
            act.wait_ge(s["spl_sig"], OPEN + n + 1)
            act.activation(sp[:, 2], sp[:, 2], ACT.Ln).then_inc(s["spl_ln"], 1)
        if step == 19:
            exponentials(act, n, 0)

    def head_dve_late(dve, step, n, ch):
        if step == 1:
            dve.wait_ge(s["tok_full"], OPEN + n + 1)
            dve.wait_ge(s["group_kept"], OPEN + n)
            ch.link(dve.tensor_tensor(h1[:, :], bank[6][0:ROWS, 0:D], addend[:, :], ALU.add))
            ch.wait()
            ch.link(dve.bn_stats(st[:, :], h1[:, :]))
            ch.wait()
            dve.memset(ve[:, :], 0.0)
            ch.link(dve.bn_aggr(mv[:, :], st[:, :]))
            ch.wait()
            dve.tensor_scalar(ve[:, :], mv[:, 1:2], 1e-5, None, ALU.add).then_inc(s["var_ready"], 1)
        if step == 3:
            dve.wait_ge(s["ab_full"], OPEN + n + 1)
            dve.tensor_copy(blog[:, :], bank[7][0:ROWS, 0:NH * H]).then_inc(s["ab_read"], 1)
            dve.tensor_tensor(sp[:, 0], bank[7][0:ROWS, NH * H:NH * H + H], dtb[:, :], ALU.add)\
                .then_inc(s["ab_read"], 1)
            dve.wait_ge(s["ab_read"], OPEN + n * 2 + 2)
            dve.scalar_tensor_tensor(sp[:, 1], sp[:, 0], -1.0, sp[:, 0], ALU.mult, ALU.max).then_inc(s["spl"], 1)
        if step == 9:
            dve.wait_ge(s["be_sig"], OPEN + n + 1)
            for m in range(PER):
                ins = dve.tensor_tensor(bs[:, m], bs[:, m], bc(sub_step[:, :], 2, H), ALU.mult)
            ch.link(ins)
            ch.wait()
            ch.link(dve.tensor_reduce(beta[:, :, :], bs[:, :, :, :].rearrange("p m i h -> p m h i"), AX.X, ALU.add))
        if step == 18:
            dve.wait_ge(s["spl_ln"], OPEN + n + 1)
            ch.link(dve.scalar_tensor_tensor(sp[:, 3], sp[:, 0], 0.0, sp[:, 2], ALU.max, ALU.subtract))
            ch.wait()
            dve.tensor_tensor(g[:, :], sp[:, 3], negA[:, :], ALU.mult).then_inc(s["g_ready"], 1)
        if step == 19:
            dve.wait_ge(s["ks_full"], OPEN + n * 4 + 4)
            dve.tensor_scalar(r2[:, :, :].rearrange("p a h -> p (a h)"), bank[6][0:MICRO, 0:4 * H], 1e-6, None,
                              ALU.add).then_inc(s["ks_read"], 1)
            dve.wait_ge(s["ks_read"], OPEN + n + 1)
            dve.reciprocal(r2[:, :, :], r2[:, :, :]).then_inc(s["r2_ready"], 1)
            dve.wait_ge(s["r2_ready"], OPEN + n + 1)
            dve.scalar_tensor_tensor(nbr2[:, :, :], beta[:, :, :], -2.0, r2[:, 1:4], ALU.mult, ALU.mult)\
                .then_inc(s["nbr2_ready"], 1)

    def head_dve(dve, step, n, ch):
        if step == 2:
            dve.wait_ge(s["rstd_ready"], OPEN + n + 1)
            dve.tensor_scalar(xn[:, :], h1[:, :], mv[:, 0:1], rstd[:, :], ALU.subtract, ALU.mult)\
                .then_inc(s["xn_ready"], 1)
        if QUAD0 < step <= QUAD0 + CQ:
            k = step - QUAD0 - 1
            dve.wait_ge(s["conv_init"], OPEN + n * CQ + k + 1)
            for tap in range(TAPS - 2, -1, -1):
                sh = TAPS - 1 - tap
                if sh > 1:
                    ch.wait()
                for j in range(4):
                    yv = y[:, k % 3, j, :].rearrange("p (m t) -> p m t", t=T)[:, :, sh:T]
                    pv = bank[4 + k % 2][:, j * ROWS:(j + 1) * ROWS].rearrange("p (m t) -> p m t", t=T)[:, :, 0:T - sh]
                    ins = dve.scalar_tensor_tensor(yv, pv, taps[:, 4 * k + j, tap:tap + 1], yv, ALU.mult, ALU.add)
                if tap:
                    ch.link(ins)
                else:
                    ins.then_inc(s["taps_done"], 1)

    def head_pool(pool, step, n, beside=True):
        if step == 1:
            pool.wait_ge(s["var_ready"], OPEN + n + 1)
            pool.tensor_tensor(rstd[:, :], ve[:, :], nhalf[:, :], ALU.pow).then_inc(s["rstd_ready"], 1)
        if QUAD0 + 2 <= step < QUAD0 + CQ + 2:
            k = step - QUAD0 - 2
            kind, i, hh = block_of(k)
            pool.wait_ge(s["sig_done"], OPEN + n * CQ + k + 1)
            for m in range(PER):
                c_ = slice(m * T, (m + 1) * T)
                if kind == "q":
                    to = KQ[:, m, hh:hh + 4, MICRO:GRAM]
                else:
                    to = (KQ if kind == "k" else V)[:, m, hh:hh + 4, i:MICRO:NH]
                ins = pool.tensor_tensor(to, y[:, k % 3, :, c_], sg[:, k % 2, :, c_], ALU.mult)
            ins.then_inc(s["prod_done"], 1)
        if step == 7:
            pool.wait_ge(s["prod_done"], OPEN + n * CQ + 2)
            pool.wait_ge(s["ks_full"], OPEN + n * 4)
            if beside:
                pool.wait_ge(s["wo_full"], OPEN + n - 1)
            for m in range(PER):
                q = KQ[:, m, :, MICRO:GRAM]
                ins = pool.tensor_tensor(sq[:, :, m * T:(m + 1) * T], q, q, ALU.mult)
            ins.then_inc(s["q_sq"], 1)
        if step in (13, 15, 17):
            m = (step - 13) // 2
            if m == 0:
                pool.wait_ge(s["prod_done"], OPEN + n * CQ + 8)
            pool.wait_ge(s["ks_full"], OPEN + n * 4 + m + 1)
            k_ = KQ[:, m, :, 0:MICRO]
            pool.tensor_tensor(sq[:, :, :], k_, k_, ALU.mult).then_inc(s["k_sq"], 1)
        if step == 18:
            pool.wait_ge(s["g_ready"], OPEN + n + 1)
            pool.tensor_tensor(g_gt[:, :, :], bc(g[:, :], 2, T), bc(s_gt[:, :], 1, H), ALU.mult)\
                .then_inc(s["gt_ready"], 1)
            pool.tensor_tensor(g_le[:, :, :], bc(g[:, :], 2, T), bc(s_le[:, :], 1, H), ALU.mult)\
                .then_inc(s["gt_ready"], 1)
        if step == 19:
            pool.wait_ge(s["r2_ready"], OPEN + n + 1)
            pool.tensor_tensor(rr[:, :, :], r2[:, 1:4], phalf[:, :].rearrange("p (a h) -> p a h", h=H), ALU.pow)\
                .then_inc(s["rr_ready"], 1)

    @block.gpsimd
    def _(pool):
        pool.memset(phalf[:, :], 0.5).then_inc(s["consts"], 1)
        pool.memset(nhalf[:, :], -0.5).then_inc(s["consts"], 1)
        pool.memset(ones[:, :], 1.0).then_inc(s["consts"], 1)
        pool.memset(all_ones[:, :], 1.0).then_inc(s["consts"], 1)
        pool.memset(PT[:, :, :, :], 0.0).then_inc(s["consts"], 1)
        pool.dma_start(taken[:, :], a["regions"]).then_inc(s["scattered"], 16)
        pool.wait_ge(s["w_const"], OPEN + W_CONST)
        pool.wait_ge(s["consts"], OPEN + 5)
        for step in range(21):
            head_pool(pool, step, 0, beside=False)

        def turn(gi, first, last):
            unit_diagonal(gi, 0)
            if not first:
                norm_power(gi - 1)
            unit_diagonal(gi, 1)
            unit_diagonal(gi, 2)
            pool.tensor_copy(r2_kept[:, :], r2[0:ROWS, 0, :])
            pool.tensor_copy(h_kept[:, :], h1[:, :]).then_inc(s["group_kept"], 1)
            for step in range(PER * L):
                if step == 8:
                    pool.wait_ge(s["group_kept"], OPEN + gi + 1)
                    if not first:
                        pool.wait_ge(s["h2_stored"], OPEN + 16 * gi)
                    pool.tensor_tensor(h2[:, :], h_kept[:, :], bc(ones[0:ROWS, 0], 1, D), ALU.mult).then_inc(s["group_moved"], 1)
                if not first:
                    tail_pool(pool, step, gi - 1)
                if not last:
                    head_pool(pool, step, gi + 1)
            if not last:
                decay_masks(gi + 1)

        def decay_masks(n):
            ch = Chain(pool, s["pool_chain"], PER, n)
            for m in range(PER):
                pool.wait_ge(s["d_exp"], OPEN + (n * PER + m) * 2 + 2)
                pool.wait_ge(s["nbr2_ready"], OPEN + n + 1)
                ch.link(pool.tensor_tensor(dj[:, m], dj[:, m], bc(nbr2[:, m], 2, T), ALU.mult))
                pool.tensor_tensor(di[:, m], di[:, m], bc(causal[:, :], 1, H), ALU.mult).then_inc(s["di_ready"], 1)
                ch.wait()
                if m == 2:
                    pool.wait_ge(s["ks_full"], OPEN + n * 4 + 4)
                for hh in range(0, H, 4):
                    ins = pool.tensor_tensor(
                        dmask[m][:, hh:hh + 4, :].rearrange("p h (t i) -> p h t i", i=NH),
                        bc(dj[:, m, hh:hh + 4, :], 3, NH),
                        bc(m_low[:, :].rearrange("p (t i) -> p t i", i=NH), 1, 4), ALU.mult)
                ins.then_inc(s["dmask_ready"], 1)

        def norm_power(t):
            pool.wait_ge(s["o_mean"], OPEN + t + 1)
            pool.tensor_tensor(rms[:, 3], rms[:, 2], phalf[0:ROWS, 0:H], ALU.pow).then_inc(s["o_pow"], 1)

        def unit_diagonal(gi, m):
            pool.wait_ge(s["n_off"], OPEN + (gi * PER + m) * 3 + 3)
            for b in range(NB):
                nv = N[:, m, HT * b:HT * b + HT, :]
                pool.tensor_tensor(nv, nv, bc(ident[0:MICRO, 0:MICRO], 1, HT), ALU.add).then_inc(s["n_ready"], 1)

        decay_masks(0)
        turn(0, True, False)
        with pool.Fori(1, GROUPS - 1) as gi:
            turn(gi, False, False)
        turn(GROUPS - 1, False, True)
        norm_power(GROUPS - 1)
        for step in range(8):
            tail_pool(pool, step, GROUPS - 1)
        pool.wait_ge(s["scattered"], 16 * GROUPS + 16)

    @block.tensor
    def _(pe):
        pe.wait_ge(s["w_tok"], OPEN + 48)
        pe.wait_ge(s["w_const"], OPEN + W_CONST)
        pe.wait_ge(s["consts"], OPEN + 5)
        for step in range(21):
            if step == QUAD0:
                pe.wait_ge(s["w_qkv"], OPEN + 32)
            head_pe(pe, step, 0, beside=False)
            half_quad(pe, step, 0, 1)
        pe.wait_ge(s["w_gate"], OPEN + 16)
        pe.wait_ge(s["w_scaled"], OPEN + 1)

        def gram(n, m):
            if m == 0:
                pe.wait_ge(s["prod_done"], OPEN + (n + 1) * CQ)
                pe.wait_ge(s["ks_read"], OPEN + n + 1)
                pe.wait_ge(s["d_exp"], OPEN + (n + 1) * PER * 2)
            for q, (h0, nh) in enumerate(TRIPLES):
                if m:
                    pe.wait_ge(s["pt_ready"], OPEN + (n * PER + m - 1) * 3 + q + 1)
                for j in range(nh):
                    ins = pe.matmul(bank[4 + q][0:MICRO, j * GRAM:(j + 1) * GRAM], KQ[:, m, h0 + j, 0:MICRO],
                                    KQ[:, m, h0 + j, :], start=True, stop=True)
                ins.then_inc(s["kk_full"], 1)

        def turn(gi, first, last):
            for n in range(2):
                if not first:
                    pe.wait_ge(s["w_ready"], OPEN + gi * PER * NB)
                for c in range(DC):
                    ins = pe.matmul(bank[2 + n][0:ROWS, :], xnT[:, c, :], wgate[:, c, n * 512:(n + 1) * 512],
                                    start=c == 0, stop=c == DC - 1)
                ins.then_inc(s["gate_full"], 1)
            for m in range(PER):
                if m:
                    gram(gi, m)
                for b in range(NB):
                    if m:
                        pe.wait_ge(s["c_ready"], OPEN + (gi * PER + m - 1) * NB + b + 1)
                    elif not first:
                        pe.wait_ge(s["o_gated"], OPEN + gi * 2)
                    for j in range(HT):
                        ins = pe.transpose(bank[b][0:MICRO, j * HD:(j + 1) * HD], V[:, m, HT * b + j, :], ident[:, :])
                    ins.then_inc(s["vt_full"], 1)
            pe.wait_ge(s["c_ready"], OPEN + (gi + 1) * PER * NB)
            pe.wait_ge(s["gate_mul"], OPEN + gi * 2 + 2)
            pe.wait_ge(s["pt_ready"], OPEN + (gi + 1) * PER * 3)
            for m in range(PER):
                for l in range(L):
                    u = (gi * PER + m) * NB
                    zn = u * L + l * NB
                    yn = (gi * PER + m) * (L - 2) + l - 1
                    for b in range(NB):
                        if l == 0:
                            pe.wait_ge(s["n_ready"], OPEN + u + b + 1)
                            for j in range(HT):
                                ins = pe.transpose(bank[b][0:MICRO, j * MICRO:(j + 1) * MICRO], N[:, m, HT * b + j, :],
                                                   ident[0:MICRO, 0:MICRO])
                        else:
                            if l == 1:
                                pe.wait_ge(s["pairs_ready"], OPEN + u + b + 1)
                            else:
                                pe.wait_ge(s[f"y{b}_ready"], OPEN + yn)
                            for j in range(HT):
                                ins = pe.matmul(bank[b][0:MICRO, j * MICRO:(j + 1) * MICRO], N[:, m, HT * b + j, :],
                                                Y[:, b, j, :], start=True, stop=True)
                        ins.then_inc(s["z_full"], 1)
                    for b in range(NB):
                        if 1 <= l <= L - 2:
                            if l == 1 and m:
                                pe.wait_ge(s["w_ready"], OPEN + u - NB + b + 1)
                            for j in range(HT):
                                ins = pe.transpose(bank[2 + b][0:MICRO, j * MICRO:(j + 1) * MICRO], Y[:, b, j, :],
                                                   ident[0:MICRO, 0:MICRO])
                            ins.then_inc(s["xt2_full"], 1)
                        if l == L - 1:
                            for j in range(HT):
                                ins = pe.matmul(bank[2 + b][0:MICRO, j * HD:(j + 1) * HD], Y[:, b, j, :],
                                                C[:, m, HT * b + j, :], start=True, stop=True)
                            ins.then_inc(s["e_full"], 1)
                    if not last:
                        head_pe(pe, m * L + l, gi + 1)
                    if not first:
                        tail_pe(pe, m * L + l, gi - 1, GROUPS if last else gi + 2)
                    if m == PER - 1 and l == L - 1 and not last:
                        gram(gi + 1, 0)
                    for b in range(NB):
                        if l == 0:
                            continue
                        pe.wait_ge(s["z_ready"], OPEN + u * (L - 1) + (l - 1) * NB + b + 1)
                        if l < L - 1:
                            pe.wait_ge(s["x_ready"], OPEN + u * (L - 2) + (l - 1) * NB + b + 1)
                            for j in range(HT):
                                ins = pe.matmul(bank[2 + b][0:MICRO, j * MICRO:(j + 1) * MICRO], X[:, b, j, :],
                                                Z[:, b, j, :], start=True, stop=True)
                            ins.then_inc(s["y_full"], 1)
                        else:
                            pe.wait_ge(s["e_ready"], OPEN + u + b + 1)
                            for j in range(HT):
                                ins = pe.matmul(bank[2 + b][0:MICRO, j * HD:(j + 1) * HD], Z[:, b, j, :], EE[:, b, j, :],
                                                start=True, stop=True)
                            ins.then_inc(s["w_full"], 1)
                    if not last:
                        half_quad(pe, m * L + l, gi + 1, 1)
            for m in range(PER):
                for b in range(NB):
                    if m == PER - 1:
                        pe.wait_ge(s["w_ready"], OPEN + (gi * PER + m) * NB + b + 1)
                    for j in range(HT):
                        ins = pe.matmul(bank[b][0:ROWS, j * HD:(j + 1) * HD], PT[:, m, HT * b + j, :],
                                        C[:, m, HT * b + j, :], start=m == 0 and j == 0,
                                        stop=m == PER - 1 and j == HT - 1)
                    if m == PER - 1:
                        ins.then_inc(s["o_full"], 1)

        gram(0, 0)
        turn(0, True, False)
        with pe.Fori(1, GROUPS - 1) as gi:
            turn(gi, False, False)
        turn(GROUPS - 1, False, True)
        for step in range(8):
            tail_pe(pe, step, GROUPS - 1, GROUPS)

    @block.scalar
    def _(act):
        act.wait_ge(s["w_const"], OPEN + W_CONST)
        act.activation(negA[:, :], negA[:, :], ACT.Exp).then_inc(s["setup"], 1)
        act.wait_ge(s["w_out"], OPEN + 16)
        act.activation(wout[:, :, :], wout[:, :, :], ACT.Copy, scale=rmsw[:, 0:1]).then_inc(s["w_scaled"], 1)
        for step in range(21):
            head_act(act, step, 0)
            head_act_late(act, step, 0)

        def turn(gi, first, last):
            for n in range(2):
                act.wait_ge(s["gate_full"], OPEN + gi * 2 + n + 1)
                if n or not first:
                    act.wait_ge(s["gate_mul"], OPEN + gi * 2 + n)
                act.activation(gsig[:, :], bank[2 + n][0:ROWS, :], ACT.Sigmoid).then_inc(s["gate_sig"], 1)
            act.wait_ge(s["br_ready"], OPEN + gi + 1)
            for m in range(PER):
                for b in range(NB):
                    act.wait_ge(s["vt_full"], OPEN + (gi * PER + m) * NB + b + 1)
                    for j in range(HT):
                        ins = act.activation(C[:, m, HT * b + j, :], bank[b][0:MICRO, j * HD:(j + 1) * HD], ACT.Copy,
                                             scale=br[:, m, HT * b + j:HT * b + j + 1])
                    ins.then_inc(s["c_ready"], 1)
            for m in range(PER):
                for l in range(L):
                    u = (gi * PER + m) * NB
                    for b in range(NB):
                        if 1 <= l <= L - 2:
                            act.wait_ge(s["xt2_full"], OPEN + u * (L - 2) + (l - 1) * NB + b + 1)
                            act.activation(X[:, b], bank[2 + b][0:MICRO, 0:HT * MICRO].rearrange("p (h c) -> p h c", h=HT),
                                           ACT.Copy).then_inc(s["x_ready"], 1)
                        if l == L - 1:
                            act.wait_ge(s["e_full"], OPEN + u + b + 1)
                            act.activation(EE[:, b], bank[2 + b][0:MICRO, :].rearrange("p (h c) -> p h c", h=HT),
                                           ACT.Copy).then_inc(s["e_ready"], 1)
                    if not last:
                        head_act(act, m * L + l, gi + 1)
                    if not first:
                        tail_act(act, m * L + l, gi - 1)
                    if 1 <= l <= L - 2:
                        for b in range(NB):
                            act.wait_ge(s["y_full"], OPEN + u * (L - 2) + (l - 1) * NB + b + 1)
                            act.activation(Y[:, b], bank[2 + b][0:MICRO, 0:HT * MICRO].rearrange("p (h c) -> p h c", h=HT),
                                           ACT.Copy).then_inc(s[f"y{b}_ready"], 1)
                    if l == L - 1:
                        for b in range(NB):
                            act.wait_ge(s["w_full"], OPEN + u + b + 1)
                            act.activation(C[:, m, HT * b:HT * b + HT, :],
                                           bank[2 + b][0:MICRO, :].rearrange("p (h c) -> p h c", h=HT), ACT.Copy)\
                                .then_inc(s["w_ready"], 1)
                    if not last:
                        head_act_late(act, m * L + l, gi + 1)
            for b in range(2):
                act.wait_ge(s["o_full"], OPEN + gi * 2 + b + 1)
                act.activation(osq[:, 4 * b:4 * b + 4, :], bank[b][0:ROWS, :].rearrange("p (h c) -> p h c", h=4),
                               ACT.Square).then_inc(s["o_sq"], 1)

        turn(0, True, False)
        with act.Fori(1, GROUPS - 1) as gi:
            turn(gi, False, False)
        turn(GROUPS - 1, False, True)
        for step in range(8):
            tail_act(act, step, GROUPS - 1)

    @block.vector
    def _(dve):
        dve.wait_ge(s["w_tok"], OPEN + 48)
        dve.tensor_tensor(addend[:, :], addend[:, :], h1[:, :], ALU.add).then_inc(s["setup2"], 1)
        dve.wait_ge(s["setup"], OPEN + 1)
        dve.tensor_scalar(negA[:, :], negA[:, :], -1.0, None, ALU.mult).then_inc(s["setup2"], 1)
        dve.wait_ge(s["setup2"], OPEN + 2)
        dve.wait_ge(s["w_const"], OPEN + W_CONST)
        dve.wait_ge(s["consts"], OPEN + 5)
        ch0 = Chain(dve, s["head_chain"], 0, 0)
        for step in range(21):
            head_dve(dve, step, 0, ch0)
            head_dve_late(dve, step, 0, ch0)
        HEAD = ch0.n
        ch0 = None

        def norm_factor(t):
            norm = Chain(dve, s["norm_chain"], 4, t)
            dve.wait_ge(s["group_kept"], OPEN + t + 1)
            norm.link(dve.tensor_reduce(rms[:, 0], osq, AX.X, ALU.add))
            norm.wait()
            norm.link(dve.scalar_tensor_tensor(rms[:, 1], rms[:, 0], 1.0 / (HD * HD), r2_kept[:, :], ALU.mult, ALU.mult))
            norm.wait()
            norm.link(dve.tensor_scalar(rms[:, 0], rms[:, 1], 1e-5, None, ALU.add))
            norm.wait()
            norm.link(dve.reciprocal(rms[:, 1], rms[:, 0]))
            norm.wait()
            dve.scalar_tensor_tensor(rms[:, 2], r2_kept[:, :], 1.0 / HD, rms[:, 1], ALU.mult, ALU.mult)\
                .then_inc(s["o_mean"], 1)

        def gram_decayed(n, m):
            dve.wait_ge(s["dmask_ready"], OPEN + n * PER + m + 1)
            for q, (h0, nh) in enumerate(TRIPLES):
                dve.wait_ge(s["kk_full"], OPEN + (n * PER + m) * 3 + q + 1)
                pv = bank[4 + q][0:MICRO, 0:nh * GRAM].rearrange("p (h c) -> p h c", h=nh)
                dve.tensor_tensor(N[:, m, h0:h0 + nh, :], pv[:, :, 0:MICRO], dmask[m][:, h0:h0 + nh, :], ALU.mult)\
                    .then_inc(s["n_off"], 1)

        def turn(gi, first, last):
            head = Chain(dve, s["head_chain"], HEAD, gi + 1)
            tail = Chain(dve, s["tail_chain"], TAIL_LINKS, gi - 1)
            dve.wait_ge(s["rr_ready"], OPEN + gi + 1)
            dve.scalar_tensor_tensor(br[:, :, :], beta[:, :, :], 2.0, rr[:, :, :], ALU.mult, ALU.mult)\
                .then_inc(s["br_ready"], 1)
            for m in range(PER):
                if m:
                    gram_decayed(gi, m)
                dve.wait_ge(s["di_ready"], OPEN + gi * PER + m + 1)
                for q, (h0, nh) in enumerate(TRIPLES):
                    pv = bank[4 + q][0:MICRO, 0:nh * GRAM].rearrange("p (h c) -> p h c", h=nh)
                    dve.tensor_tensor(PT[:, m, h0:h0 + nh, m * T:(m + 1) * T], pv[:, :, MICRO:GRAM],
                                      di[:, m, h0:h0 + nh, :], ALU.mult).then_inc(s["pt_ready"], 1)
                if m == 0:
                    if not first:
                        dve.wait_ge(s["o_gated"], OPEN + gi * 2)
                    for n in range(2):
                        dve.wait_ge(s["gate_sig"], OPEN + gi * 2 + n + 1)
                        dve.tensor_tensor(gs[:, 4 * n:4 * n + 4, :], bank[2 + n][0:ROWS, :].rearrange("p (h c) -> p h c", h=4),
                                          gsig[:, :].rearrange("p (h c) -> p h c", h=4), ALU.mult)\
                            .then_inc(s["gate_mul"], 1)
                if m == 1 and not first:
                    norm_factor(gi - 1)
            for m in range(PER):
                for l in range(L):
                    u = (gi * PER + m) * NB
                    for b in range(NB):
                        dve.wait_ge(s["z_full"], OPEN + u * L + l * NB + b + 1)
                        to, done = (Y, "pairs_ready") if l == 0 else (Z, "z_ready")
                        dve.tensor_tensor(to[:, b], bank[b][0:MICRO, 0:HT * MICRO].rearrange("p (h c) -> p h c", h=HT),
                                          bc(m_lvl[:, l, :], 1, HT), ALU.mult).then_inc(s[done], 1)
                    if not last:
                        head_dve(dve, m * L + l, gi + 1, head)
                    if not last:
                        head_dve_late(dve, m * L + l, gi + 1, head)
                    if not first:
                        tail_dve(dve, m * L + l, gi - 1, tail)
            if not last:
                gram_decayed(gi + 1, 0)
            assert head.n in (0, HEAD) and tail.n in (0, TAIL_LINKS), (tail.n, head.n)
            for b in range(2):
                dve.wait_ge(s["o_sq"], OPEN + gi * 2 + b + 1)
                dve.tensor_tensor(O[:, 4 * b:4 * b + 4, :], bank[b][0:ROWS, :].rearrange("p (h d) -> p h d", h=4),
                                  gs[:, 4 * b:4 * b + 4, :], ALU.mult).then_inc(s["o_gated"], 1)

        gram_decayed(0, 0)
        turn(0, True, False)
        with dve.Fori(1, GROUPS - 1) as gi:
            turn(gi, False, False)
        turn(GROUPS - 1, False, True)
        norm_factor(GROUPS - 1)
        tail = Chain(dve, s["tail_chain"], TAIL_LINKS, GROUPS - 1)
        for step in range(8):
            tail_dve(dve, step, GROUPS - 1, tail)


def choose(dve, ch, lg, mx, countdown, out, ready):
    ch.wait()
    ch.link(dve.tensor_reduce(mx[:, 0:1], lg, AX.X, ALU.max))
    ch.wait()
    ch.link(dve.scalar_tensor_tensor(lg, lg, mx[:, 0:1], countdown, ALU.is_equal, ALU.mult))
    ch.wait()
    ch.link(dve.tensor_reduce(mx[:, 1:2], lg, AX.X, ALU.max))
    ch.wait()
    dve.tensor_scalar(out, lg, mx[:, 1:2], None, ALU.is_equal).then_inc(ready, 1)


def block_of(k):
    if k < 2:
        return "q", 0, 4 * k
    k -= 2
    kind = "k" if k < 6 else "v"
    k %= 6
    return kind, k // 2, 4 * (k % 2)


def host_layouts(i):
    f = np.float32
    x = np.asarray(i["x"])
    p = x.reshape(IMAGES, CHANNELS, GRID, PATCH, GRID, PATCH).transpose(0, 2, 4, 1, 3, 5).reshape(IMAGES, PATCHES, F)
    tok = np.zeros((IMAGES, T, F), f)
    tok[:, 1:] = p
    first = [min(PER * g, FIRST_OF_LAST) for g in range(GROUPS + 1)]
    xg = np.stack([tok[b:b + PER] for b in first]).reshape(-1, ROWS, FC, 128).transpose(0, 3, 2, 1)

    def rows(w):
        w = np.asarray(w)
        return np.ascontiguousarray(w.reshape(-1, 128, w.shape[1]).transpose(1, 0, 2))

    blin = np.asarray(i["L0_tok_b_lin"])
    one = np.concatenate([np.asarray(i["L0_tok_class_token"])[0], np.broadcast_to(blin, (PATCHES, D))])
    taps = np.concatenate([np.asarray(i[f"L0_attn_conv_{c}"]) for c in "qkv"])
    r, c = np.arange(MICRO)[:, None], np.arange(MICRO)[None]
    lvl = [((r // (2 * s)) == (c // (2 * s))) & ((r // s) % 2 == 1) & ((c // s) % 2 == 0) | (r == c) for s in LEVELS]
    tl = (np.arange(ROWS) % T)[:, None]
    im = (np.arange(ROWS) // T)[:, None]
    step_t = (np.arange(MICRO) // NH)[None]
    return dict(
        x=xg, wlin=rows(np.asarray(i["L0_tok_W_lin"]).T), pos3=np.tile(np.asarray(i["L0_tok_position_embeddings"])[0], (PER, 1)),
        rowadd=np.tile(one, (PER, 1)),
        wqkv=rows(np.concatenate([np.asarray(i[f"L0_attn_W{c}"]) for c in "qkv"], 1)),
        wgate=rows(i["L0_attn_Wg"]), wout=rows(i["L0_attn_Wo"]),
        wab=rows(np.concatenate([np.asarray(i["L0_attn_Wb"]), np.asarray(i["L0_attn_Wa"])], 1)),
        wrt=rows(i["L0_ffn_router_w"]), taps=taps.reshape(CB, 128, TAPS).transpose(1, 0, 2),
        dtb=np.asarray(i["L0_attn_dt_bias"]), alog=np.asarray(i["L0_attn_A_log"]),
        rmsw=np.asarray(i["L0_attn_rms_weight"])[:, None], rbias=np.asarray(i["L0_ffn_router_b"]),
        ident=np.eye(128, dtype=f), m_low=(r > c).astype(f),
        m_lvl=np.stack([m.T for m in lvl], 1).astype(f),
        s_gt=(tl > np.arange(T)[None]).astype(f), s_le=(tl <= np.arange(T)[None]).astype(f),
        up_to=np.stack([(im == m) & (tl <= step_t) for m in range(PER)], 1).astype(f),
        after=np.stack([(im == m) & (tl > step_t) for m in range(PER)], 1).astype(f),
        causal=(step_t.T <= np.arange(T)[None]).astype(f),
        spread=np.stack([(im == m) & (tl == step_t) for m in range(PER)], 1).astype(f),
        sub_step=(r % NH == np.arange(NH)[None]).astype(f),
        countdown=np.tile(np.arange(E, 0, -1).astype(f), (ROWS, 1)),
    )


SLOTS = 256
REGION = (-(-TOKENS // SLOTS) + 1) * SLOTS
EMPTY = E * REGION
SORTED_ROWS = EMPTY + SLOTS
MAX_TILES = (TOKENS + E * (SLOTS - 1)) // SLOTS
PER_EXPERT = -(-TOKENS // SLOTS)


def mixture_phase(nc, ctx, tag, w1_dram, b1_dram, w2_dram, b2_dram, gated, a, taken, sorted_x, y_dram):
    def sb(name, shape, dt=F32):
        return ctx.enter_context(nc.sbuf_tensor(tag + name, shape, dt))

    bank = [ctx.enter_context(nc.psum_tensor(f"{tag}bank{i}", [128, 512], F32)) for i in range(8)]
    WIDE = 2 * HID if gated else HID
    FB = HID // 128
    NT = MAX_TILES
    PAIRS = (NT - 1) // 2
    assert NT % 2 == 1
    w1 = sb("w1", [128, 2, DC, WIDE])
    w2 = sb("w2", [128, 2, FB, D])
    b1 = sb("b1", [128, 2, WIDE // 128])
    b2 = sb("b2", [128, 2, D])
    ones = sb("ones", [1, 1])
    ident = sb("ident", [128, 128])
    zero = sb("zero", [128, 2, D + 1])
    xr = sb("xr", [128, 2, 2, D + 1])
    to_row = sb("to_row", [128, 2, 2], I32)
    carrier = sb("carrier", [1, 1])
    xT = sb("xT", [128, 2, DC, SLOTS])
    sig = sb("sig", [128, 2, SLOTS])
    hid = sb("hid", [128, FB, SLOTS])
    yo = sb("yo", [128, 2, 2, D])
    region = sb("region", [1, E])
    full = sb("full", [1, E, PER_EXPERT])
    upto = sb("upto", [1, E, E])
    number = sb("number", [1, NT + 1, E])
    t_e = sb("t_e", [1, 6, E])
    t_ek = sb("t_ek", [1, E, PER_EXPERT])
    t_ee = sb("t_ee", [1, E, E])
    t_te = sb("t_te", [1, 2, NT + 1, E])
    t_t = sb("t_t", [1, 6, NT + 1])
    table = sb("table", [1, 2, NT + 1], I32)
    tails = sb("tails", [1, E], I32)
    s = {n: nc.alloc_semaphore(tag + n) for n in """consts weights0 weights1 rows0 rows1 zeroed
        chain table_ready xt_full xt_ready up_full sig_done hid_ready y_full y_ready sent carried to_row_ready loads""".split()}
    loaded, rows_in = [s["weights0"], s["weights1"]], [s["rows0"], s["rows1"]]
    block = ctx.enter_context(nc.Block())

    @block.sync
    def _(sync):
        open_counts(sync, [x for n, x in s.items() if n != "sent"])
        for t, n in ((region, "region"), (full, "full"), (upto, "upto"), (number, "number"), (ident, "ident")):
            sync.dma_start(t[tuple(slice(None) for _ in t.shape)], a[n]).then_inc(s["loads"], 16)
        sync.wait_ge(s["sent"], 16)
        sync.dma_start(sorted_x[EMPTY:EMPTY + SLOTS, :].rearrange("(h p) d -> p h d", p=128), zero[:, :, :])\
            .then_inc(s["zeroed"], 16)

        def load_weights(n, b):
            e = sync.value_load(table[0:1, 0:1, bass.ds(n, 1)].rearrange("p a b -> p (a b)"), min_val=0, max_val=E - 1)
            e = bass.ds(e, 1)
            sync.dma_start(w1[:, b], w1_dram[e].rearrange("a p c n -> p (a c) n")).then_inc(loaded[b], 16)
            sync.dma_start(b1[:, b], b1_dram[e].rearrange("a p n -> p (a n)")).then_inc(loaded[b], 16)
            sync.dma_start(w2[:, b], w2_dram[e].rearrange("a p c n -> p (a c) n")).then_inc(loaded[b], 16)
            sync.dma_start(b2[:, b], b2_dram[e].rearrange("a d -> (a d)").partition_broadcast(128)).then_inc(loaded[b], 16)

        def rows_of(n):
            r = sync.value_load(table[0:1, 1:2, bass.ds(n, 1)].rearrange("p a b -> p (a b)"), min_val=0, max_val=EMPTY)
            return bass.ds(r, SLOTS)

        def load_rows(n, b):
            sync.dma_start(xr[:, b], sorted_x[rows_of(n), :].rearrange("(h p) d -> p h d", p=128))\
                .then_inc(rows_in[b], 16)

        sync.wait_ge(s["table_ready"], OPEN + 3)
        for e in range(E):
            r = sync.value_load(tails[0:1, e:e + 1], min_val=e * REGION, max_val=e * REGION + TOKENS)
            sync.dma_start(sorted_x[bass.ds(r, SLOTS), :].rearrange("(h p) d -> p h d", p=128), zero[:, :, :])\
                .then_inc(s["zeroed"], 16)
        load_weights(0, 0)
        sync.wait_ge(s["zeroed"], OPEN + 16 * (E + 1))
        load_rows(0, 0)
        load_rows(1, 1)
        load_weights(1, 1)
        with sync.Fori(0, PAIRS) as pair:
            for b in range(2):
                n = 2 * pair + b
                sync.wait_ge(s["xt_full"], OPEN + n + 1)
                sync.wait_ge(s["to_row_ready"], OPEN + n + 1)
                load_rows(n + 2, b)
                sync.wait_ge(s["y_ready"], OPEN + n + 1)
                load_weights(n + 2, b)
        sync.wait_ge(rows_in[1], OPEN + 16 * (PAIRS + 1))
        sync.wait_ge(loaded[1], OPEN + 64 * (PAIRS + 1))

    @block.gpsimd
    def _(pool):
        pool.memset(ones[:, :], 1.0).then_inc(s["consts"], 1)

        def send_rows(n, b, nb):
            pool.wait_ge(s["y_ready"], OPEN + n + 1)
            pool.tensor_tensor(carrier[:, :], ones[:, 0:1], ones[:, 0:1], ALU.mult).then_inc(s["carried"], 1)
            for half in range(2):
                pool.indirect_dma_start(y_dram, bass.IndirectOffsetOnAxis(to_row[:, b, half:half + 1], 0),
                                        yo[:, b, half, :], None).then_inc(s["sent"], 16)

        pool.wait_ge(s["consts"], OPEN + 1)
        pool.dma_start(zero[:, :, :], a["zero_rows"]).then_inc(s["sent"], 16)
        with pool.Fori(0, PAIRS) as pair:
            for b in range(2):
                send_rows(2 * pair + b, b, pair)
        send_rows(NT - 1, 0, PAIRS)
        pool.wait_ge(s["sent"], 32 * NT + 16)

    @block.tensor
    def _(pe):
        pe.wait_ge(s["loads"], OPEN + 80)

        def turn(n, b, nb):
            pe.wait_ge(rows_in[b], OPEN + 16 * (nb + 1))
            for c in range(DC):
                for h in range(2):
                    ins = pe.transpose(bank[7][:, c * SLOTS + h * 128:c * SLOTS + (h + 1) * 128],
                                       xr[:, b, h, c * 128:(c + 1) * 128], ident[:, :])
            ins.then_inc(s["xt_full"], 1)

        def tile(n, b, nb, last=False):
            pe.wait_ge(loaded[b], OPEN + (nb + 1) * 64)
            pe.wait_ge(s["xt_ready"], OPEN + n + 1)
            for f in range(FB):
                pe.wait_ge(s["hid_ready"], OPEN + n * FB + max(f - 2, 0))
                for up in range(2 if gated else 1):
                    for c in range(DC):
                        col = up * HID + f * 128
                        ins = pe.matmul(bank[(f % 3) * 2 + up][:, 0:SLOTS], w1[:, b, c, col:col + 128], xT[:, b, c, :],
                                        start=c == 0, stop=c == DC - 1)
                ins.then_inc(s["up_full"], 1)
            if not last:
                turn(n + 1, 1 - b, nb + b)
            pe.wait_ge(s["hid_ready"], OPEN + n * FB + FB)
            pe.wait_ge(s["y_ready"], OPEN + n)
            for half in range(2):
                y = bank[6][:, half * D:(half + 1) * D]
                for f in range(FB):
                    ins = pe.matmul(y, hid[:, f, half * 128:(half + 1) * 128], w2[:, b, f, :], start=f == 0,
                                    stop=f == FB - 1)
            ins.then_inc(s["y_full"], 1)

        turn(0, 0, 0)
        with pe.Fori(0, PAIRS) as pair:
            for b in range(2):
                tile(2 * pair + b, b, pair)
        tile(NT - 1, 0, PAIRS, last=True)

    @block.scalar
    def _(act):
        def turned(n, b):
            act.wait_ge(s["xt_full"], OPEN + n + 1)
            act.activation(xT[:, b], bank[7][:, :].rearrange("p (c n) -> p c n", c=DC), ACT.Copy)\
                .then_inc(s["xt_ready"], 1)

        def tile(n, b, nb, last=False):
            act.wait_ge(loaded[b], OPEN + (nb + 1) * 64)
            if not gated:
                act.wait_ge(s["y_full"], OPEN + n)
            for f in range(FB):
                act.wait_ge(s["up_full"], OPEN + n * FB + f + 1)
                if gated:
                    act.wait_ge(s["hid_ready"], OPEN + n * FB + max(f - 1, 0))
                    act.activation(sig[:, f % 2, :], bank[(f % 3) * 2 + 1][:, 0:SLOTS], ACT.Sigmoid,
                                   bias=b1[:, b, FB + f:FB + f + 1]).then_inc(s["sig_done"], 1)
                else:
                    act.activation(hid[:, f, :], bank[(f % 3) * 2][:, 0:SLOTS], ACT.Relu,
                                   bias=b1[:, b, f:f + 1]).then_inc(s["hid_ready"], 1)
            if not last:
                turned(n + 1, 1 - b)

        turned(0, 0)
        with act.Fori(0, PAIRS) as pair:
            for b in range(2):
                tile(2 * pair + b, b, pair)
        tile(NT - 1, 0, PAIRS, last=True)

    @block.vector
    def _(dve):
        ch = Chain(dve, s["chain"], 0, 0)
        TT, RED = dve.tensor_tensor, dve.tensor_reduce
        dve.wait_ge(s["loads"], OPEN + 80)
        cnt, nt, cum = t_e[:, 0], t_e[:, 1], t_e[:, 2]
        ch.link(TT(cnt, taken[0:1, :], region[:, :], ALU.subtract))
        ch.wait()
        ch.link(TT(t_ek[:, :, :], bc(cnt, 2, PER_EXPERT), full[:, :, :], ALU.is_gt))
        ch.wait()
        ch.link(RED(nt, t_ek[:, :, :], AX.X, ALU.add))
        ch.wait()
        ch.link(TT(t_ee[:, :, :], bc(nt, 1, E), upto[:, :, :], ALU.mult))
        ch.wait()
        ch.link(RED(cum, t_ee[:, :, :], AX.X, ALU.add))
        ch.wait()
        ch.link(TT(t_te[:, 0], number[:, :, :], bc(cum, 1, NT + 1), ALU.is_ge))
        ch.wait()
        ch.link(RED(t_t[:, 0], t_te[:, 0], AX.X, ALU.add))
        ch.link(TT(t_te[:, 1], t_te[:, 0], bc(nt, 1, NT + 1), ALU.mult))
        ch.wait()
        ch.link(RED(t_t[:, 1], t_te[:, 1], AX.X, ALU.add))
        ch.wait()
        ch.link(TT(t_t[:, 2], number[:, :, 0], t_t[:, 1], ALU.subtract))
        ch.link(dve.tensor_scalar(t_t[:, 3], t_t[:, 0], float(E), float(SLOTS), ALU.is_lt, ALU.mult))
        ch.wait()
        ch.link(TT(t_t[:, 4], t_t[:, 2], t_t[:, 3], ALU.mult))
        ch.wait()
        dve.scalar_tensor_tensor(table[:, 1], t_t[:, 0], float(REGION), t_t[:, 4], ALU.mult, ALU.add)\
            .then_inc(s["table_ready"], 1)
        dve.tensor_scalar(table[:, 0], t_t[:, 0], float(E - 1), None, ALU.min).then_inc(s["table_ready"], 1)
        dve.tensor_copy(tails[:, :], taken[0:1, :]).then_inc(s["table_ready"], 1)

        def tile(n, b, nb):
            if gated:
                dve.wait_ge(loaded[b], OPEN + (nb + 1) * 64)
                dve.wait_ge(s["y_full"], OPEN + n)
                for f in range(FB):
                    dve.wait_ge(s["sig_done"], OPEN + n * FB + f + 1)
                    dve.scalar_tensor_tensor(hid[:, f, :], bank[(f % 3) * 2][:, 0:SLOTS], b1[:, b, f:f + 1],
                                             sig[:, f % 2, :], ALU.add, ALU.mult).then_inc(s["hid_ready"], 1)
            if not gated:
                dve.wait_ge(loaded[b], OPEN + (nb + 1) * 64)
            dve.wait_ge(s["y_full"], OPEN + n + 1)
            dve.wait_ge(s["carried"], OPEN + n)
            dve.wait_ge(s["sent"], 32 * n + 16)
            dve.wait_ge(rows_in[b], OPEN + 16 * (nb + 1))
            dve.tensor_copy(to_row[:, b, :], xr[:, b, :, D]).then_inc(s["to_row_ready"], 1)
            dve.tensor_tensor(yo[:, b], bank[6][:, :].rearrange("p (h d) -> p h d", h=2), bc(b2[:, b, :], 1, 2),
                              ALU.add).then_inc(s["y_ready"], 1)

        with dve.Fori(0, PAIRS) as pair:
            for b in range(2):
                tile(2 * pair + b, b, pair)
        tile(NT - 1, 0, PAIRS)


def attention_phase(nc, ctx, a, h_dram, y_dram, h_all, sorted_x, taken, prob):
    def sb(name, shape, dt=F32):
        return ctx.enter_context(nc.sbuf_tensor("a_" + name, shape, dt))

    def two(name, shape, dt=F32):
        return [sb(name + str(p), shape, dt) for p in range(2)]

    bank = [ctx.enter_context(nc.psum_tensor(f"a_bank{i}", [128, 512], F32)) for i in range(8)]
    assert GROUPS % 2 == 0
    AC = AH // 4
    wq = sb("wq", [128, DC, AC * 128])
    wk = sb("wk", [128, DC, AC * 128])
    wv = sb("wv", [128, DC, D])
    wo = sb("wo", [128, DC, D])
    wg = sb("wg", [128, DC, E])
    bq = sb("bq", [128, AC])
    bk = sb("bk", [128, AC])
    bv = sb("bv", [ROWS, D])
    bo = sb("bo", [ROWS, D])
    bg = sb("bg", [ROWS, E])
    ident = sb("ident", [128, 128])
    mask = sb("mask", [ROWS, ROWS])
    countdown = sb("countdown", [ROWS, E])
    nhalf = sb("nhalf", [ROWS, 1])
    before = sb("before", [ROWS, ROWS])
    all_ones = sb("all_ones", [ROWS, ROWS])
    row_number = sb("row_number", [ROWS, GROUPS])
    carrier = sb("carrier", [1, 2])
    h_in, y_in = two("h_in", [ROWS, D]), two("y_in", [ROWS, D])
    hcur, hb, xn = two("hcur", [ROWS, D]), two("hb", [ROWS, D]), two("xn", [ROWS, D])
    st, mv, ve, rstd = two("st", [ROWS, 6]), two("mv", [ROWS, 2]), two("ve", [ROWS, 1]), two("rstd", [ROWS, 1])
    xnT, xrT = two("xnT", [128, DC, ROWS]), two("xrT", [128, DC, ROWS])
    qT, kT = two("qT", [128, AC, ROWS]), two("kT", [128, AC, ROWS])
    v = two("v", [ROWS, D])
    S, PT = two("S", [ROWS, AC, 4, ROWS]), two("PT", [ROWS, AC, 4, ROWS])
    mx, sums, rinv = two("mx", [ROWS, AH]), two("sums", [ROWS, AH]), two("rinv", [ROWS, AH])
    yv, yT = two("yv", [ROWS, D]), two("yT", [128, DC, ROWS])
    lg, lm, ex, gx = two("lg", [ROWS, E]), two("lm", [ROWS, E]), two("ex", [ROWS, E]), two("gx", [ROWS, 4])
    hot, place = two("hot", [ROWS, E]), two("place", [ROWS, E])
    slotf, slot = two("slotf", [ROWS, 1]), two("slot", [ROWS, 1], I32)
    xrow = two("xrow", [ROWS, D + 1])

    s = {n: nc.alloc_semaphore("a_" + n) for n in """weights consts scaled loaded0 loaded1 merged
        front_chain sums_chain back_chain route_chain var_ready rstd_ready var2_ready rstd2_ready xn_ready
        xt_full xt_ready q_full k_full v_full q_ready k_ready v_ready
        hb_ready s_full masked max_ready shifted exp_done sums_ready pt_full pt_ready y_full y_ready yt_full yt_ready
        wo_full h_ready xrow_ready x2t_full x2t_ready lg_full lg_read lg_shift lg_exp hot_ready
        rank_full slot_ready numbered sent0 sent1""".split()}
    block = ctx.enter_context(nc.Block())
    LOADED = 16 * 14
    sent = [s["sent0"], s["sent1"]]

    assert GROUPS % 2 == 0

    def run_steps(eng, step):
        step(0, 0, 0, back=False, route=False)
        step(1, 1, 0, route=False)
        with eng.Fori(1, GROUPS // 2) as half:
            step(2 * half, 0, half)
            step(2 * half + 1, 1, half)
        step(GROUPS, 0, GROUPS // 2, front=False)
        step(GROUPS + 1, 1, GROUPS // 2, front=False, back=False)

    @block.sync
    def _(sync):
        open_counts(sync, [x for n, x in s.items() if n not in ("sent0", "sent1")])
        for t, n in ((ident, "ident"), (wq, "awq"), (wk, "awk"), (wv, "awv"), (wo, "awo"), (wg, "awg"), (bq, "abq"),
                     (bk, "abk"), (mask, "amask"), (countdown, "countdown"), (before, "before")):
            sync.dma_start(t[tuple(slice(None) for _ in t.shape)], a[n]).then_inc(s["weights"], 16)
        for t, n in ((bv, "abv"), (bo, "abo"), (bg, "abg")):
            sync.dma_start(t[:, :], a[n].partition_broadcast(ROWS)).then_inc(s["weights"], 16)

        def load(g, p):
            sync.dma_start(h_in[p][:, :], h_dram[:, bass.ds(g, 1), :].rearrange("p a d -> p (a d)"))\
                .then_inc(s[f"loaded{p}"], 16)
            sync.dma_start(y_in[p][:, :], y_dram[bass.ds(g * ROWS, ROWS), :]).then_inc(s[f"loaded{p}"], 16)

        load(0, 0)
        load(1, 1)
        with sync.Fori(0, GROUPS // 2 - 1) as turn:
            for p in range(2):
                g = 2 * turn + 2 + p
                sync.wait_ge(s["merged"], OPEN + g - 1)
                load(g, p)

    @block.gpsimd
    def _(pool):
        pool.memset(nhalf[:, :], -0.5).then_inc(s["consts"], 1)
        pool.memset(all_ones[:, :], 1.0).then_inc(s["consts"], 1)
        pool.wait_ge(s["weights"], OPEN + LOADED)
        pool.wait_ge(s["consts"], OPEN + 2)
        pool.dma_start(taken[:, :], a["regions"]).then_inc(s["sent0"], 16)
        pool.dma_start(row_number[:, :], a["row_number"]).then_inc(s["sent1"], 16)

        def step(k, p, t, front=True, back=True, route=True):
            g = k
            if front:
                pool.wait_ge(s["var_ready"], OPEN + g + 1)
                pool.tensor_tensor(rstd[p][:, :], ve[p][:, :], nhalf[:, :], ALU.pow).then_inc(s["rstd_ready"], 1)
                pool.tensor_tensor(hb[p][:, :], hcur[p][:, :], bo[:, :], ALU.add).then_inc(s["hb_ready"], 1)
                for c in range(AC):
                    pool.wait_ge(s["max_ready"], OPEN + g * AC + c + 1)
                    pool.tensor_tensor(S[p][:, c], S[p][:, c], bc(mx[p][:, 4 * c:4 * c + 4], 2, ROWS), ALU.subtract)\
                        .then_inc(s["shifted"], 1)
            if back:
                g, q = k - 1, 1 - p
                pool.wait_ge(s["var2_ready"], OPEN + g + 1)
                pool.tensor_tensor(rstd[q][:, :], ve[q][:, :], nhalf[:, :], ALU.pow).then_inc(s["rstd2_ready"], 1)
            if route:
                g = k - 2
                pool.wait_ge(s["slot_ready"], OPEN + g + 1)
                pool.tensor_tensor(carrier[:, p:p + 1], nhalf[0:1, 0:1], nhalf[0:1, 0:1], ALU.mult)
                pool.indirect_dma_start(sorted_x, bass.IndirectOffsetOnAxis(slot[p][:, 0:1], 0), xrow[p][:, :], None)\
                    .then_inc(sent[p], 16)

        run_steps(pool, step)
        for p in range(2):
            pool.wait_ge(sent[p], 16 * (GROUPS // 2) + 16)

    @block.tensor
    def _(pe):
        def turned(out, rows):
            for c in range(DC):
                ins = pe.transpose(out[:, c * ROWS:(c + 1) * ROWS], rows[:, c * 128:(c + 1) * 128],
                                   ident[0:ROWS, 0:ROWS])
            return ins

        pe.wait_ge(s["weights"], OPEN + LOADED)
        pe.wait_ge(s["scaled"], OPEN + 1)

        def step(k, p, t, front=True, back=True, route=True):
            f, b, r = k, k - 1, k - 2
            if back:
                for c in range(AC):
                    pe.wait_ge(s["exp_done"], OPEN + b * AC + c + 1)
                    for j in range(4):
                        ins = pe.transpose(bank[4 + c][0:ROWS, j * ROWS:(j + 1) * ROWS], S[1 - p][:, c, j, :],
                                           ident[0:ROWS, 0:ROWS])
                    ins.then_inc(s["pt_full"], 1)
            if front:
                pe.wait_ge(s["xn_ready"], OPEN + f + 1)
                if back and not (isinstance(k, int) and k < 3):
                    pe.wait_ge(s["slot_ready"], OPEN + r)
                turned(bank[0], xn[p]).then_inc(s["xt_full"], 1)
            if route:
                pe.wait_ge(s["xrow_ready"], OPEN + r + 1)
                turned(bank[3], xrow[p]).then_inc(s["x2t_full"], 1)
            if front:
                pe.wait_ge(s["xt_ready"], OPEN + f + 1)
                if route and not (isinstance(k, int) and k < 3):
                    pe.wait_ge(s["lg_read"], OPEN + r)
                for w, bk_, full in ((wq, 1, "q_full"), (wk, 2, "k_full")):
                    for j in range(AC):
                        for c in range(DC):
                            ins = pe.matmul(bank[bk_][:, j * ROWS:(j + 1) * ROWS], w[:, c, j * 128:(j + 1) * 128],
                                            xnT[p][:, c, :], start=c == 0, stop=c == DC - 1)
                    ins.then_inc(s[full], 1)
                for c in range(DC):
                    ins = pe.matmul(bank[0][0:ROWS, 0:D], xnT[p][:, c, :], wv[:, c, :], start=c == 0, stop=c == DC - 1)
                ins.then_inc(s["v_full"], 1)
            if back:
                pe.wait_ge(s["v_ready"], OPEN + b + 1)
                if route:
                    pe.wait_ge(s["x2t_ready"], OPEN + r + 1)
                for c in range(AC):
                    pe.wait_ge(s["pt_ready"], OPEN + b * AC + c + 1)
                    for j in range(4):
                        hh = 4 * j + c
                        ins = pe.matmul(bank[3][0:ROWS, hh * AD:(hh + 1) * AD], PT[1 - p][:, c, j, :],
                                        v[1 - p][:, hh * AD:(hh + 1) * AD], start=True, stop=True)
                ins.then_inc(s["y_full"], 1)
            if route:
                pe.wait_ge(s["x2t_ready"], OPEN + r + 1)
                if front:
                    pe.wait_ge(s["q_ready"], OPEN + f + 1)
                for c in range(DC):
                    ins = pe.matmul(bank[1][0:ROWS, 0:E], xrT[p][:, c, :], wg[:, c, :], start=c == 0,
                                    stop=c == DC - 1)
                ins.then_inc(s["lg_full"], 1)
            if front:
                pe.wait_ge(s["q_ready"], OPEN + f + 1)
                pe.wait_ge(s["k_ready"], OPEN + f + 1)
                if back:
                    pe.wait_ge(s["pt_ready"], OPEN + b * AC + AC)
                for c in range(AC):
                    for j in range(4):
                        ins = pe.matmul(bank[4 + j][0:ROWS, c * ROWS:(c + 1) * ROWS], qT[p][32 * j:32 * j + 32, c, :],
                                        kT[p][32 * j:32 * j + 32, c, :], start=True, stop=True)
                        if c == AC - 1:
                            ins.then_inc(s["s_full"], 1)
            if back:
                pe.wait_ge(s["y_ready"], OPEN + b + 1)
                if front:
                    pe.wait_ge(s["k_ready"], OPEN + f + 1)
                turned(bank[2], yv[1 - p]).then_inc(s["yt_full"], 1)
            if route:
                pe.wait_ge(s["hot_ready"], OPEN + r + 1)
                if front:
                    pe.wait_ge(s["v_ready"], OPEN + f + 1)
                pe.matmul(bank[0][0:ROWS, 0:E], before[:, :], hot[p][:, :], start=True, stop=True)
                pe.matmul(bank[0][0:ROWS, E:2 * E], all_ones[:, :], hot[p][:, :], start=True, stop=True)\
                    .then_inc(s["rank_full"], 1)
            if back:
                pe.wait_ge(s["yt_ready"], OPEN + b + 1)
                for c in range(DC):
                    ins = pe.matmul(bank[3][0:ROWS, 0:D], yT[1 - p][:, c, :], wo[:, c, :], start=c == 0,
                                    stop=c == DC - 1)
                ins.then_inc(s["wo_full"], 1)

        run_steps(pe, step)

    @block.scalar
    def _(act):
        act.wait_ge(s["weights"], OPEN + LOADED)

        def step(k, p, t, front=True, back=True, route=True):
            f, b, r = k, k - 1, k - 2
            if back:
                for c in range(AC):
                    act.wait_ge(s["pt_full"], OPEN + b * AC + c + 1)
                    act.activation(PT[1 - p][:, c], bank[4 + c][0:ROWS, 0:4 * ROWS], ACT.Copy).then_inc(s["pt_ready"], 1)
            if front:
                act.wait_ge(s["xt_full"], OPEN + f + 1)
                act.activation(xnT[p][:, :, :], bank[0][:, 0:DC * ROWS], ACT.Copy).then_inc(s["xt_ready"], 1)
            if route:
                act.wait_ge(s["x2t_full"], OPEN + r + 1)
                act.activation(xrT[p][:, :, :], bank[3][:, 0:DC * ROWS], ACT.Copy).then_inc(s["x2t_ready"], 1)
            if front:
                act.wait_ge(s["k_full"], OPEN + f + 1)
                for j in range(AC):
                    ins = act.activation(kT[p][:, j, :], bank[2][:, j * ROWS:(j + 1) * ROWS], ACT.Identity,
                                         bias=bk[:, j:j + 1])
                ins.then_inc(s["k_ready"], 1)
            if route:
                act.wait_ge(s["lg_shift"], OPEN + r + 1)
                act.activation(ex[p][:, :], lm[p][:, :], ACT.Exp).then_inc(s["lg_exp"], 1)
            if back:
                act.wait_ge(s["yt_full"], OPEN + b + 1)
                act.activation(yT[1 - p][:, :, :], bank[2][:, 0:DC * ROWS], ACT.Copy).then_inc(s["yt_ready"], 1)
            if front:
                for c in range(AC):
                    act.wait_ge(s["shifted"], OPEN + f * AC + c + 1)
                    act.activation(S[p][:, c], S[p][:, c], ACT.Exp).then_inc(s["exp_done"], 1)

        run_steps(act, step)

    @block.vector
    def _(dve):
        def statistics(ch, p, h, ready):
            ch.link(dve.bn_stats(st[p][:, :], h))
            ch.wait()
            dve.memset(ve[p][:, :], 0.0)
            ch.link(dve.bn_aggr(mv[p][:, :], st[p][:, :]))
            ch.wait()
            dve.tensor_scalar(ve[p][:, :], mv[p][:, 1:2], 1e-5, None, ALU.add).then_inc(ready, 1)

        dve.wait_ge(s["weights"], OPEN + LOADED)
        dve.tensor_scalar(bq[:, :], bq[:, :], AD ** -0.5, None, ALU.mult).then_inc(s["scaled"], 1)
        dve.wait_ge(s["scaled"], OPEN + 1)
        dve.wait_ge(s["sent0"], 16)
        dve.wait_ge(s["sent1"], 16)

        def step(k, p, t, front=True, back=True, route=True):
            q, g = 1 - p, k
            if front:
                ch = Chain(dve, s["front_chain"], 2, g)
                if route:
                    dve.wait_ge(s["xrow_ready"], OPEN + g - 1)
                dve.wait_ge(s[f"loaded{p}"], OPEN + 32 * t + 32)
                dve.tensor_tensor(hcur[p][:, :], h_in[p][:, :], y_in[p][:, :], ALU.add).then_inc(s["merged"], 1)
                dve.wait_ge(s["merged"], OPEN + g + 1)
                statistics(ch, p, hcur[p][:, :], s["var_ready"])
                dve.wait_ge(s["rstd_ready"], OPEN + g + 1)
                dve.tensor_scalar(xn[p][:, :], hcur[p][:, :], mv[p][:, 0:1], rstd[p][:, :], ALU.subtract, ALU.mult)\
                    .then_inc(s["xn_ready"], 1)
            if back:
                sm = Chain(dve, s["sums_chain"], 4, k - 1)
                for c in range(AC):
                    dve.wait_ge(s["exp_done"], OPEN + (k - 1) * AC + c + 1)
                    sm.link(dve.tensor_reduce(sums[q][:, 4 * c:4 * c + 4], S[q][:, c], AX.X, ALU.add))
                sm.wait()
                dve.reciprocal(rinv[q][:, :], sums[q][:, :]).then_inc(s["sums_ready"], 1)
            if front:
                dve.wait_ge(s["q_full"], OPEN + g + 1)
                for j in range(AC):
                    ins = dve.tensor_scalar(qT[p][:, j, :], bank[1][:, j * ROWS:(j + 1) * ROWS], AD ** -0.5,
                                            bq[:, j:j + 1], ALU.mult, ALU.add)
                ins.then_inc(s["q_ready"], 1)
                dve.wait_ge(s["v_full"], OPEN + g + 1)
                dve.tensor_tensor(v[p][:, :], bank[0][0:ROWS, 0:D], bv[:, :], ALU.add).then_inc(s["v_ready"], 1)
            if back:
                g = k - 1
                dve.wait_ge(s["y_full"], OPEN + g + 1)
                dve.wait_ge(s["sums_ready"], OPEN + g + 1)
                dve.tensor_tensor(yv[q][:, :].rearrange("p (c j d) -> p c j d", c=AC, j=4),
                                  bank[3][0:ROWS, 0:D].rearrange("p (c j d) -> p c j d", c=AC, j=4),
                                  bc(rinv[q][:, :].rearrange("p (j c) -> p c j", j=4), 3, AD), ALU.mult)\
                    .then_inc(s["y_ready"], 1)
            if route:
                g = k - 2
                rt = Chain(dve, s["route_chain"], ROUTE_LINKS, g)
                dve.wait_ge(s["lg_full"], OPEN + g + 1)
                dve.tensor_tensor(lg[p][:, :], bank[1][0:ROWS, 0:E], bg[:, :], ALU.add).then_inc(s["lg_read"], 1)
                dve.wait_ge(s["lg_read"], OPEN + g + 1)
                rt.link(dve.tensor_reduce(gx[p][:, 2:3], lg[p][:, :], AX.X, ALU.max))
                rt.wait()
                dve.tensor_scalar(lm[p][:, :], lg[p][:, :], gx[p][:, 2:3], None, ALU.subtract).then_inc(s["lg_shift"], 1)
                choose(dve, rt, lg[p][:, :], gx[p], countdown[:, :], hot[p][:, :], s["hot_ready"])
            if front:
                g = k
                for c in range(AC):
                    dve.wait_ge(s["s_full"], OPEN + g * AC + c + 1)
                    dve.tensor_tensor(S[p][:, c], bank[4 + c][0:ROWS, 0:4 * ROWS].rearrange("p (h k) -> p h k", h=4),
                                      bc(mask[:, :], 1, 4), ALU.add).then_inc(s["masked"], 1)
                    dve.wait_ge(s["masked"], OPEN + g * AC + c + 1)
                    dve.tensor_reduce(mx[p][:, 4 * c:4 * c + 4], S[p][:, c], AX.X, ALU.max).then_inc(s["max_ready"], 1)
            if route:
                g = k - 2
                dve.wait_ge(s["lg_exp"], OPEN + g + 1)
                rt.link(dve.tensor_reduce(gx[p][:, 2:3], ex[p][:, :], AX.X, ALU.add))
                rt.wait()
                rt.link(dve.reciprocal(gx[p][:, 3:4], gx[p][:, 2:3]))
                rt.wait()
                rt.link(dve.tensor_copy(prob[:, bass.ds(g, 1)], gx[p][:, 3:4]))
                place_rows(dve, rt, bank[0][0:ROWS, 0:E], bank[0][0:ROWS, E:2 * E], hot[p], place[p],
                           slotf[p], slot[p], taken, g, s["rank_full"], s["slot_ready"], sent[p], 16 * t)
                assert rt.n == ROUTE_LINKS, rt.n
            if back:
                g = k - 1
                bt = Chain(dve, s["back_chain"], 3, g)
                dve.wait_ge(s["wo_full"], OPEN + g + 1)
                dve.wait_ge(s["hb_ready"], OPEN + g + 1)
                dve.tensor_tensor(hcur[q][:, :], bank[3][0:ROWS, 0:D], hb[q][:, :], ALU.add).then_inc(s["h_ready"], 1)
                dve.wait_ge(s["h_ready"], OPEN + g + 1)
                statistics(bt, q, hcur[q][:, :], s["var2_ready"])
                bt.link(dve.tensor_scalar(h_all[:, bass.ds(g, 1), :].rearrange("p a d -> p (a d)"), hcur[q][:, :], 1.0,
                                          None, ALU.mult))
                assert bt.n == 3, bt.n
                dve.wait_ge(sent[q], 16 * (t - 1 + p) + 16)
                dve.tensor_scalar(xrow[q][:, D:D + 1], row_number[:, bass.ds(g, 1)], 1.0, None, ALU.mult)\
                    .then_inc(s["numbered"], 1)
                dve.wait_ge(s["rstd2_ready"], OPEN + g + 1)
                dve.tensor_scalar(xrow[q][:, 0:D], hcur[q][:, :], mv[q][:, 0:1], rstd[q][:, :], ALU.subtract, ALU.mult)\
                    .then_inc(s["xrow_ready"], 1)

        run_steps(dve, step)


def place_rows(dve, ch, ranks, totals, hot, place, slotf, slot, taken, gi, rank_full, slot_ready, scattered, sent):
    dve.wait_ge(scattered, sent)
    dve.wait_ge(rank_full, OPEN + gi + 1)
    ch.link(dve.tensor_tensor(place[:, :], ranks, taken[:, :], ALU.add))
    ch.link(dve.tensor_tensor(taken[:, :], totals, taken[:, :], ALU.add))
    ch.wait()
    ch.link(dve.tensor_tensor(place[:, :], place[:, :], hot[:, :], ALU.mult))
    ch.wait()
    ch.link(dve.tensor_reduce(slotf[:, :], place[:, :], AX.X, ALU.add))
    ch.wait()
    dve.tensor_copy(slot[:, :], slotf[:, :]).then_inc(slot_ready, 1)


def output_phase(nc, ctx, h_all, y_dram, prob, out):
    DEEP = 3
    TURNS = (GROUPS - 1) // DEEP
    assert (GROUPS - 1) % DEEP == 0
    y = ctx.enter_context(nc.sbuf_tensor("o_y", [ROWS, DEEP, D], F32))
    share = ctx.enter_context(nc.sbuf_tensor("o_share", [ROWS, DEEP], F32))
    res = ctx.enter_context(nc.sbuf_tensor("o_res", [ROWS, DEEP, D], F32))
    s = {n: nc.alloc_semaphore("o_" + n) for n in
         "loaded0 loaded1 loaded2 added0 added1 added2 stored0 stored1 stored2 share_ready".split()}
    block = ctx.enter_context(nc.Block())

    @block.sync
    def _(sync):
        open_counts(sync, s.values())

        def load(g, b):
            sync.dma_start(y[:, b, :], y_dram[bass.ds(g * ROWS, ROWS), :]).then_inc(s[f"loaded{b}"], 16)

        for b in range(DEEP):
            load(b, b)
        with sync.Fori(0, TURNS - 1) as t:
            for b in range(DEEP):
                sync.wait_ge(s[f"added{b}"], OPEN + t + 1)
                sync.dma_start(out[bass.ds((t * DEEP + b) * ROWS, ROWS), :], res[:, b, :]).then_inc(s[f"stored{b}"], 16)
                load((t + 1) * DEEP + b, b)
        for b in range(DEEP):
            sync.wait_ge(s[f"added{b}"], OPEN + TURNS)
            sync.dma_start(out[((TURNS - 1) * DEEP + b) * ROWS:((TURNS - 1) * DEEP + b + 1) * ROWS, :], res[:, b, :])\
                .then_inc(s[f"stored{b}"], 16)
            if b == 0:
                load(GROUPS - 1, 0)
        sync.wait_ge(s["added0"], OPEN + TURNS + 1)
        sync.dma_start(out[(GROUPS - 1) * ROWS:(GROUPS - 1) * ROWS + NEW_ROWS_OF_LAST, :],
                       res[ROWS - NEW_ROWS_OF_LAST:ROWS, 0, :]).then_inc(s["stored0"], 16)
        sync.wait_ge(s["stored0"], OPEN + 16 * TURNS + 16)
        sync.wait_ge(s["stored1"], OPEN + 16 * TURNS)
        sync.wait_ge(s["stored2"], OPEN + 16 * TURNS)

    @block.vector
    def _(dve):
        def add(g, b, t):
            dve.wait_ge(s[f"loaded{b}"], OPEN + 16 * t + 16)
            dve.wait_ge(s[f"stored{b}"], OPEN + 16 * t)
            dve.scalar_tensor_tensor(res[:, b, :], y[:, b, :], share[:, b:b + 1],
                                     h_all[:, bass.ds(g, 1), :].rearrange("p a d -> p (a d)"), ALU.mult, ALU.add)\
                .then_inc(s[f"added{b}"], 1)

        with dve.Fori(0, TURNS) as t:
            for b in range(DEEP):
                dve.wait_ge(s[f"added{b}"], OPEN + t)
                dve.tensor_scalar(share[:, b:b + 1], prob[:, bass.ds(t * DEEP + b, 1)], 1.0, None, ALU.mult)\
                    .then_inc(s["share_ready"], 1)
            dve.wait_ge(s["share_ready"], OPEN + (t + 1) * DEEP)
            for b in range(DEEP):
                add(t * DEEP + b, b, t)
        dve.wait_ge(s["added0"], OPEN + TURNS)
        dve.tensor_copy(share[:, 0:1], prob[:, GROUPS - 1:GROUPS]).then_inc(s["share_ready"], 1)
        dve.wait_ge(s["share_ready"], OPEN + GROUPS)
        add(GROUPS - 1, 0, TURNS)


def host_layouts_rest(i):
    f = np.float32

    def rows(w):
        w = np.asarray(w)
        return np.ascontiguousarray(w.reshape(-1, 128, w.shape[1]).transpose(1, 0, 2))

    def pad_heads(w):
        w = np.asarray(w).reshape(-1, AH, AD)
        o = np.zeros((w.shape[0], AH, 32), f)
        o[:, :, :AD] = w
        return o.reshape(-1, AH * 32)

    def per_expert(w):
        w = np.asarray(w)
        return np.ascontiguousarray(w.reshape(E, -1, 128, w.shape[2]).transpose(0, 2, 1, 3))

    def bias(b):
        b = np.asarray(b)
        return np.ascontiguousarray(b.reshape(E, -1, 128).transpose(0, 2, 1))

    r = np.arange(ROWS)
    ok = (r[:, None] // T == r[None] // T) & (r[None] <= r[:, None])
    return dict(
        awq=rows(pad_heads(i["L1_attn_Wq"])), awk=rows(pad_heads(i["L1_attn_Wk"])), awv=rows(i["L1_attn_Wv"]),
        awo=rows(i["L1_attn_Wo"]), awg=rows(i["L1_ffn_w_gate"]),
        abq=pad_heads(np.asarray(i["L1_attn_bq"])[None]).reshape(-1, 128).T,
        abk=pad_heads(np.asarray(i["L1_attn_bk"])[None]).reshape(-1, 128).T,
        abv=np.asarray(i["L1_attn_bv"]), abo=np.asarray(i["L1_attn_bo"]), abg=np.asarray(i["L1_ffn_b_gate"]),
        amask=np.where(ok, 0.0, -1e30).astype(f),
        m0w1=per_expert(i["L0_ffn_w1"]), m0b1=bias(i["L0_ffn_b1"]), m0w2=per_expert(i["L0_ffn_w2"]),
        m0b2=np.asarray(i["L0_ffn_b2"]),
        m1w1=per_expert(i["L1_ffn_W1"]), m1b1=bias(i["L1_ffn_b1"]), m1w2=per_expert(i["L1_ffn_W2"]),
        m1b2=np.asarray(i["L1_ffn_b2"]),
    )


def host_layouts_mixtures():
    f = np.float32
    e = np.arange(E)
    return dict(
        region=(e * REGION).astype(f)[None],
        full=np.broadcast_to(np.arange(PER_EXPERT) * SLOTS, (1, E, PER_EXPERT)).astype(f),
        upto=(e[None] <= e[:, None]).astype(f)[None],
        number=np.broadcast_to(np.arange(MAX_TILES + 1)[:, None], (1, MAX_TILES + 1, E)).astype(f),
        zero_rows=np.concatenate([np.zeros((SLOTS, D), f), np.arange(TOKENS, TOKENS + SLOTS, dtype=f)[:, None]], 1)
        .reshape(2, 128, D + 1).transpose(1, 0, 2),
        row_number=np.arange(TOKENS, dtype=f).reshape(GROUPS, ROWS).T,
        before=(np.arange(ROWS)[:, None] < np.arange(ROWS)[None]).astype(f),
        regions=np.tile((e * REGION).astype(f), (ROWS, 1)),
    )


def build(nc, a, out):
    h_dram = nc.dram_tensor("h_kept", (ROWS, GROUPS, D), F32, kind="Internal").ap()
    sorted_x = nc.dram_tensor("sorted_x", (SORTED_ROWS, D + 1), F32, kind="Internal").ap()
    y_dram = nc.dram_tensor("y_rows", (TOKENS + SLOTS, D), F32, kind="Internal").ap()
    with ExitStack() as kept:
        taken = kept.enter_context(nc.sbuf_tensor("taken", [ROWS, E], F32))
        with nc.cleanup_on_exit(), ExitStack() as ctx:
            delta_phase(nc, ctx, a, h_dram, sorted_x, taken)
        with nc.cleanup_on_exit(), ExitStack() as ctx:
            mixture_phase(nc, ctx, "m0_", a["m0w1"], a["m0b1"], a["m0w2"], a["m0b2"], True, a, taken, sorted_x, y_dram)
        h_all = kept.enter_context(nc.sbuf_tensor("h_all", [ROWS, GROUPS, D], F32))
        prob = kept.enter_context(nc.sbuf_tensor("prob", [ROWS, GROUPS], F32))
        with nc.cleanup_on_exit(), ExitStack() as ctx:
            attention_phase(nc, ctx, a, h_dram, y_dram, h_all, sorted_x, taken, prob)
        with nc.cleanup_on_exit(), ExitStack() as ctx:
            mixture_phase(nc, ctx, "m1_", a["m1w1"], a["m1b1"], a["m1w2"], a["m1b2"], False, a, taken, sorted_x, y_dram)
        with nc.cleanup_on_exit(), ExitStack() as ctx:
            output_phase(nc, ctx, h_all, y_dram, prob, out.rearrange("b t d -> (b t) d"))


def kernel(**inputs):
    import concourse.bacc as bacc
    from concourse.bass_utils import run_bass_kernel_spmd as run

    nc = bacc.Bacc("TRN2", target_bir_lowering=False, num_devices=1)
    arrays, a = {}, {}
    for name, v in {**host_layouts(inputs), **host_layouts_rest(inputs), **host_layouts_mixtures()}.items():
        v = np.ascontiguousarray(v)
        arrays["in_" + name] = v
        a[name] = nc.dram_tensor("in_" + name, v.shape, F32, kind="ExternalInput").ap()
    out = nc.dram_tensor("out", (IMAGES, T, D), F32, kind="ExternalOutput").ap()
    build(nc, a, out)
    return run(nc, [arrays], core_ids=[0]).results[0]["out"]
```
